# Optimizing a Trainium2 kernel written in Bass

```python
import numpy as np
import jax
import jax.numpy as jnp

def _softmax(x, axis=-1):
    return jax.nn.softmax(x, axis=axis)

def _gelu(x):
    return jax.nn.gelu(x, approximate=True)

def _silu(x):
    return jax.nn.silu(x)

def _sigmoid(x):
    return jax.nn.sigmoid(x)

def _layernorm(x, axis=-1, eps=1e-05):
    m = jnp.mean(x, axis=axis, keepdims=True)
    v = jnp.var(x, axis=axis, keepdims=True)
    return (x - m) / jnp.sqrt(v + eps)

def _scatter_add(tgt, idx, src, axis=0):
    return tgt.at[idx].add(src)

def _segment_sum(src, seg, n):
    return jax.ops.segment_sum(src, seg, n)
kernel_name = 'mk_adj_resnorm_d2_adj_r2_8a5f0f'

def setup_inputs(seed: int=0):
    np.random.seed(seed)
    _w = jnp.asarray

    def _rec_inputs():
        import jax
        import jax.numpy as jnp
        _gk = jax.random.key(seed)
        x = -0.0005207 + 1.001 * jax.random.normal(jax.random.fold_in(_gk, 1), (4096, 128), jnp.float32)
        _w = (1.0 + jnp.arange(4096, dtype=jnp.float32)) ** (-0.5)
        _w = _w / _w.mean()
        _pij = jnp.clip(0.000976562 * _w[:, None] * _w[None, :], 0.0, 1.0)
        _a = jax.random.uniform(jax.random.fold_in(_gk, 2), (4096, 4096)) < _pij
        _a = jnp.logical_or(_a, jnp.eye(4096, dtype=bool))
        _af = _a.astype(jnp.float32)
        _af = _af * jax.random.uniform(jax.random.fold_in(_gk, 3), (4096, 4096), jnp.float32, 0.05, 1)
        adj = _af
        return (x, adj)
    x, adj = _rec_inputs()

    def _L0_gnn_setup():
        import jax, jax.numpy as jnp
        import numpy as np
        THRESH = 1e-06
        EPS = 1e-08
        LN_EPS = 1e-05

        def _layer(h, M, W_in, b_in, W_out, b_out, W_self, b_self, gamma, beta):
            A = M / (jnp.sum(M, axis=0, keepdims=True) + EPS)
            mask = A > THRESH
            W = jnp.where(mask, A, 0.0)
            T = h @ W_in + b_in
            weighted_sum = jnp.einsum('ji,jd->id', W, T)
            weight_sum = jnp.sum(W, axis=0)
            has_edge = jnp.any(mask, axis=0)
            agg = jnp.where(has_edge[:, None], weighted_sum / (weight_sum[:, None] + EPS), T)
            agg = agg @ W_out + b_out
            out = agg + (h @ W_self + b_self)
            mu = jnp.mean(out, axis=-1, keepdims=True)
            var = jnp.mean(jnp.square(out - mu), axis=-1, keepdims=True)
            out = (out - mu) * jax.lax.rsqrt(var + LN_EPS) * gamma + beta
            return out
        key = jax.random.key(seed)
        ks = jax.random.split(key, 16)
        N, D_IN, D_H, D_OUT = (4096, 128, 256, 128)
        s = 0.05
        return {'node_features': jax.random.normal(ks[0], (N, D_IN), jnp.float32), 'mobility_matrix': jax.random.uniform(ks[1], (N, N), jnp.float32), 'W_in1': jax.random.normal(ks[2], (D_IN, D_H)) * s, 'b_in1': jnp.zeros((D_H,)), 'W_out1': jax.random.normal(ks[3], (D_H, D_H)) * s, 'b_out1': jnp.zeros((D_H,)), 'W_self1': jax.random.normal(ks[4], (D_IN, D_H)) * s, 'b_self1': jnp.zeros((D_H,)), 'g1': jnp.ones((D_H,)), 'be1': jnp.zeros((D_H,)), 'W_in2': jax.random.normal(ks[5], (D_H, D_OUT)) * s, 'b_in2': jnp.zeros((D_OUT,)), 'W_out2': jax.random.normal(ks[6], (D_OUT, D_OUT)) * s, 'b_out2': jnp.zeros((D_OUT,)), 'W_self2': jax.random.normal(ks[7], (D_H, D_OUT)) * s, 'b_self2': jnp.zeros((D_OUT,)), 'g2': jnp.ones((D_OUT,)), 'be2': jnp.zeros((D_OUT,))}
    _L0_gnn_all = _L0_gnn_setup()
    _L0_gnn_in = {k: v for k, v in _L0_gnn_all.items() if k in ('W_in1', 'b_in1', 'W_out1', 'b_out1', 'W_self1', 'b_self1', 'g1', 'be1', 'W_in2', 'b_in2', 'W_out2', 'b_out2', 'W_self2', 'b_self2', 'g2', 'be2')}
    del _L0_gnn_all

    def _L1_gnn_setup():
        import jax, jax.numpy as jnp
        import numpy as np
        N = 4096
        D = 128
        L = 3

        def _cxin_conv(x, a, eps, W, b):
            ax = a @ x
            h = ax + (1.0 + eps[0]) * ax
            for i in range(L):
                h = jax.nn.relu(h @ W[i].T + b[i])
            return h
        key = jax.random.key(seed)
        ks = jax.random.split(key, 8)
        s = 1.0 / np.sqrt(D)
        return {'x1': jax.random.normal(ks[0], (N, D), jnp.float32), 'x2': jax.random.normal(ks[1], (N, D), jnp.float32), 'G1': jax.random.uniform(ks[2], (N, N), jnp.float32), 'G2': jax.random.uniform(ks[3], (N, N), jnp.float32), 'eps1': jnp.zeros((1,), jnp.float32), 'eps2': jnp.zeros((1,), jnp.float32), 'W1': jax.random.normal(ks[4], (L, D, D), jnp.float32) * s, 'b1': jnp.zeros((L, D), jnp.float32), 'W2': jax.random.normal(ks[5], (L, D, D), jnp.float32) * s, 'b2': jnp.zeros((L, D), jnp.float32), 'Wm': jax.random.normal(ks[6], (D, 2 * D), jnp.float32) * (1.0 / np.sqrt(2 * D)), 'bm': jnp.zeros((D,), jnp.float32)}
    _L1_gnn_all = _L1_gnn_setup()
    _L1_gnn_in = {k: v for k, v in _L1_gnn_all.items() if k in ('x2', 'eps1', 'eps2', 'W1', 'b1', 'W2', 'b2', 'Wm', 'bm')}
    del _L1_gnn_all
    return {'x': x, 'adj': adj, 'L0_gnn_W_in1': _L0_gnn_in['W_in1'], 'L0_gnn_b_in1': _L0_gnn_in['b_in1'], 'L0_gnn_W_out1': _L0_gnn_in['W_out1'], 'L0_gnn_b_out1': _L0_gnn_in['b_out1'], 'L0_gnn_W_self1': _L0_gnn_in['W_self1'], 'L0_gnn_b_self1': _L0_gnn_in['b_self1'], 'L0_gnn_g1': _L0_gnn_in['g1'], 'L0_gnn_be1': _L0_gnn_in['be1'], 'L0_gnn_W_in2': _L0_gnn_in['W_in2'], 'L0_gnn_b_in2': _L0_gnn_in['b_in2'], 'L0_gnn_W_out2': _L0_gnn_in['W_out2'], 'L0_gnn_b_out2': _L0_gnn_in['b_out2'], 'L0_gnn_W_self2': _L0_gnn_in['W_self2'], 'L0_gnn_b_self2': _L0_gnn_in['b_self2'], 'L0_gnn_g2': _L0_gnn_in['g2'], 'L0_gnn_be2': _L0_gnn_in['be2'], 'L1_gnn_x2': _L1_gnn_in['x2'], 'L1_gnn_eps1': _L1_gnn_in['eps1'], 'L1_gnn_eps2': _L1_gnn_in['eps2'], 'L1_gnn_W1': _L1_gnn_in['W1'], 'L1_gnn_b1': _L1_gnn_in['b1'], 'L1_gnn_W2': _L1_gnn_in['W2'], 'L1_gnn_b2': _L1_gnn_in['b2'], 'L1_gnn_Wm': _L1_gnn_in['Wm'], 'L1_gnn_bm': _L1_gnn_in['bm']}

def reference(x, adj, L0_gnn_W_in1, L0_gnn_b_in1, L0_gnn_W_out1, L0_gnn_b_out1, L0_gnn_W_self1, L0_gnn_b_self1, L0_gnn_g1, L0_gnn_be1, L0_gnn_W_in2, L0_gnn_b_in2, L0_gnn_W_out2, L0_gnn_b_out2, L0_gnn_W_self2, L0_gnn_b_self2, L0_gnn_g2, L0_gnn_be2, L1_gnn_x2, L1_gnn_eps1, L1_gnn_eps2, L1_gnn_W1, L1_gnn_b1, L1_gnn_W2, L1_gnn_b2, L1_gnn_Wm, L1_gnn_bm):
    import jax
    import jax.numpy as jnp

    def _L0_gnn_ref(node_features, mobility_matrix, W_in1, b_in1, W_out1, b_out1, W_self1, b_self1, g1, be1, W_in2, b_in2, W_out2, b_out2, W_self2, b_self2, g2, be2):
        import jax, jax.numpy as jnp
        import numpy as np
        THRESH = 1e-06
        EPS = 1e-08
        LN_EPS = 1e-05

        def _layer(h, M, W_in, b_in, W_out, b_out, W_self, b_self, gamma, beta):
            A = M / (jnp.sum(M, axis=0, keepdims=True) + EPS)
            mask = A > THRESH
            W = jnp.where(mask, A, 0.0)
            T = h @ W_in + b_in
            weighted_sum = jnp.einsum('ji,jd->id', W, T)
            weight_sum = jnp.sum(W, axis=0)
            has_edge = jnp.any(mask, axis=0)
            agg = jnp.where(has_edge[:, None], weighted_sum / (weight_sum[:, None] + EPS), T)
            agg = agg @ W_out + b_out
            out = agg + (h @ W_self + b_self)
            mu = jnp.mean(out, axis=-1, keepdims=True)
            var = jnp.mean(jnp.square(out - mu), axis=-1, keepdims=True)
            out = (out - mu) * jax.lax.rsqrt(var + LN_EPS) * gamma + beta
            return out
        h = _layer(node_features, mobility_matrix, W_in1, b_in1, W_out1, b_out1, W_self1, b_self1, g1, be1)
        h = jax.nn.relu(h)
        h = _layer(h, mobility_matrix, W_in2, b_in2, W_out2, b_out2, W_self2, b_self2, g2, be2)
        h = jax.nn.relu(h)
        return h

    def _L1_gnn_ref(x1, x2, G1, G2, eps1, eps2, W1, b1, W2, b2, Wm, bm):
        import jax, jax.numpy as jnp
        import numpy as np
        N = 4096
        D = 128
        L = 3

        def _cxin_conv(x, a, eps, W, b):
            ax = a @ x
            h = ax + (1.0 + eps[0]) * ax
            for i in range(L):
                h = jax.nn.relu(h @ W[i].T + b[i])
            return h
        out1 = _cxin_conv(x1, G1, eps1, W1, b1)
        out2 = _cxin_conv(x2, G2, eps2, W2, b2)
        merged = jnp.concatenate((out1, out2), axis=1)
        return merged @ Wm.T + bm
    x = _layernorm(x + _L0_gnn_ref(x, adj, L0_gnn_W_in1, L0_gnn_b_in1, L0_gnn_W_out1, L0_gnn_b_out1, L0_gnn_W_self1, L0_gnn_b_self1, L0_gnn_g1, L0_gnn_be1, L0_gnn_W_in2, L0_gnn_b_in2, L0_gnn_W_out2, L0_gnn_b_out2, L0_gnn_W_self2, L0_gnn_b_self2, L0_gnn_g2, L0_gnn_be2), axis=-1)
    x = _layernorm(x + _L1_gnn_ref(x, L1_gnn_x2, adj, adj, L1_gnn_eps1, L1_gnn_eps2, L1_gnn_W1, L1_gnn_b1, L1_gnn_W2, L1_gnn_b2, L1_gnn_Wm, L1_gnn_bm), axis=-1)
    return x

_drawn_inputs = setup_inputs


def setup_inputs(seed=0):
    import zlib

    import numpy as np

    out = dict(_drawn_inputs(seed))
    spreads = {'L0_gnn_b_in1': (0.0, 0.1),
     'L0_gnn_b_out1': (0.0, 0.1),
     'L0_gnn_b_self1': (0.0, 0.1),
     'L0_gnn_g1': (1.0, 0.2),
     'L0_gnn_be1': (0.0, 0.1),
     'L0_gnn_b_in2': (0.0, 0.1),
     'L0_gnn_b_out2': (0.0, 0.1),
     'L0_gnn_b_self2': (0.0, 0.1),
     'L0_gnn_g2': (1.0, 0.2),
     'L0_gnn_be2': (0.0, 0.1),
     'L1_gnn_b1': (0.0, 0.1),
     'L1_gnn_b2': (0.0, 0.1),
     'L1_gnn_bm': (0.0, 0.1)}
    factors = {}
    for name, (base, spread) in spreads.items():
        noise = np.random.default_rng([zlib.crc32(name.encode()), seed]).standard_normal(out[name].shape)
        drawn = base * np.exp(spread * noise) if base else spread * noise
        out[name] = jnp.asarray(drawn.astype(out[name].dtype))
    for name, factor in factors.items():
        out[name] = (out[name] * factor).astype(out[name].dtype)
    return out
```

```python
from contextlib import ExitStack

import concourse.bass as bass
from concourse import mybir

FP32 = mybir.dt.float32
F32R = mybir.dt.float32r
I32 = mybir.dt.int32
I8 = mybir.dt.int8
U8 = mybir.dt.uint8
ALU = mybir.AluOpType
ACT = mybir.ActivationFunctionType
AX = mybir.AxisListType

N = 4096
D = 128
H = 256
P = 128
PANEL = 512
PANELS = N // PANEL
SLOTS = 8
BLK = PANEL // P
CHUNKS = N // P
SLOTW = BLK * PANEL
THRESH = 1e-06
EPS = 1e-08
LN_EPS = 1e-05
BIG = 2.0 ** -7
CS_LIMIT = 0.99 * BIG / THRESH
RSQRT_SEED = float(0x5F3759DF)
ACT_ZERO_SLOTS = (0, 2, 4, 6, 7)
DVE_ZERO_SLOTS = tuple(q for q in range(SLOTS) if q not in ACT_ZERO_SLOTS)


class Steps:

    def __init__(self, eng, sem):
        self.eng, self.sem, self.base, self.n = eng, sem, 0, 0

    def did(self, ins):
        ins.then_inc(self.sem, 1)
        self.n += 1

    def settle(self):
        self.eng.wait_ge(self.sem, self.base + self.n)

    def enter(self, base):
        self.base, self.n = base, 0


class Pass1Signals:

    def __init__(self, sem, tag, loaded, xp_in):
        self.loaded, self.xp_in = loaded, xp_in
        self.slot_pe = sem("slot_pe_" + tag)
        self.slot_act = sem("slot_act_" + tag)
        self.slot_dve = sem("slot_dve_" + tag)
        self.folded = sem("folded_" + tag)
        self.sums_out = sem("sums_out_" + tag)
        self.edge_ready = sem("edge_ready_" + tag)
        self.u_done = sem("u_done_" + tag)
        self.xp_used = sem("xp_used_" + tag)
        self.u_copied = sem("u_copied_" + tag)
        self.xt_copied = sem("xt_copied_" + tag)
        self.p12_done = sem("p12_done_" + tag)
        self.t1_ready = sem("t1_ready_" + tag)
        self.z_ready = sem("z_ready_" + tag)
        self.stats_ready = sem("stats_ready_" + tag)
        self.normed = sem("normed_" + tag)
        self.h_ready = sem("h_ready_" + tag)
        self.ht_done = sem("ht_done_" + tag)
        self.ht_copied = sem("ht_copied_" + tag)
        self.w2_done = sem("w2_done_" + tag)
        self.v_done = sem("v_done_" + tag)
        self.dve_step = sem("dve_step_" + tag)
        self.pool_step = sem("pool_step_" + tag)


def panel_loop(eng, steps, per_panel, body):
    body(0, 0)
    before = steps.n if steps else 0
    assert not steps or steps.base == 0
    with eng.Fori(0, (PANELS - 2) // 2) as pair:
        for k in range(2):
            p = pair * 2 + (1 + k)
            if steps:
                steps.enter(pair * (2 * per_panel) + (before + k * per_panel))
            body(p, (1 + k) % 2)
            assert not steps or steps.n == per_panel, (steps.n, per_panel)
    if steps:
        steps.enter(before + (PANELS - 2) * per_panel)
    body(PANELS - 1, (PANELS - 1) % 2)


def gnn_program(nc, x, adj, W_in1, b_in1, W_out1, b_out1, W_self1, b_self1, g1, be1,
                W_in2, b_in2, W_out2, b_out2, W_self2, b_self2, g2, be2,
                x2, eps1, eps2, W1, b1, W2, b2, Wm, bm, out):
    ctx = ExitStack()
    with ctx:
        def sb(name, shape, dt=FP32, where=ctx):
            return where.enter_context(nc.sbuf_tensor(name, shape, dt))

        def sem(name):
            return ctx.enter_context(nc.semaphore(name))

        masked_dram = nc.dram_tensor("masked_adj", [N, N], FP32, kind="Internal").ap()
        cs_dram = nc.dram_tensor("column_sums", [N], FP32, kind="Internal").ap()

        ring = sb("ring", [P, SLOTS, SLOTW])
        vh = sb("vh", [P, CHUNKS, D], F32R)
        vl = sb("vl", [P, CHUNKS, D], F32R)
        self2 = sb("self2", [P, CHUNKS, D])
        z = sb("z", [P, BLK, H])
        uts = sb("uts", [P, PANEL])
        xts = sb("xts", [P, PANEL])
        xp = sb("xp", [P, 2, BLK, D])
        ident = sb("ident", [P, P])
        ones = sb("ones", [P, P])
        w1t = sb("w1t", [P, 3, D])
        w2t = sb("w2t", [P, 3, D])
        wmt = sb("wmt", [P, 2, D])
        g2B = sb("g2B", [P, D])
        be2B = sb("be2B", [P, D])
        bmB = sb("bmB", [P, D])
        bcol = sb("bcol", [P, 2, 3])
        scl = sb("scl", [P, 2])
        s_all = sb("s_all", [P, CHUNKS])
        cs_all = sb("cs_all", [P, CHUNKS])
        s4 = sb("s4", [P, BLK])
        bnst = sb("bnst", [P, BLK, 6])
        mv = sb("mv", [P, BLK, 2])
        ln = sb("ln", [P, 5, BLK])
        spare = sb("spare", [P, 1])
        flag_i = sb("flag_i", [P, 1], I32)

        only1 = ExitStack()
        xs = sb("xs", [P, CHUNKS, D], where=only1)
        acc = sb("acc", [P, SLOTW], where=only1)
        accf = sb("accf", [P, PANEL], where=only1)
        junk_a = sb("junk_a", [P, SLOTW], I8, where=only1)
        junk_b = sb("junk_b", [P, SLOTW], I8, where=only1)
        junk_d = sb("junk_d", [P, SLOTW], U8, where=only1)
        t1 = sb("t1", [P, BLK, H], where=only1)
        hT = sb("hT", [P, 2, PANEL], where=only1)
        diag = sb("diag", [P, BLK, P], where=only1)
        wA = sb("wA", [P, 2, H], where=only1)
        wB = sb("wB", [P, 2, H], where=only1)
        bw1B = sb("bw1B", [P, H], where=only1)
        bs1B = sb("bs1B", [P, H], where=only1)
        g1B = sb("g1B", [P, H], where=only1)
        be1B = sb("be1B", [P, H], where=only1)
        bb2B = sb("bb2B", [P, D], where=only1)
        bo2B = sb("bo2B", [P, D], where=only1)
        st = sb("st", [P, 2, 3, BLK], where=only1)
        ed = sb("ed", [P, 6, BLK], where=only1)
        nz = sb("nz", [P, PANELS * SLOTS], where=only1)
        sg = sb("sg", [P, PANELS * SLOTS], where=only1)
        fl = sb("fl", [P, 4], where=only1)
        nbig = sb("nbig", [P, 1], where=only1)
        crow = sb("crow", [CHUNKS, P], where=only1)
        bincol = sb("bincol", [P, 3], where=only1)
        only1.close()
        only23 = ExitStack()
        ctx.enter_context(only23)
        x1h = sb("x1h", [P, CHUNKS, D], F32R, where=only23)
        x1l = sb("x1l", [P, CHUNKS, D], F32R, where=only23)
        mh = sb("mh", [P, 8, PANEL], F32R, where=only23)
        ml = sb("ml", [P, 8, PANEL], F32R, where=only23)

        ps = ctx.enter_context(nc.psum_tensor("ps", [P, 8, PANEL], FP32))

        stage = ring[:, SLOTS - 2:SLOTS, :].rearrange("p s n -> p (s n)")
        st_in1 = stage[:, 0:256]
        st_out1 = stage[:, 256:768].rearrange("p (c n) -> p c n", c=2)
        st_in2 = stage[:, 768:1024].rearrange("p (c n) -> p c n", c=2)
        st_out2 = stage[:, 1024:1152]
        st_w1 = stage[:, 1152:1536].rearrange("p (l n) -> p l n", l=3)
        st_w2 = stage[:, 1536:1920].rearrange("p (l n) -> p l n", l=3)
        st_wm = stage[:, 1920:2176]
        st_b = stage[:, 2176:2560].rearrange("p (k n) -> p k n", k=3)
        st_in1T = stage[:, 2560:2816].rearrange("p (c n) -> p c n", c=2)
        st_in2T = stage[:, 2816:3072].rearrange("p (c n) -> p c n", c=2)
        st_bs = stage[:, 3072:3328]
        st_bo = stage[:, 3328:3456]

        SMALL, T = 2, (3, 4, 5, 6)

        def T2(i):
            return ps[:, T[i], :]

        weights_in = sem("weights_in")
        consts_in = sem("consts_in")
        x_in = sem("x_in")
        const_ready = sem("const_ready")
        setup_t = sem("setup_t")
        setup_c = sem("setup_c")
        setup_m = sem("setup_m")
        setup_done = sem("setup_done")
        bad_ready = sem("bad_ready")
        bad_summed = sem("bad_summed")
        flag_ready = sem("flag_ready")
        loaded = [sem(f"loaded{q}") for q in range(SLOTS)]
        xp_in = [sem(f"xp_in{k}") for k in range(2)]
        x2_in = [sem(f"x2_in{k}") for k in range(PANELS)]

        S1 = Pass1Signals(sem, "a", loaded, xp_in)
        SG = Pass1Signals(sem, "g", [sem(f"loaded_g{q}") for q in range(SLOTS)], [sem(f"xp_in_g{k}") for k in range(2)])
        gen_enter = sem("gen_enter")
        gen_leave = sem("gen_leave")
        gen_cs_t = sem("gen_cs_t")
        gen_cs_row = sem("gen_cs_row")
        gen_cs_in = sem("gen_cs_in")
        gen_in = sem("gen_in")
        gen_masked = sem("gen_masked")
        gen_stored = sem("gen_stored")
        gen_step = sem("gen_step")

        hi2 = sem("hi2")
        lo2 = sem("lo2")
        used2 = sem("used2")
        y_copied = sem("y_copied")
        yt_done = sem("yt_done")
        z2_ready = sem("z2_ready")
        stats2 = sem("stats2")
        normed2 = sem("normed2")
        affine2 = sem("affine2")
        x1_done = sem("x1_done")
        self_used = sem("self_used")
        dve_step2 = sem("dve_step2")
        pool_step2 = sem("pool_step2")
        x2_hi = sem("x2_hi")
        x2_lo = sem("x2_lo")
        tr_done = sem("tr_done")
        hi3 = sem("hi3")
        lo3 = sem("lo3")
        used3 = sem("used3")
        a_copied = sem("a_copied")
        mlp_done = sem("mlp_done")
        relu_done = sem("relu_done")
        merged = sem("merged")
        z3_ready = sem("z3_ready")
        stats3 = sem("stats3")
        normed3 = sem("normed3")
        stored = sem("stored")
        dve_step3 = sem("dve_step3")

        rows_of = x.rearrange("(k p) d -> p k d", p=P)
        x2_rows = x2.rearrange("(k p) d -> p k d", p=P)
        out_rows = out.rearrange("(k p) d -> p k d", p=P)
        by_rows = adj.rearrange("(q b r) c -> r q b c", b=BLK, r=P)

        def column_panel(src, p, q):
            return src.rearrange("(q b r) c -> r q b c", b=BLK, r=P)[:, q, :, bass.ds(p * PANEL, PANEL)]

        def row_panel(p, q):
            return adj[:, q * PANEL:(q + 1) * PANEL].rearrange("(k r) c -> r k c", r=P)[:, bass.ds(p * BLK, BLK), :]

        def blocks(t, p):
            return t[:, bass.ds(p * BLK, BLK)]

        def blocks3(t, p):
            return t[:, bass.ds(p * BLK, BLK), :]

        def one_block(t, p, b):
            return t[:, bass.ds(p * BLK + b, 1), :].rearrange("p o d -> p (o d)")

        def slot_view(q):
            return ring[:, q, :].rearrange("p (b c) -> p b c", b=BLK)

        def sp_pass1(sp, S, src, first_from):
            def panel(p, par):
                for q in range(SLOTS):
                    if first_from is not None and isinstance(p, int) and p == 0:
                        if q >= SLOTS - 2:
                            sp.wait_ge(setup_done, 1)
                    elif not (isinstance(p, int) and p == 0):
                        sp.wait_ge(S.slot_pe, p * SLOTS + (q + 1 - SLOTS))
                        sp.wait_ge(S.slot_act, p * SLOTS + (q + 1 - SLOTS))
                        sp.wait_ge(S.slot_dve, p * SLOTS + (q + 1 - SLOTS))
                    sp.dma_start(slot_view(q), column_panel(src, p, q)).then_inc(S.loaded[q], 16)
                    if q == 2:
                        sp.dma_start(xp[:, par], blocks3(rows_of, p)).then_inc(S.xp_in[par], 16)
            panel_loop(sp, None, 0, panel)

        def sp_pass2(sp, src):
            def panel(p, par):
                for q in range(SLOTS):
                    if isinstance(p, int) and p == 0:
                        sp.wait_ge(S1.slot_pe, (PANELS - 1) * SLOTS + q + 1)
                        sp.wait_ge(S1.slot_act, (PANELS - 1) * SLOTS + q + 1)
                        sp.wait_ge(S1.slot_dve, (PANELS - 1) * SLOTS + q + 1)
                    else:
                        sp.wait_ge(hi2, p * (2 * SLOTS) + (2 * q + 2 - 2 * SLOTS))
                        sp.wait_ge(lo2, p * (2 * SLOTS) + (2 * q + 2 - 2 * SLOTS))
                    sp.dma_start(slot_view(q), column_panel(src, p, q)).then_inc(loaded[q], 16)
                if isinstance(p, int) and p < 2:
                    sp.wait_ge(S1.xp_used, PANELS - 1 + p)
                else:
                    sp.wait_ge(S1.xp_used, PANELS)
                sp.dma_start(xp[:, par], blocks3(rows_of, p)).then_inc(xp_in[par], 16)
            panel_loop(sp, None, 0, panel)

        def sp_x2(sp, p):
            sp.wait_ge(self_used, p + 1)
            sp.dma_start(self2[:, BLK * p:BLK * p + BLK, :], x2_rows[:, BLK * p:BLK * p + BLK, :]).then_inc(x2_in[p], 16)

        def sp_pass3(sp):
            def panel(p, par):
                for q in range(SLOTS):
                    if isinstance(p, int) and p == 0:
                        sp.wait_ge(hi2, (PANELS - 1) * 2 * SLOTS + 2 * q + 2)
                        sp.wait_ge(lo2, (PANELS - 1) * 2 * SLOTS + 2 * q + 2)
                    else:
                        sp.wait_ge(tr_done, p * CHUNKS + (BLK * (q + 1) - CHUNKS))
                    sp.dma_start(slot_view(q), row_panel(p, q)).then_inc(loaded[q], 16)
                if isinstance(p, int) and p == 0:
                    for k in range(PANELS):
                        sp_x2(sp, k)
            panel_loop(sp, None, 0, panel)

        def pe_pass1(pe, S):
            def stage_sums(r):
                pe.wait_ge(S.folded, r + 1)
                for b in range(BLK):
                    last = pe.matmul(ps[:, SMALL, b:b + 1], accf[:, b * P:(b + 1) * P], ones[:, 0:1],
                                     start=True, stop=True)
                last.then_inc(S.sums_out, 1)

            def stage_own(r, par):
                pe.wait_ge(S.edge_ready, r + 1)
                pe.wait_ge(S.xp_in[par], xp_count(r, par))
                for b in range(BLK):
                    last = pe.matmul(ps[:, par, b * P:(b + 1) * P], xp[:, par, b, :], diag[:, b, :],
                                     start=False, stop=True, skip_group_check=True)
                last.then_inc(S.u_done, 1)
                for b in range(BLK):
                    last = pe.transpose(ps[:, T[0], b * P:(b + 1) * P], xp[:, par, b, :], ident[:, :])
                last.then_inc(S.xp_used, 1)

            def stage_layer1(r):
                pe.wait_ge(S.u_copied, r + 1)
                pe.wait_ge(S.xt_copied, r + 1)
                if isinstance(r, int) and r == PANELS - 1:
                    pe.wait_ge(S.v_done, r)
                else:
                    pe.wait_ge(S.slot_dve, r * SLOTS + (SLOTS + 2))
                for b in range(BLK):
                    pe.matmul(ps[:, T[b], 0:H], uts[:, b * P:(b + 1) * P], wA[:, 0, :], start=True, stop=True)
                    pe.matmul(ps[:, T[b], H:2 * H], xts[:, b * P:(b + 1) * P], wA[:, 1, :],
                              start=True, stop=True).then_inc(S.p12_done, 1)

            def stage_hT(r):
                pe.wait_ge(S.h_ready, r + 1)
                for c in range(2):
                    for b in range(BLK):
                        last = pe.transpose(ps[:, T[c], b * P:(b + 1) * P], z[:, b, c * P:(c + 1) * P], ident[:, :])
                    last.then_inc(S.ht_done, 1)

            def stage_layer2(r):
                pe.wait_ge(S.ht_copied, r * 2 + 2)
                for b in range(BLK):
                    for c in range(2):
                        last = pe.matmul(ps[:, T[2 + b // 2], (b % 2) * H:(b % 2) * H + H],
                                         hT[:, c, b * P:(b + 1) * P], wB[:, c, :], start=(c == 0), stop=(c == 1))
                last.then_inc(S.w2_done, 1)

            def panel(p, par):
                after = {}
                if not (isinstance(p, int) and p == 0):
                    r, rp = p - 1, 1 - par
                    after = {0: lambda: stage_sums(r), 1: lambda: stage_own(r, rp), 2: lambda: stage_layer1(r),
                             4: lambda: stage_hT(r), 6: lambda: stage_layer2(r)}
                for q in range(SLOTS):
                    pe.wait_ge(S.loaded[q], (p + 1) * 16)
                    for b in range(BLK):
                        k = BLK * q + b
                        last = pe.matmul(ps[:, par, :], xs[:, k, :], ring[:, q, b * PANEL:(b + 1) * PANEL],
                                         start=(k == 0), stop=False, skip_group_check=True)
                    last.then_inc(S.slot_pe, 1)
                    if q in after:
                        after[q]()
            panel_loop(pe, None, 0, panel)
            r = PANELS - 1
            stage_sums(r)
            stage_own(r, 1)
            stage_layer1(r)
            stage_hT(r)
            stage_layer2(r)

        def xp_count(r, par):
            if isinstance(r, int):
                return 16 * (r // 2 + 1)
            return (r - par) * 8 + 16

        def act_pass1(act, S, detect):
            def count_slot(p, q):
                act.wait_ge(S.loaded[q], (p + 1) * 16)
                col = p * SLOTS + q
                if detect:
                    if not (isinstance(p, int) and p == 0 and q == 0):
                        act.wait_ge(S.slot_act, p * SLOTS + q)
                    ins = act.activation(junk_a[:, :], ring[:, q, :], ACT.Sign, bias=nbig[:, :],
                                         accum_out=sg[:, bass.ds(col, 1)])
                    if q in ACT_ZERO_SLOTS:
                        ins = act.activation(junk_b[:, :], ring[:, q, :], ACT.Exp, scale=-2.0 ** 100,
                                             accum_out=nz[:, bass.ds(col, 1)])
                    ins.then_inc(S.slot_act, 1)
                else:
                    act.sem_inc(S.slot_act, 1)

            def copies(r, rp):
                act.wait_ge(S.u_done, r + 1)
                act.activation(uts[:, :], ps[:, rp, :], ACT.Copy).then_inc(S.u_copied, 1)
                act.wait_ge(S.xp_used, r + 1)
                act.activation(xts[:, :], T2(0), ACT.Copy).then_inc(S.xt_copied, 1)

            def normalise(r):
                act.wait_ge(S.stats_ready, r + 1)
                for b in range(BLK):
                    last = act.activation(z[:, b, :], z[:, b, :], ACT.Identity, scale=ln[:, 3, b:b + 1],
                                          bias=ln[:, 4, b:b + 1])
                last.then_inc(S.normed, 1)

            def relus(r):
                for c in range(2):
                    act.wait_ge(S.ht_done, r * 2 + (c + 1))
                    act.activation(hT[:, c, :], T2(c), ACT.Relu).then_inc(S.ht_copied, 1)

            def panel(p, par):
                post = not (isinstance(p, int) and p == 0)
                for q in range(SLOTS):
                    count_slot(p, q)
                    if post and q == 1:
                        copies(p - 1, 1 - par)
                    if post and q == 3:
                        normalise(p - 1)
                    if post and q == 5:
                        relus(p - 1)
            panel_loop(act, None, 0, panel)
            r = PANELS - 1
            copies(r, 1)
            normalise(r)
            relus(r)

        def pool_pass1(pool, S):
            steps = Steps(pool, S.pool_step)

            def post(r, rp):
                pool.wait_ge(S.edge_ready, r + 1)
                steps.did(pool.tensor_tensor(t1[:, :, :], bw1B[:, :].unsqueeze(1).to_broadcast([P, BLK, H]),
                                             st[:, rp, 2, :].unsqueeze(2).to_broadcast([P, BLK, H]), ALU.mult))
                steps.settle()
                pool.tensor_tensor(t1[:, :, :], t1[:, :, :], bs1B[:, :].unsqueeze(1).to_broadcast([P, BLK, H]),
                                   ALU.add).then_inc(S.t1_ready, 1)
                pool.wait_ge(S.normed, r + 1)
                steps.did(pool.tensor_tensor(z[:, :, :], z[:, :, :],
                                             g1B[:, :].unsqueeze(1).to_broadcast([P, BLK, H]), ALU.mult))
                steps.settle()
                pool.tensor_tensor(z[:, :, :], z[:, :, :], be1B[:, :].unsqueeze(1).to_broadcast([P, BLK, H]),
                                   ALU.add).then_inc(S.h_ready, 1)

            def panel(p, par):
                if not (isinstance(p, int) and p == 0):
                    post(p - 1, 1 - par)
            panel_loop(pool, steps, 2, panel)
            post(PANELS - 1, 1)

        def rsqrt_steps(steps, dve):
            v, half, y, t = ln[:, 0, :], ln[:, 1, :], ln[:, 3, :], ln[:, 2, :]
            steps.did(dve.tensor_scalar(v, mv[:, :, 1], LN_EPS, None, ALU.add))
            steps.settle()
            steps.did(dve.tensor_scalar(half.bitcast(I32), v.bitcast(I32), 1, None, ALU.arith_shift_right))
            steps.settle()
            steps.did(dve.tensor_scalar(y.bitcast(I32), half.bitcast(I32), -1.0, RSQRT_SEED, ALU.mult, ALU.add))
            steps.settle()
            for _ in range(4):
                steps.did(dve.tensor_tensor(t, y, y, ALU.mult))
                steps.settle()
                steps.did(dve.scalar_tensor_tensor(t, t, -0.5, v, ALU.mult, ALU.mult))
                steps.settle()
                steps.did(dve.scalar_tensor_tensor(y, t, 1.5, y, ALU.add, ALU.mult))
                steps.settle()
            return dve.scalar_tensor_tensor(ln[:, 4, :], mv[:, :, 0], -1.0, y, ALU.mult, ALU.mult)

        def ln_stats(steps, dve, rows):
            for b in range(BLK):
                steps.did(dve.bn_stats(bnst[:, b, :], rows(b)))
            steps.settle()
            dve.memset(spare[:, :], 0.0)
            for b in range(BLK):
                steps.did(dve.bn_aggr(mv[:, b, :], bnst[:, b, :]))
            steps.settle()
            return rsqrt_steps(steps, dve)

        def dve_pass1(dve, S, detect, per_panel):
            steps = Steps(dve, S.dve_step)

            def slot(p, q):
                dve.wait_ge(S.loaded[q], (p + 1) * 16)
                if detect and q in DVE_ZERO_SLOTS:
                    if not (isinstance(p, int) and p == 0 and q <= 1):
                        dve.wait_ge(S.slot_dve, p * SLOTS + (q if q > 1 else 0))
                    dve.tensor_scalar(junk_d[:, :], ring[:, q, :], 0.0, None, ALU.is_equal, ALU.add,
                                      accum_out=nz[:, bass.ds(p * SLOTS + q, 1)])
                if q == 1:
                    if not (isinstance(p, int) and p == 0):
                        dve.wait_ge(S.folded, p)
                    dve.tensor_tensor(acc[:, :], ring[:, 0, :], ring[:, 1, :], ALU.add).then_inc(S.slot_dve, 2)
                elif q > 1:
                    dve.wait_ge(S.slot_dve, p * SLOTS + q)
                    dve.tensor_tensor(acc[:, :], acc[:, :], ring[:, q, :], ALU.add).then_inc(S.slot_dve, 1)

            def fold(p):
                dve.wait_ge(S.slot_dve, p * SLOTS + SLOTS)
                steps.did(dve.tensor_tensor(acc[:, 0:2 * PANEL], acc[:, 0:2 * PANEL], acc[:, 2 * PANEL:], ALU.add))
                steps.settle()
                dve.tensor_tensor(accf[:, :], acc[:, 0:PANEL], acc[:, PANEL:2 * PANEL], ALU.add).then_inc(S.folded, 1)

            def edge(r, rp):
                cs, e, w = ps[:, SMALL, 0:BLK], ed, st[:, rp]
                dve.wait_ge(S.sums_out, r + 1)
                if detect:
                    steps.did(dve.tensor_copy(blocks(cs_all, r), cs))
                    steps.did(dve.tensor_scalar(e[:, 0, :], cs, EPS, None, ALU.add))
                else:
                    steps.did(dve.tensor_scalar(e[:, 1, :], cs, 0.0, None, ALU.add))
                    steps.did(dve.tensor_scalar(e[:, 0, :], blocks(cs_all, r), EPS, None, ALU.add))
                steps.did(dve.tensor_scalar(e[:, 2, :], cs, 0.0, None, ALU.not_equal))
                steps.settle()
                steps.did(dve.reciprocal(e[:, 1, :], e[:, 0, :]))
                steps.did(dve.tensor_scalar(w[:, 1, :], e[:, 2, :], -1.0, 1.0, ALU.mult, ALU.add))
                steps.settle()
                steps.did(dve.tensor_tensor(e[:, 3, :], cs, e[:, 1, :], ALU.mult))
                for b in range(BLK):
                    steps.did(dve.tensor_scalar(diag[:, b, :], ident[:, :], w[:, 1, b:b + 1], None, ALU.mult))
                steps.settle()
                steps.did(dve.tensor_scalar(e[:, 0, :], e[:, 3, :], EPS, None, ALU.add))
                steps.settle()
                steps.did(dve.reciprocal(e[:, 4, :], e[:, 0, :]))
                steps.settle()
                steps.did(dve.tensor_tensor(e[:, 5, :], e[:, 4, :], e[:, 2, :], ALU.mult))
                steps.settle()
                steps.did(dve.tensor_tensor(e[:, 1, :], e[:, 1, :], e[:, 5, :], ALU.mult))
                steps.did(dve.tensor_tensor(e[:, 3, :], e[:, 3, :], e[:, 5, :], ALU.mult))
                steps.settle()
                steps.did(dve.tensor_tensor(w[:, 0, :], e[:, 1, :], w[:, 1, :], ALU.add))
                steps.did(dve.tensor_tensor(w[:, 2, :], e[:, 3, :], w[:, 1, :], ALU.add))
                steps.settle()
                dve.tensor_copy(blocks(s_all, r), w[:, 0, :]).then_inc(S.edge_ready, 1)

            def layer1(r, rp):
                dve.wait_ge(S.t1_ready, r + 1)
                for b in range(BLK):
                    dve.wait_ge(S.p12_done, r * BLK + (b + 1))
                    steps.did(dve.scalar_tensor_tensor(z[:, b, :], ps[:, T[b], 0:H], st[:, rp, 0, b:b + 1],
                                                       t1[:, b, :], ALU.mult, ALU.add))
                steps.settle()
                for b in range(BLK):
                    ins = dve.tensor_tensor(z[:, b, :], z[:, b, :], ps[:, T[b], H:2 * H], ALU.add)
                    steps.did(ins)
                steps.settle()
                dve.sem_inc(S.z_ready, 1)
                ln_stats(steps, dve, lambda b: z[:, b, :]).then_inc(S.stats_ready, 1)

            def layer2(r, rp):
                dve.wait_ge(S.w2_done, r + 1)
                v, t = z[:, :, 0:D], z[:, :, D:2 * D]
                for g in range(2):
                    res = T2(2 + g).rearrange("p (b n) -> p b n", b=2)
                    steps.did(dve.tensor_tensor(v[:, 2 * g:2 * g + 2, :], res[:, :, 0:D],
                                                bb2B[:, :].unsqueeze(1).to_broadcast([P, 2, D]), ALU.add))
                steps.settle()
                steps.did(dve.tensor_copy(blocks3(vh, r), v))
                for b in range(BLK):
                    steps.did(dve.scalar_tensor_tensor(t[:, b, :], v[:, b, :], st[:, rp, 1, b:b + 1], bo2B[:, :],
                                                       ALU.mult, ALU.add))
                steps.settle()
                steps.did(dve.tensor_tensor(blocks3(vl, r), v, blocks3(vh, r).bitcast(FP32), ALU.subtract))
                for g in range(2):
                    res = T2(2 + g).rearrange("p (b n) -> p b n", b=2)
                    steps.did(dve.tensor_tensor(self2[:, bass.ds(r * BLK + 2 * g, 2), :], t[:, 2 * g:2 * g + 2, :],
                                                res[:, :, D:2 * D], ALU.add))
                steps.settle()
                dve.sem_inc(S.v_done, 1)

            def panel(p, par):
                post = not (isinstance(p, int) and p == 0)
                if post:
                    r, rp = p - 1, 1 - par
                for q in range(SLOTS):
                    slot(p, q)
                    if post and q == 1:
                        edge(r, rp)
                    if post and q == 3:
                        layer1(r, rp)
                if post:
                    dve.wait_ge(S.sums_out, p)
                fold(p)
                if post:
                    layer2(r, rp)
            panel_loop(dve, steps, per_panel, panel)
            r = PANELS - 1
            edge(r, 1)
            layer1(r, 1)
            layer2(r, 1)
            return steps

        def general_gate(eng, gate):
            eng.drain().then_inc(gate, 1)
            eng.wait_ge(gate, 5)

        def sp_general(sp):
            general_gate(sp, gen_enter)
            sp.wait_ge(gen_cs_row, 1)
            sp.dma_start(cs_dram.rearrange("(k p) -> k p", p=P), crow[:, :]).then_inc(gen_stored, 16)
            sp.wait_ge(gen_stored, 16)
            with sp.Fori(0, PANELS) as p:
                sp.dma_start(t1[:, 0:2, :].rearrange("p b n -> p (b n)"),
                             cs_dram[bass.ds(p * PANEL, PANEL)].partition_broadcast(P)).then_inc(gen_cs_in, 16)
                for q in range(SLOTS):
                    sp.wait_ge(gen_stored, p * (16 * SLOTS) + (16 * q + 16))
                    sp.dma_start(slot_view(0), column_panel(adj, p, q)).then_inc(gen_in, 16)
                    sp.wait_ge(gen_masked, p * SLOTS + (q + 1))
                    sp.dma_start(column_panel(masked_dram, p, q), slot_view(0)).then_inc(gen_stored, 16)
            sp.wait_ge(gen_stored, 16 * PANELS * SLOTS + 16)
            sp_pass1(sp, SG, masked_dram, None)
            general_gate(sp, gen_leave)

        def dve_general(dve):
            general_gate(dve, gen_enter)
            steps = Steps(dve, gen_step)
            per = 2 + SLOTS * BLK * 2
            rB, tmp = z[:, 0:2, :].rearrange("p b n -> p (b n)"), z[:, 2:4, :].rearrange("p b n -> p (b n)")
            with dve.Fori(0, PANELS) as p:
                steps.enter(p * per)
                dve.wait_ge(gen_cs_in, p * 16 + 16)
                steps.did(dve.tensor_scalar(rB, t1[:, 0:2, :].rearrange("p b n -> p (b n)"), EPS, None, ALU.add))
                steps.settle()
                steps.did(dve.reciprocal(rB, rB))
                steps.settle()
                for q in range(SLOTS):
                    dve.wait_ge(gen_in, p * (16 * SLOTS) + 16 * (q + 1))
                    for b in range(BLK):
                        m = ring[:, 0, b * PANEL:(b + 1) * PANEL]
                        steps.did(dve.tensor_tensor(tmp, m, rB, ALU.mult))
                        steps.settle()
                        steps.did(dve.scalar_tensor_tensor(m, tmp, THRESH, m, ALU.is_gt, ALU.mult))
                        steps.settle()
                    dve.sem_inc(gen_masked, 1)
                assert steps.n == per
            dve_pass1(dve, SG, False, PER_DVE1G)
            general_gate(dve, gen_leave)

        def pe_general(pe):
            general_gate(pe, gen_enter)
            pe.transpose(ps[0:CHUNKS, T[0], 0:P], cs_all[:, :], ident[:, :]).then_inc(gen_cs_t, 1)
            pe_pass1(pe, SG)
            general_gate(pe, gen_leave)

        def act_general(act):
            general_gate(act, gen_enter)
            act.wait_ge(gen_cs_t, 1)
            act.activation(crow[:, :], ps[0:CHUNKS, T[0], 0:P], ACT.Copy).then_inc(gen_cs_row, 1)
            act_pass1(act, SG, False)
            general_gate(act, gen_leave)

        def pool_general(pool):
            general_gate(pool, gen_enter)
            pool_pass1(pool, SG)
            general_gate(pool, gen_leave)

        def general(eng, path):
            eng.wait_ge(flag_ready, 1)
            flag = eng.value_load(flag_i[0:1, 0:1], min_val=0, max_val=1)
            with eng.If(flag > 0):
                path(eng)

        PER_DVE1, PER_DVE1G, PER_DVE2, PER_DVE3 = 59, 59, 54, 26

        HALF = SLOTW // 2

        def half_of(t, h):
            k = h % 4
            return t[:, 2 * k:2 * k + 2, :].rearrange("p a n -> p (a n)")

        def split_waits(eng, p, h):
            if isinstance(p, int) and p == 0:
                if h >= 4:
                    eng.wait_ge(used2, h - 3)
            else:
                eng.wait_ge(used2, p * (2 * SLOTS) + (h - 3))

        def act_pass2(act):
            act.wait_ge(S1.v_done, PANELS)

            def half(p, h):
                if h % 2 == 0:
                    act.wait_ge(loaded[h // 2], (p + (PANELS + 1)) * 16)
                split_waits(act, p, h)
                act.activation(half_of(mh, h), ring[:, h // 2, (h % 2) * HALF:(h % 2 + 1) * HALF],
                               ACT.Copy).then_inc(hi2, 1)

            def post_a(r, rp):
                act.wait_ge(used2, r * (2 * SLOTS) + 2 * SLOTS)
                act.activation(uts[:, :], ps[:, rp, :], ACT.Copy).then_inc(y_copied, 1)

            def norm(r, which, dst):
                act.wait_ge(stats2, r * 2 + (which + 1))
                for b in range(BLK):
                    last = act.activation(dst(b), z[:, b, 0:D], ACT.Identity, scale=ln[:, 3, b:b + 1],
                                          bias=ln[:, 4, b:b + 1])
                last.then_inc(normed2, 1)

            def panel(p, par):
                post = not (isinstance(p, int) and p == 0)
                for h in range(2 * SLOTS):
                    half(p, h)
                    if post and h == 1:
                        post_a(p - 1, 1 - par)
                    if post and h == 7:
                        norm(p - 1, 0, lambda b: z[:, b, D:2 * D])
                    if post and h == 13:
                        norm(p - 1, 1, lambda b: z[:, b, D:2 * D])
            panel_loop(act, None, 0, panel)
            r = PANELS - 1
            post_a(r, 1)
            norm(r, 0, lambda b: z[:, b, D:2 * D])
            norm(r, 1, lambda b: z[:, b, D:2 * D])

        def pool_pass2(pool):
            steps = Steps(pool, pool_step2)

            def post(r):
                pool.wait_ge(normed2, r * 2 + 1)
                steps.did(pool.tensor_tensor(z[:, :, D:2 * D], z[:, :, D:2 * D],
                                             g2B[:, :].unsqueeze(1).to_broadcast([P, BLK, D]), ALU.mult))
                steps.settle()
                pool.tensor_tensor(z[:, :, D:2 * D], z[:, :, D:2 * D],
                                   be2B[:, :].unsqueeze(1).to_broadcast([P, BLK, D]), ALU.add).then_inc(affine2, 1)

            def panel(p, par):
                if not (isinstance(p, int) and p == 0):
                    post(p - 1)
            panel_loop(pool, steps, 1, panel)
            post(PANELS - 1)

        def dve_pass2(dve):
            steps = Steps(dve, dve_step2)

            def half(p, h):
                if h % 2 == 0:
                    dve.wait_ge(loaded[h // 2], (p + (PANELS + 1)) * 16)
                split_waits(dve, p, h)
                dve.wait_ge(hi2, p * (2 * SLOTS) + (h + 1))
                dve.tensor_tensor(half_of(ml, h), ring[:, h // 2, (h % 2) * HALF:(h % 2 + 1) * HALF],
                                  half_of(mh, h).bitcast(FP32), ALU.subtract).then_inc(lo2, 1)

            def layer(r):
                steps.did(dve.tensor_copy(s4[:, :], blocks(s_all, r)))
                steps.settle()
                dve.wait_ge(yt_done, r + 1)
                for b in range(BLK):
                    steps.did(dve.scalar_tensor_tensor(z[:, b, 0:D], ps[:, T[0], b * P:(b + 1) * P], s4[:, b:b + 1],
                                                       one_block(self2, r, b), ALU.mult, ALU.add))
                steps.settle()
                dve.sem_inc(self_used, 1)
                dve.sem_inc(z2_ready, 1)
                ln_stats(steps, dve, lambda b: z[:, b, 0:D]).then_inc(stats2, 1)

            def residual(r, rp):
                dve.wait_ge(affine2, r + 1)
                dve.wait_ge(xp_in[rp], xp2_count(r, rp))
                steps.did(dve.scalar_tensor_tensor(z[:, :, 0:D], z[:, :, D:2 * D], 0.0, xp[:, rp], ALU.max, ALU.add))
                steps.settle()
                ln_stats(steps, dve, lambda b: z[:, b, 0:D]).then_inc(stats2, 1)

            def split_x1(r):
                dve.wait_ge(normed2, r * 2 + 2)
                steps.did(dve.tensor_copy(blocks3(x1h, r), z[:, :, D:2 * D]))
                steps.settle()
                steps.did(dve.tensor_tensor(blocks3(x1l, r), z[:, :, D:2 * D], blocks3(x1h, r).bitcast(FP32),
                                            ALU.subtract))
                steps.settle()
                dve.sem_inc(x1_done, 1)

            def panel(p, par):
                post = not (isinstance(p, int) and p == 0)
                for h in range(2 * SLOTS):
                    half(p, h)
                    if post and h == 5:
                        layer(p - 1)
                    if post and h == 11:
                        residual(p - 1, 1 - par)
                if post:
                    split_x1(p - 1)
            panel_loop(dve, steps, PER_DVE2, panel)
            r = PANELS - 1
            layer(r)
            residual(r, 1)
            split_x1(r)

        def xp2_count(r, par):
            if isinstance(r, int):
                return 16 * (PANELS // 2 + r // 2 + 1)
            return (r - par) * 8 + (16 + 8 * PANELS)

        def pe_pass2(pe):
            def stage(r):
                pe.wait_ge(y_copied, r + 1)
                if isinstance(r, int) and r == PANELS - 1:
                    pe.wait_ge(z2_ready, r)
                for b in range(BLK):
                    last = pe.transpose(ps[:, T[0], b * P:(b + 1) * P], uts[:, b * P:(b + 1) * P], ident[:, :])
                last.then_inc(yt_done, 1)

            def panel(p, par):
                post = not (isinstance(p, int) and p == 0)
                for h in range(2 * SLOTS):
                    pe.wait_ge(hi2, p * (2 * SLOTS) + (h + 1))
                    if h == 0:
                        pe.wait_ge(S1.u_copied, PANELS)
                    for a in range(2):
                        k = 2 * h + a
                        m = mh[:, 2 * (h % 4) + a, :]
                        pe.matmul(ps[:, par, :], vh[:, k, :], m, start=(k == 0), stop=False)
                        pe.matmul(ps[:, par, :], vl[:, k, :], m, start=False, stop=False)
                    pe.wait_ge(lo2, p * (2 * SLOTS) + (h + 1))
                    for a in range(2):
                        k = 2 * h + a
                        last = pe.matmul(ps[:, par, :], vh[:, k, :], ml[:, 2 * (h % 4) + a, :], start=False,
                                         stop=(k == CHUNKS - 1))
                    last.then_inc(used2, 1)
                    if post and h == 3:
                        stage(p - 1)
            panel_loop(pe, None, 0, panel)
            stage(PANELS - 1)

        TR, M3 = (3, 4), (5, 6)
        A3 = ((0, 2), (1, 7))

        def pe_pass3(pe):
            def transposes(p, k):
                q, jc = k // BLK, k % BLK
                if jc == 0:
                    pe.wait_ge(loaded[q], (p + (2 * PANELS + 1)) * 16)
                if isinstance(p, int) and p == 0:
                    if k >= 2:
                        pe.wait_ge(hi3, k - 1)
                        pe.wait_ge(lo3, k - 1)
                    else:
                        pe.wait_ge(z2_ready, PANELS)
                else:
                    pe.wait_ge(hi3, p * CHUNKS + (k - 1))
                    pe.wait_ge(lo3, p * CHUNKS + (k - 1))
                for b in range(BLK):
                    last = pe.transpose(ps[:, TR[k % 2], b * P:(b + 1) * P],
                                        ring[:, q, b * PANEL + jc * P:b * PANEL + (jc + 1) * P], ident[:, :])
                last.then_inc(tr_done, 1)

            def products(p, par, k):
                a1, a2 = A3[par]
                h, l = mh[:, k % 8, :], ml[:, k % 8, :]
                pe.wait_ge(hi3, p * CHUNKS + (k + 1))
                for bank, sh, sl in ((a1, x1h, x1l), (a2, vh, vl)):
                    pe.matmul(ps[:, bank, :], sh[:, k, :], h, start=(k == 0), stop=False)
                    pe.matmul(ps[:, bank, :], sl[:, k, :], h, start=False, stop=False)
                pe.wait_ge(lo3, p * CHUNKS + (k + 1))
                for bank, sh in ((a1, x1h), (a2, vh)):
                    last = pe.matmul(ps[:, bank, :], sh[:, k, :], l, start=False, stop=(k == CHUNKS - 1))
                last.then_inc(used3, 1)

            def mlp(r, layer):
                if layer == 0:
                    pe.wait_ge(a_copied, r * 2 + 2)
                else:
                    pe.wait_ge(relu_done, r * 6 + 2 * layer)
                for g, (w, src) in enumerate(((w1t, uts), (w2t, xts))):
                    last = pe.matmul(ps[:, M3[g], :], w[:, layer, :], src[:, :], start=True, stop=True)
                    last.then_inc(mlp_done, 1)

            def merge(r):
                pe.wait_ge(relu_done, r * 6 + 6)
                for b in range(BLK):
                    pe.matmul(ps[:, M3[0], b * P:(b + 1) * P], uts[:, b * P:(b + 1) * P], wmt[:, 0, :],
                              start=True, stop=False, skip_group_check=True)
                    last = pe.matmul(ps[:, M3[0], b * P:(b + 1) * P], xts[:, b * P:(b + 1) * P], wmt[:, 1, :],
                                     start=False, stop=True, skip_group_check=True)
                last.then_inc(merged, 1)

            pe.wait_ge(x1_done, PANELS)
            pe.wait_ge(x2_hi, PANELS)
            pe.wait_ge(x2_lo, PANELS)

            def panel(p, par):
                post = not (isinstance(p, int) and p == 0)
                if isinstance(p, int) and p == 0:
                    transposes(p, 0)
                for k in range(CHUNKS):
                    if k + 1 < CHUNKS:
                        transposes(p, k + 1)
                    elif not (isinstance(p, int) and p == PANELS - 1):
                        transposes(p + 1, 0)
                    products(p, par, k)
                    if post and k in (3, 7, 11):
                        mlp(p - 1, (k - 3) // 4)
                    if post and k == 15:
                        merge(p - 1)
            panel_loop(pe, None, 0, panel)
            r = PANELS - 1
            for layer in range(3):
                mlp(r, layer)
            merge(r)

        def act_x2(act):
            for k in range(PANELS):
                act.wait_ge(used2, (PANELS - 1) * 2 * SLOTS + 2 * k + 2)
                act.wait_ge(x2_in[k], 16)
                act.activation(vh[:, BLK * k:BLK * k + BLK, :], self2[:, BLK * k:BLK * k + BLK, :],
                               ACT.Copy).then_inc(x2_hi, 1)

        def dve_x2(dve):
            for k in range(PANELS):
                dve.wait_ge(x2_in[k], 16)
                dve.wait_ge(x2_hi, k + 1)
                dve.tensor_tensor(vl[:, BLK * k:BLK * k + BLK, :], self2[:, BLK * k:BLK * k + BLK, :],
                                  vh[:, BLK * k:BLK * k + BLK, :].bitcast(FP32), ALU.subtract).then_inc(x2_lo, 1)

        def buffer_free(eng, p, k):
            if isinstance(p, int) and p == 0:
                if k >= 8:
                    eng.wait_ge(used3, k - 7)
                else:
                    eng.wait_ge(used2, PANELS * 2 * SLOTS)
            else:
                eng.wait_ge(used3, p * CHUNKS + (k - 7))

        def act_pass3(act):
            act.sem_inc(stored, 16)
            act_x2(act)

            def chunk(p, k):
                act.wait_ge(tr_done, p * CHUNKS + (k + 1))
                buffer_free(act, p, k)
                act.activation(mh[:, k % 8, :], ps[:, TR[k % 2], :], ACT.Copy).then_inc(hi3, 1)

            def copies(r, rp):
                act.wait_ge(used3, r * CHUNKS + CHUNKS)
                for g, dst in enumerate((uts, xts)):
                    act.activation(dst[:, :], ps[:, A3[rp][g], :], ACT.Copy, scale=scl[:, g:g + 1]) \
                        .then_inc(a_copied, 1)

            def relus(r, layer):
                for g, dst in enumerate((uts, xts)):
                    act.wait_ge(mlp_done, r * 6 + (2 * layer + 2))
                    act.activation(dst[:, :], ps[:, M3[g], :], ACT.Relu, bias=bcol[:, g, layer:layer + 1]) \
                        .then_inc(relu_done, 1)

            def norm(r, rp):
                act.wait_ge(stats3, r + 1)
                act.wait_ge(stored, r * 16 + 16)
                for b in range(BLK):
                    last = act.activation(z[:, b, D:2 * D], z[:, b, 0:D], ACT.Identity, scale=ln[:, 3, b:b + 1],
                                          bias=ln[:, 4, b:b + 1])
                last.then_inc(normed3, 1)
                act.wait_ge(normed3, r + 1)
                act.dma_start(blocks3(out_rows, r), z[:, :, D:2 * D]).then_inc(stored, 16)

            def panel(p, par):
                post = not (isinstance(p, int) and p == 0)
                for k in range(CHUNKS):
                    chunk(p, k)
                    if post and k == 0:
                        copies(p - 1, 1 - par)
                    if post and k in (4, 8, 12):
                        relus(p - 1, (k - 4) // 4)
                    if post and k == 24:
                        norm(p - 1, 1 - par)
            panel_loop(act, None, 0, panel)
            r = PANELS - 1
            copies(r, 1)
            for layer in range(3):
                relus(r, layer)
            norm(r, 1)
            act.wait_ge(stored, 16 * PANELS + 16)

        def dve_pass3(dve):
            dve_x2(dve)
            steps = Steps(dve, dve_step3)

            def chunk(p, k):
                buffer_free(dve, p, k)
                dve.wait_ge(hi3, p * CHUNKS + (k + 1))
                dve.tensor_tensor(ml[:, k % 8, :], ps[:, TR[k % 2], :], mh[:, k % 8, :].bitcast(FP32),
                                  ALU.subtract).then_inc(lo3, 1)

            def residual(r, rp):
                zz = z[:, :, 0:D]
                steps.did(dve.tensor_tensor(zz, blocks3(x1h, r).bitcast(FP32), blocks3(x1l, r).bitcast(FP32), ALU.add))
                steps.settle()
                steps.did(dve.tensor_tensor(zz, zz, bmB[:, :].unsqueeze(1).to_broadcast([P, BLK, D]), ALU.add))
                steps.settle()
                dve.wait_ge(merged, r + 1)
                steps.did(dve.tensor_tensor(zz, zz, ps[:, M3[0], :].rearrange("p (b d) -> p b d", b=BLK), ALU.add))
                steps.settle()
                dve.sem_inc(z3_ready, 1)
                ln_stats(steps, dve, lambda b: z[:, b, 0:D]).then_inc(stats3, 1)

            def panel(p, par):
                post = not (isinstance(p, int) and p == 0)
                for k in range(CHUNKS):
                    chunk(p, k)
                    if post and k == 18:
                        residual(p - 1, 1 - par)
            panel_loop(dve, steps, PER_DVE3, panel)
            residual(PANELS - 1, 1)

        block = ctx.enter_context(nc.Block())

        @block.sync
        def _(sp):
            sp.dma_start(st_in1, W_in1).then_inc(weights_in, 16)
            sp.dma_start(st_out1, W_out1.rearrange("(c k) n -> k c n", c=2)).then_inc(weights_in, 16)
            sp.dma_start(st_in2, W_in2.rearrange("(c k) n -> k c n", c=2)).then_inc(weights_in, 16)
            sp.dma_start(st_out2, W_out2).then_inc(weights_in, 16)
            sp.dma_start(st_w1, W1.rearrange("l o i -> o l i")).then_inc(weights_in, 16)
            sp.dma_start(st_w2, W2.rearrange("l o i -> o l i")).then_inc(weights_in, 16)
            sp.dma_start(st_wm, Wm).then_inc(weights_in, 16)
            sp.dma_start(xs[:, :, :], rows_of).then_inc(x_in, 16)
            sp_pass1(sp, S1, adj, True)
            sp.wait_ge(flag_ready, 1)
            flag = sp.value_load(flag_i[0:1, 0:1], min_val=0, max_val=1)
            with sp.If(flag > 0):
                sp_general(sp)
                sp_pass2(sp, masked_dram)
            with sp.Else():
                sp_pass2(sp, adj)
            sp_pass3(sp)

        @block.gpsimd
        def _(pool):
            pool.memset(ident[:, :], 0.0).then_inc(const_ready, 1)
            pool.memset(ones[:, :], 1.0).then_inc(const_ready, 1)
            pool.memset(nbig[:, :], -BIG).then_inc(const_ready, 1)
            pool.wait_ge(const_ready, 3)
            pool.affine_select(out=ident[:, :], in_=ident[:, :], compare_op=ALU.not_equal, fill=1.0, base=0,
                               pattern=[[-1, P]], channel_multiplier=1).then_inc(const_ready, 1)
            pool_pass1(pool, S1)
            general(pool, pool_general)
            pool_pass2(pool)

        @block.scalar
        def _(act):
            for dst, src in ((wA[:, 1, :], W_self1), (wB[:, :, D:2 * D], W_self2.rearrange("(c k) n -> k c n", c=2)),
                             (bs1B[:, :], b_out1.partition_broadcast(P)), (st_bs, b_self1.partition_broadcast(P)),
                             (g1B[:, :], g1.partition_broadcast(P)), (be1B[:, :], be1.partition_broadcast(P)),
                             (bo2B[:, :], b_out2.partition_broadcast(P)), (st_bo, b_self2.partition_broadcast(P)),
                             (g2B[:, :], g2.partition_broadcast(P)), (be2B[:, :], be2.partition_broadcast(P)),
                             (bmB[:, :], bm.partition_broadcast(P)),
                             (scl[:, 0:1], eps1.partition_broadcast(P)), (scl[:, 1:2], eps2.partition_broadcast(P))):
                act.dma_start(dst, src).then_inc(consts_in, 16)
            with nc.allow_non_contiguous_dma("columns of the small bias vectors"):
                for dst, src in ((bincol[:, 0:2], b_in1.rearrange("(c k) -> k c", c=2)),
                                 (bincol[:, 2:3], b_in2.rearrange("(c k) -> k c", c=1)),
                                 (bcol[:, 0, :], b1.rearrange("l d -> d l")),
                                 (bcol[:, 1, :], b2.rearrange("l d -> d l"))):
                    act.dma_start(dst, src).then_inc(consts_in, 16)
            act.wait_ge(setup_t, 1)
            act.activation(st_in1T, ps[:, T[0], 0:2 * P].rearrange("p (c n) -> p c n", c=2), ACT.Copy) \
                .then_inc(setup_c, 1)
            act.activation(st_in2T, ps[:, T[0], 2 * P:4 * P].rearrange("p (c n) -> p c n", c=2), ACT.Copy) \
                .then_inc(setup_c, 1)
            act.activation(w1t[:, :, :], ps[:, T[1], 0:3 * P].rearrange("p (c n) -> p c n", c=3), ACT.Copy) \
                .then_inc(setup_c, 1)
            act.activation(w2t[:, :, :], ps[:, T[2], 0:3 * P].rearrange("p (c n) -> p c n", c=3), ACT.Copy) \
                .then_inc(setup_c, 1)
            act.activation(wmt[:, :, :], ps[:, T[3], 0:2 * P].rearrange("p (c n) -> p c n", c=2), ACT.Copy) \
                .then_inc(setup_c, 1)
            act_pass1(act, S1, True)
            general(act, act_general)
            act_pass2(act)
            act_pass3(act)

        @block.tensor
        def _(pe):
            pe.wait_ge(const_ready, 4)
            pe.wait_ge(weights_in, 16 * 7)
            for c in range(2):
                pe.transpose(ps[:, T[0], c * P:(c + 1) * P], st_in1[:, c * P:(c + 1) * P], ident[:, :])
                pe.transpose(ps[:, T[0], (2 + c) * P:(3 + c) * P], st_in2[:, c, :], ident[:, :])
                last = pe.transpose(ps[:, T[3], c * P:(c + 1) * P], st_wm[:, c * P:(c + 1) * P], ident[:, :])
            for l in range(3):
                pe.transpose(ps[:, T[1], l * P:(l + 1) * P], st_w1[:, l, :], ident[:, :])
                last = pe.transpose(ps[:, T[2], l * P:(l + 1) * P], st_w2[:, l, :], ident[:, :])
            last.then_inc(setup_t, 1)
            pe.wait_ge(setup_c, 7)
            for c in range(2):
                pe.matmul(ps[:, T[0], 0:H], st_in1T[:, c, :], st_out1[:, c, :], start=(c == 0), stop=(c == 1))
            for c in range(2):
                pe.matmul(ps[:, T[0], H:2 * H], st_b[:, c, :], st_out1[:, c, :], start=(c == 0), stop=(c == 1))
            for c in range(2):
                pe.matmul(ps[:, T[1], c * D:(c + 1) * D], st_in2T[:, c, :], st_out2, start=True, stop=True)
            pe.matmul(ps[:, T[1], 2 * D:3 * D], st_b[:, 2, :], st_out2, start=True, stop=True).then_inc(setup_m, 1)
            pe.wait_ge(x_in, 16)
            pe_pass1(pe, S1)
            pe.wait_ge(bad_ready, 1)
            pe.matmul(ps[:, SMALL, 8:9], ones[:, :], fl[:, 3:4], start=True, stop=True).then_inc(bad_summed, 1)
            general(pe, pe_general)
            pe_pass2(pe)
            pe_pass3(pe)

        @block.vector
        def _(dve):
            dve.wait_ge(const_ready, 4)
            dve.wait_ge(consts_in, 16 * 17)
            for k in range(3):
                last = dve.tensor_scalar(st_b[:, k, :], ones[:, :], bincol[:, k:k + 1], None, ALU.mult)
            dve.drain()
            dve.sem_inc(setup_c, 2)
            dve.tensor_tensor(bs1B[:, :], bs1B[:, :], st_bs, ALU.add)
            dve.tensor_tensor(bo2B[:, :], bo2B[:, :], st_bo, ALU.add)
            dve.tensor_scalar(scl[:, :], scl[:, :], 2.0, None, ALU.add)
            dve.wait_ge(setup_m, 1)
            dve.tensor_copy(wA[:, 0, :], ps[:, T[0], 0:H])
            dve.tensor_copy(bw1B[:, :], ps[:, T[0], H:2 * H])
            dve.tensor_copy(wB[:, :, 0:D], ps[:, T[1], 0:2 * D].rearrange("p (c n) -> p c n", c=2))
            dve.tensor_copy(bb2B[:, :], ps[:, T[1], 2 * D:3 * D])
            dve.drain().then_inc(setup_done, 1)
            steps = dve_pass1(dve, S1, True, PER_DVE1)
            dve.wait_ge(S1.slot_act, PANELS * SLOTS)
            dve.scalar_tensor_tensor(sg[:, :], nz[:, :], 2.0, sg[:, :], ALU.mult, ALU.add, accum_out=fl[:, 0:1])
            dve.reduce_max(fl[:, 1:2], cs_all[:, :], AX.X)
            dve.drain()
            dve.tensor_scalar(fl[:, 0:1], fl[:, 0:1], float(PANELS * SLOTS * SLOTW), None, ALU.not_equal)
            dve.tensor_scalar(fl[:, 1:2], fl[:, 1:2], CS_LIMIT, None, ALU.is_gt)
            dve.drain()
            dve.tensor_tensor(fl[:, 3:4], fl[:, 0:1], fl[:, 1:2], ALU.max).then_inc(bad_ready, 1)
            dve.wait_ge(bad_summed, 1)
            dve.tensor_scalar(flag_i[:, :], ps[:, SMALL, 8:9], 1.0, None, ALU.min).then_inc(flag_ready, 1)
            general(dve, dve_general)
            dve_pass2(dve)
            dve_pass3(dve)


_INS = ['x', 'adj'] + ['L0_gnn_' + n for n in ('W_in1', 'b_in1', 'W_out1', 'b_out1', 'W_self1', 'b_self1', 'g1', 'be1',
                                               'W_in2', 'b_in2', 'W_out2', 'b_out2', 'W_self2', 'b_self2', 'g2', 'be2')] \
    + ['L1_gnn_' + n for n in ('x2', 'eps1', 'eps2', 'W1', 'b1', 'W2', 'b2', 'Wm', 'bm')]
_OUTS = [((N, D), 'float32')]


def kernel(**inputs):
    import numpy as _np
    import concourse.bacc as _bacc
    from concourse import mybir as _mybir
    from concourse.bass_utils import run_bass_kernel_spmd as _run

    nc = _bacc.Bacc("TRN2", target_bir_lowering=False, num_devices=1)
    arrays, args = {}, []
    for name in _INS:
        a = _np.ascontiguousarray(inputs[name])
        arrays[f"in_{name}_dram"] = a
        args.append(nc.dram_tensor(f"in_{name}_dram", a.shape, _mybir.dt.from_np(a.dtype), kind="ExternalInput").ap())
    for i, (shape, dtype) in enumerate(_OUTS):
        dt = _mybir.dt.from_np(_np.dtype(dtype))
        args.append(nc.dram_tensor(f"out_{i}_dram", shape, dt, kind="ExternalOutput").ap())
    gnn_program(nc, *args)
    r = _run(nc, [arrays], core_ids=[0])
    got = tuple(r.results[0][f"out_{i}_dram"] for i in range(len(_OUTS)))
    return got[0]
```

```python
from contextlib import ExitStack

import concourse.bass as bass
from concourse import mybir

FP32 = mybir.dt.float32
F32R = mybir.dt.float32r
I32 = mybir.dt.int32
I8 = mybir.dt.int8
U8 = mybir.dt.uint8
ALU = mybir.AluOpType
ACT = mybir.ActivationFunctionType
AX = mybir.AxisListType

N = 4096
D = 128
H = 256
P = 128
PANEL = 512
PANELS = N // PANEL
SLOTS = 8
BLK = PANEL // P
CHUNKS = N // P
SLOTW = BLK * PANEL
SQ = 32
QUADS = P // SQ
ROW_SLOTS = 4
QUARTERS = 4
QC = CHUNKS // QUARTERS
THRESH = 1e-06
EPS = 1e-08
LN_EPS = 1e-05
BIG = 2.0 ** -7
CS_LIMIT = 0.99 * BIG / THRESH
RSQRT_SEED = float(0x5F3759DF)
ACT_ZERO_SLOTS = (0, 1, 2, 4, 5, 7)
DVE_ZERO_SLOTS = tuple(q for q in range(SLOTS) if q not in ACT_ZERO_SLOTS)


class Steps:

    def __init__(self, eng, sem):
        self.eng, self.sem, self.base, self.n = eng, sem, 0, 0

    def did(self, ins):
        ins.then_inc(self.sem, 1)
        self.n += 1

    def settle(self):
        self.eng.wait_ge(self.sem, self.base + self.n)

    def enter(self, base):
        self.base, self.n = base, 0


class Pass1Signals:

    def __init__(self, sem, tag, loaded, xp_in):
        self.loaded, self.xp_in = loaded, xp_in
        self.slot_pe = sem("slot_pe_" + tag)
        self.slot_act = sem("slot_act_" + tag)
        self.slot_dve = sem("slot_dve_" + tag)
        self.folded = sem("folded_" + tag)
        self.sums_out = sem("sums_out_" + tag)
        self.edge_ready = sem("edge_ready_" + tag)
        self.u_done = sem("u_done_" + tag)
        self.xp_used = sem("xp_used_" + tag)
        self.u_copied = sem("u_copied_" + tag)
        self.xt_copied = sem("xt_copied_" + tag)
        self.p12_done = sem("p12_done_" + tag)
        self.t1_ready = sem("t1_ready_" + tag)
        self.z_ready = sem("z_ready_" + tag)
        self.factors = sem("factors_" + tag)
        self.stats_ready = sem("stats_ready_" + tag)
        self.normed = sem("normed_" + tag)
        self.ht_done = sem("ht_done_" + tag)
        self.ht_copied = sem("ht_copied_" + tag)
        self.w2_done = sem("w2_done_" + tag)
        self.v_done = sem("v_done_" + tag)
        self.dve_step = sem("dve_step_" + tag)
        self.pool_step = sem("pool_step_" + tag)


def panel_loop(eng, steps, per_panel, body):
    body(0, 0)
    before = steps.n if steps else 0
    assert not steps or steps.base == 0
    with eng.Fori(0, (PANELS - 2) // 2) as pair:
        for k in range(2):
            p = pair * 2 + (1 + k)
            if steps:
                steps.enter(pair * (2 * per_panel) + (before + k * per_panel))
            body(p, (1 + k) % 2)
            assert not steps or steps.n == per_panel, (steps.n, per_panel)
    if steps:
        steps.enter(before + (PANELS - 2) * per_panel)
    body(PANELS - 1, (PANELS - 1) % 2)


def gnn_program(nc, x, adj, W_in1, b_in1, W_out1, b_out1, W_self1, b_self1, g1, be1,
                W_in2, b_in2, W_out2, b_out2, W_self2, b_self2, g2, be2,
                x2, eps1, eps2, W1, b1, W2, b2, Wm, bm, out):
    ctx = ExitStack()
    with ctx:
        def sb(name, shape, dt=FP32, where=ctx):
            return where.enter_context(nc.sbuf_tensor(name, shape, dt))

        def sem(name):
            return ctx.enter_context(nc.semaphore(name))

        masked_dram = nc.dram_tensor("masked_adj", [N, N], FP32, kind="Internal").ap()
        cs_dram = nc.dram_tensor("column_sums", [N], FP32, kind="Internal").ap()
        x1_dram = nc.dram_tensor("x1_rows", [N, D], FP32, kind="Internal").ap()

        ring = sb("ring", [P, SLOTS, SLOTW])
        vh = sb("vh", [P, CHUNKS, D], F32R)
        vl = sb("vl", [P, CHUNKS, D], F32R)
        self2 = sb("self2", [P, CHUNKS, D])
        z = sb("z", [P, BLK, H])
        uts = sb("uts", [P, PANEL])
        xts = sb("xts", [P, PANEL])
        xp = sb("xp", [P, 2, BLK, D])
        ident = sb("ident", [P, P])
        ones = sb("ones", [P, P])
        w1t = sb("w1t", [P, 3, D])
        w2t = sb("w2t", [P, 3, D])
        wmt = sb("wmt", [P, 2, D])
        g2B = sb("g2B", [P, D])
        be2B = sb("be2B", [P, D])
        bmB = sb("bmB", [P, D])
        bcol = sb("bcol", [P, 2, 3])
        scl = sb("scl", [P, 2])
        s_all = sb("s_all", [P, CHUNKS])
        cs_all = sb("cs_all", [P, CHUNKS])
        s4 = sb("s4", [P, BLK])
        bnst = sb("bnst", [P, BLK, 6])
        mv = sb("mv", [P, BLK, 2])
        ln = sb("ln", [P, 5, BLK])
        spare = sb("spare", [P, 1])
        flag_i = sb("flag_i", [P, 1], I32)

        lnc = sb("lnc", [P, 4, BLK])

        first = ExitStack()
        xs = sb("xs", [P, CHUNKS, D], where=first)
        acc = sb("acc", [P, SLOTW], where=first)
        accf = sb("accf", [P, PANEL], where=first)
        junk_a = sb("junk_a", [P, SLOTW], I8, where=first)
        junk_b = sb("junk_b", [P, SLOTW], I8, where=first)
        junk_d = sb("junk_d", [P, SLOTW], U8, where=first)
        first.close()
        mh = sb("mh", [P, 8, PANEL], F32R)
        ml = sb("ml", [P, 8, PANEL], F32R)

        second = ExitStack()
        t1 = sb("t1", [P, BLK, H], where=second)
        hT = sb("hT", [P, 2, PANEL], where=second)
        diag = sb("diag", [P, BLK, P], where=second)
        wA = sb("wA", [P, 2, H], where=second)
        wB = sb("wB", [P, 2, H], where=second)
        bw1B = sb("bw1B", [P, H], where=second)
        bs1B = sb("bs1B", [P, H], where=second)
        bb2B = sb("bb2B", [P, D], where=second)
        bo2B = sb("bo2B", [P, D], where=second)
        g1col = sb("g1col", [P, 2], where=second)
        be1col = sb("be1col", [P, 2], where=second)
        st = sb("st", [P, 2, 3, BLK], where=second)
        ed = sb("ed", [P, 6, BLK], where=second)
        nz = sb("nz", [P, PANELS * SLOTS], where=second)
        sg = sb("sg", [P, PANELS * SLOTS], where=second)
        fl = sb("fl", [P, 4], where=second)
        nbig = sb("nbig", [P, 1], where=second)
        crow = sb("crow", [CHUNKS, P], where=second)
        bincol = sb("bincol", [P, 3], where=second)
        second.close()
        x1h = sb("x1h", [P, CHUNKS, D], F32R)
        x1l = sb("x1l", [P, CHUNKS, D], F32R)

        ps = ctx.enter_context(nc.psum_tensor("ps", [P, 8, PANEL], FP32))

        stage = self2[:, :, :].rearrange("p k n -> p (k n)")
        st_in1 = stage[:, 0:256]
        st_out1 = stage[:, 256:768].rearrange("p (c n) -> p c n", c=2)
        st_in2 = stage[:, 768:1024].rearrange("p (c n) -> p c n", c=2)
        st_out2 = stage[:, 1024:1152]
        st_w1 = stage[:, 1152:1536].rearrange("p (l n) -> p l n", l=3)
        st_w2 = stage[:, 1536:1920].rearrange("p (l n) -> p l n", l=3)
        st_wm = stage[:, 1920:2176]
        st_b = stage[:, 2176:2560].rearrange("p (k n) -> p k n", k=3)
        st_in1T = stage[:, 2560:2816].rearrange("p (c n) -> p c n", c=2)
        st_in2T = stage[:, 2816:3072].rearrange("p (c n) -> p c n", c=2)
        st_bs = stage[:, 3072:3328]
        st_bo = stage[:, 3328:3456]

        SMALL, T, YT = 2, (3, 4, 5, 6), 7

        def T2(i):
            return ps[:, T[i], :]

        weights_in = sem("weights_in")
        consts_in = sem("consts_in")
        x_in = [sem(f"x_in{q}") for q in range(SLOTS)]
        const_ready = sem("const_ready")
        setup_t = sem("setup_t")
        setup_c = sem("setup_c")
        setup_m = sem("setup_m")
        setup_done = sem("setup_done")
        bad_ready = sem("bad_ready")
        bad_summed = sem("bad_summed")
        flag_ready = sem("flag_ready")
        loaded = [sem(f"loaded{q}") for q in range(SLOTS)]
        xp_in = [sem(f"xp_in{k}") for k in range(2)]
        rows_in = [sem(f"rows_in{k}") for k in range(ROW_SLOTS)]
        x2_in = [sem(f"x2_in{k}") for k in range(QUARTERS)]
        x1_in = [sem(f"x1_in{k}") for k in range(2)]

        S1 = Pass1Signals(sem, "a", loaded, xp_in)
        SG = Pass1Signals(sem, "g", [sem(f"loaded_g{q}") for q in range(SLOTS)], [sem(f"xp_in_g{k}") for k in range(2)])
        gen_enter = sem("gen_enter")
        gen_leave = sem("gen_leave")
        gen_cs_t = sem("gen_cs_t")
        gen_cs_row = sem("gen_cs_row")
        gen_cs_in = sem("gen_cs_in")
        gen_in = sem("gen_in")
        gen_masked = sem("gen_masked")
        gen_stored = sem("gen_stored")
        gen_step = sem("gen_step")
        gen_again = sem("gen_again")

        hi2 = sem("hi2")
        lo2 = sem("lo2")
        used2 = sem("used2")
        y_copied = sem("y_copied")
        yt_done = sem("yt_done")
        z2_ready = sem("z2_ready")
        stats2 = sem("stats2")
        factors2 = sem("factors2")
        normed2 = sem("normed2")
        affine2 = sem("affine2")
        x1_stored = sem("x1_stored")
        self_used = sem("self_used")
        dve_step2 = sem("dve_step2")
        pool_step2 = sem("pool_step2")
        x2_hi = sem("x2_hi")
        x2_lo = sem("x2_lo")
        x1_hi = sem("x1_hi")
        x1_lo = sem("x1_lo")
        turned = sem("turned")
        hi3 = sem("hi3")
        lo3 = sem("lo3")
        used3 = sem("used3")
        a_copied = sem("a_copied")
        mlp_done = sem("mlp_done")
        relu_done = sem("relu_done")
        merged = sem("merged")
        z3_ready = sem("z3_ready")
        stats3 = sem("stats3")
        factors3 = sem("factors3")
        base3 = sem("base3")
        pool_step3 = sem("pool_step3")
        normed3 = sem("normed3")
        stored = sem("stored")
        dve_step3 = sem("dve_step3")

        rows_of = x.rearrange("(k p) d -> p k d", p=P)
        x1_rows = x1_dram.rearrange("(k p) d -> p k d", p=P)
        out_rows = out.rearrange("(k p) d -> p k d", p=P)
        by_rows = adj.rearrange("(q b r) c -> r q b c", b=BLK, r=P)

        def column_panel(src, p, q):
            return src.rearrange("(q b r) c -> r q b c", b=BLK, r=P)[:, q, :, bass.ds(p * PANEL, PANEL)]

        by_squares = adj.rearrange("(g i) (a c) -> a i g c", i=SQ, a=QUADS)
        x1_squares = x1_dram.rearrange("(a t j) d -> a j t d", a=QUADS, j=SQ)
        x2_squares = x2.rearrange("(a t j) d -> a j t d", a=QUADS, j=SQ)

        def quadrant(t, a):
            return t[a * SQ:(a + 1) * SQ]

        def blocks(t, p):
            return t[:, bass.ds(p * BLK, BLK)]

        def blocks3(t, p):
            return t[:, bass.ds(p * BLK, BLK), :]

        def one_block(t, p, b):
            return t[:, bass.ds(p * BLK + b, 1), :].rearrange("p o d -> p (o d)")

        def slot_view(q):
            return ring[:, q, :].rearrange("p (b c) -> p b c", b=BLK)

        def sp_pass1(sp, S, src, load_x):
            def panel(p, par):
                for q in range(SLOTS):
                    if isinstance(p, int) and p == 0:
                        if load_x:
                            sp.dma_start(xs[:, BLK * q:BLK * q + BLK, :], rows_of[:, BLK * q:BLK * q + BLK, :]) \
                                .then_inc(x_in[q], 16)
                    else:
                        sp.wait_ge(S.slot_pe, p * SLOTS + (q + 1 - SLOTS))
                        sp.wait_ge(S.slot_act, p * SLOTS + (q + 1 - SLOTS))
                        sp.wait_ge(S.slot_dve, p * SLOTS + (q + 1 - SLOTS))
                    sp.dma_start(slot_view(q), column_panel(src, p, q)).then_inc(S.loaded[q], 16)
                    if q == 3:
                        sp.dma_start(xp[:, par], blocks3(rows_of, p)).then_inc(S.xp_in[par], 16)
            panel_loop(sp, None, 0, panel)

        def sp_pass2_first(sp, S, src, in_sems):
            for q in range(SLOTS):
                sp.wait_ge(S.slot_pe, (PANELS - 1) * SLOTS + q + 1)
                sp.wait_ge(S.slot_act, (PANELS - 1) * SLOTS + q + 1)
                sp.wait_ge(S.slot_dve, (PANELS - 1) * SLOTS + q + 1)
                sp.dma_start(slot_view(q), column_panel(src, 0, q)).then_inc(in_sems[q], 16)

        def sp_pass2(sp, src):
            def panel(p, par):
                if not (isinstance(p, int) and p == 0):
                    for q in range(SLOTS):
                        sp.wait_ge(hi2, p * (2 * SLOTS) + (2 * q + 2 - 2 * SLOTS))
                        sp.wait_ge(lo2, p * (2 * SLOTS) + (2 * q + 2 - 2 * SLOTS))
                        sp.dma_start(slot_view(q), column_panel(src, p, q)).then_inc(loaded[q], 16)
                if isinstance(p, int) and p < 2:
                    sp.wait_ge(S1.xp_used, PANELS - 1 + p)
                else:
                    sp.wait_ge(S1.xp_used, PANELS)
                sp.dma_start(xp[:, par], blocks3(rows_of, p)).then_inc(xp_in[par], 16)
            panel_loop(sp, None, 0, panel)

        def sp_x2(sp, k):
            sp.wait_ge(self_used, 2 * k + 2)
            for a in range(QUADS):
                sp.dma_start(quadrant(self2[:, QC * k:QC * k + QC, :], a), x2_squares[a, :, QC * k:QC * k + QC, :]) \
                    .then_inc(x2_in[k], 16)

        def sp_x1(sp, k):
            if k == 0:
                sp.wait_ge(hi2, (PANELS - 1) * 2 * SLOTS + 12)
                sp.wait_ge(lo2, (PANELS - 1) * 2 * SLOTS + 12)
            sp.wait_ge(x1_stored, 16 * (PANELS + k))
            for a in range(QUADS):
                dst = quadrant(ring[:, ROW_SLOTS + k, :], a).rearrange("p (t d) -> p t d", d=D)
                sp.dma_start(dst, x1_squares[a, :, 2 * QC * k:2 * QC * (k + 1), :]).then_inc(x1_in[k], 16)

        def sp_pass3(sp):
            def panel(p, par):
                first_panel = isinstance(p, int) and p == 0
                if first_panel:
                    for k in range(QUARTERS - 1):
                        sp_x2(sp, k)
                for q in range(SLOTS):
                    if first_panel and q < ROW_SLOTS:
                        sp.wait_ge(hi2, (PANELS - 1) * 2 * SLOTS + 2 * q + 2)
                        sp.wait_ge(lo2, (PANELS - 1) * 2 * SLOTS + 2 * q + 2)
                    else:
                        sp.wait_ge(turned, p * SLOTS + (q + 1 - ROW_SLOTS))
                    for a in range(QUADS):
                        sp.dma_start(quadrant(ring[:, q % ROW_SLOTS, :], a).rearrange("p (g c) -> p g c", c=P),
                                     by_squares[a, :, bass.ds(p * (PANEL // SQ), PANEL // SQ), q * P:(q + 1) * P]) \
                            .then_inc(rows_in[q % ROW_SLOTS], 16)
                    if first_panel and q == 1:
                        sp_x1(sp, 0)
                    if first_panel and q == 5:
                        sp_x2(sp, QUARTERS - 1)
                    if q == 6:
                        if first_panel:
                            sp.wait_ge(x1_stored, 16 * PANELS)
                        elif isinstance(p, int):
                            sp.wait_ge(base3, p)
                        else:
                            sp.wait_ge(base3, p)
                            sp.wait_ge(x1_stored, 16 * PANELS + 16)
                        sp.dma_start(xp[:, par], blocks3(x1_rows, p)).then_inc(xp_in[par], 16)
                if first_panel:
                    sp_x1(sp, 1)
            panel_loop(sp, None, 0, panel)

        def pe_setup(pe):
            pe.wait_ge(const_ready, 8)
            pe.wait_ge(weights_in, 16 * 7)
            for c in range(2):
                pe.transpose(ps[:, T[0], c * P:(c + 1) * P], st_in1[:, c * P:(c + 1) * P], ident[:, :])
                pe.transpose(ps[:, T[0], (2 + c) * P:(3 + c) * P], st_in2[:, c, :], ident[:, :])
                last = pe.transpose(ps[:, T[3], c * P:(c + 1) * P], st_wm[:, c * P:(c + 1) * P], ident[:, :])
            for l in range(3):
                pe.transpose(ps[:, T[1], l * P:(l + 1) * P], st_w1[:, l, :], ident[:, :])
                last = pe.transpose(ps[:, T[2], l * P:(l + 1) * P], st_w2[:, l, :], ident[:, :])
            last.then_inc(setup_t, 1)

        def pe_setup_products(pe):
            pe.wait_ge(setup_c, 7)
            for c in range(2):
                pe.matmul(ps[:, T[0], 0:H], st_in1T[:, c, :], st_out1[:, c, :], start=(c == 0), stop=(c == 1))
            for c in range(2):
                pe.matmul(ps[:, T[0], H:2 * H], st_b[:, c, :], st_out1[:, c, :], start=(c == 0), stop=(c == 1))
            for c in range(2):
                pe.matmul(ps[:, T[1], c * D:(c + 1) * D], st_in2T[:, c, :], st_out2, start=True, stop=True)
            pe.matmul(ps[:, T[1], 2 * D:3 * D], st_b[:, 2, :], st_out2, start=True, stop=True).then_inc(setup_m, 1)

        def act_setup(act):
            act.wait_ge(setup_t, 1)
            act.activation(st_in1T, ps[:, T[0], 0:2 * P].rearrange("p (c n) -> p c n", c=2), ACT.Copy) \
                .then_inc(setup_c, 1)
            act.activation(st_in2T, ps[:, T[0], 2 * P:4 * P].rearrange("p (c n) -> p c n", c=2), ACT.Copy) \
                .then_inc(setup_c, 1)
            act.activation(w1t[:, :, :], ps[:, T[1], 0:3 * P].rearrange("p (c n) -> p c n", c=3), ACT.Copy) \
                .then_inc(setup_c, 1)
            act.activation(w2t[:, :, :], ps[:, T[2], 0:3 * P].rearrange("p (c n) -> p c n", c=3), ACT.Copy) \
                .then_inc(setup_c, 1)
            act.activation(wmt[:, :, :], ps[:, T[3], 0:2 * P].rearrange("p (c n) -> p c n", c=2), ACT.Copy) \
                .then_inc(setup_c, 1)

        def dve_setup(dve):
            dve.wait_ge(consts_in, 16 * 17)
            for k in range(3):
                last = dve.tensor_scalar(st_b[:, k, :], ones[:, :], bincol[:, k:k + 1], None, ALU.mult)
            dve.drain()
            dve.sem_inc(setup_c, 2)
            dve.tensor_tensor(bs1B[:, :], bs1B[:, :], st_bs, ALU.add)
            dve.tensor_tensor(bo2B[:, :], bo2B[:, :], st_bo, ALU.add)
            dve.tensor_scalar(scl[:, :], scl[:, :], 2.0, None, ALU.add)

        def dve_setup_products(dve):
            dve.wait_ge(setup_m, 1)
            dve.tensor_copy(wA[:, 0, :], ps[:, T[0], 0:H])
            dve.tensor_copy(bw1B[:, :], ps[:, T[0], H:2 * H])
            dve.tensor_copy(wB[:, :, 0:D], ps[:, T[1], 0:2 * D].rearrange("p (c n) -> p c n", c=2))
            dve.tensor_copy(bb2B[:, :], ps[:, T[1], 2 * D:3 * D])
            dve.drain().then_inc(setup_done, 1)

        def pe_stages1(pe, S):
            def stage_sums(r):
                pe.wait_ge(S.folded, r + 1)
                for b in range(BLK):
                    last = pe.matmul(ps[:, SMALL, b:b + 1], accf[:, b * P:(b + 1) * P], ones[:, 0:1],
                                     start=True, stop=True)
                last.then_inc(S.sums_out, 1)

            def stage_own(r, par):
                pe.wait_ge(S.edge_ready, r + 1)
                pe.wait_ge(S.xp_in[par], xp_count(r, par))
                for b in range(BLK):
                    last = pe.matmul(ps[:, par, b * P:(b + 1) * P], xp[:, par, b, :], diag[:, b, :],
                                     start=False, stop=True, skip_group_check=True)
                last.then_inc(S.u_done, 1)
                for b in range(BLK):
                    last = pe.transpose(ps[:, T[0], b * P:(b + 1) * P], xp[:, par, b, :], ident[:, :])
                last.then_inc(S.xp_used, 1)

            def stage_layer1(r):
                pe.wait_ge(S.u_copied, r + 1)
                pe.wait_ge(S.xt_copied, r + 1)
                if isinstance(r, int) and r == PANELS - 1:
                    pe.wait_ge(S.v_done, r)
                else:
                    pe.wait_ge(S.slot_dve, r * SLOTS + (SLOTS + 2))
                for b in range(BLK):
                    pe.matmul(ps[:, T[b], 0:H], uts[:, b * P:(b + 1) * P], wA[:, 0, :], start=True, stop=True)
                    pe.matmul(ps[:, T[b], H:2 * H], xts[:, b * P:(b + 1) * P], wA[:, 1, :],
                              start=True, stop=True).then_inc(S.p12_done, 1)

            def stage_hT(r):
                pe.wait_ge(S.normed, r + 1)
                for c in range(2):
                    for b in range(BLK):
                        last = pe.transpose(ps[:, T[c], b * P:(b + 1) * P], z[:, b, c * P:(c + 1) * P], ident[:, :])
                    last.then_inc(S.ht_done, 1)

            def stage_layer2(r):
                pe.wait_ge(S.ht_copied, r * 2 + 2)
                for b in range(BLK):
                    for c in range(2):
                        last = pe.matmul(ps[:, T[2 + b // 2], (b % 2) * H:(b % 2) * H + H],
                                         hT[:, c, b * P:(b + 1) * P], wB[:, c, :], start=(c == 0), stop=(c == 1))
                last.then_inc(S.w2_done, 1)

            return stage_sums, stage_own, stage_layer1, stage_hT, stage_layer2

        def pe_pass1(pe, S, wait_x):
            stage_sums, stage_own, stage_layer1, stage_hT, stage_layer2 = pe_stages1(pe, S)

            def panel(p, par):
                post = not (isinstance(p, int) and p == 0)
                for q in range(SLOTS):
                    pe.wait_ge(S.loaded[q], (p + 1) * 16)
                    if wait_x and not post:
                        pe.wait_ge(x_in[q], 16)
                    for b in range(BLK):
                        k = BLK * q + b
                        last = pe.matmul(ps[:, par, :], xs[:, k, :], ring[:, q, b * PANEL:(b + 1) * PANEL],
                                         start=(k == 0), stop=False, skip_group_check=True)
                    last.then_inc(S.slot_pe, 1)
                    if wait_x and not post and q == 3:
                        pe_setup(pe)
                    if wait_x and not post and q == 5:
                        pe_setup_products(pe)
                    if post and q == 0:
                        stage_sums(p - 1)
                    if post and q == 2:
                        stage_own(p - 1, 1 - par)
                    if post and q == 3:
                        stage_layer1(p - 1)
                    if post and q == 6:
                        stage_hT(p - 1)
                    if q == 7 and isinstance(p, int) and p == PANELS - 1:
                        stage_sums(p)
                    if post and q == 7:
                        stage_layer2(p - 1)
            panel_loop(pe, None, 0, panel)

        def xp_count(r, par):
            if isinstance(r, int):
                return 16 * (r // 2 + 1)
            return (r - par) * 8 + 16

        def act_stages1(act, S):
            def copies(r, rp):
                act.wait_ge(S.u_done, r + 1)
                act.activation(uts[:, :], ps[:, rp, :], ACT.Copy).then_inc(S.u_copied, 1)
                act.wait_ge(S.xp_used, r + 1)
                act.activation(xts[:, :], T2(0), ACT.Copy).then_inc(S.xt_copied, 1)

            def normalise(r):
                act.wait_ge(S.factors, r + 1)
                for b in range(BLK):
                    last = act.activation(z[:, b, :], z[:, b, :], ACT.Identity, scale=ln[:, 3, b:b + 1],
                                          bias=ln[:, 4, b:b + 1])
                last.then_inc(S.normed, 1)

            def relus(r):
                for c in range(2):
                    act.wait_ge(S.ht_done, r * 2 + (c + 1))
                    act.activation(hT[:, c, :], T2(c), ACT.Relu, scale=g1col[:, c:c + 1],
                                   bias=be1col[:, c:c + 1]).then_inc(S.ht_copied, 1)
            return copies, normalise, relus

        def act_pass1(act, S, detect):
            copies, normalise, relus = act_stages1(act, S)

            def count_slot(p, q):
                act.wait_ge(S.loaded[q], (p + 1) * 16)
                col = p * SLOTS + q
                if detect:
                    if not (isinstance(p, int) and p == 0 and q == 0):
                        act.wait_ge(S.slot_act, p * SLOTS + q)
                    ins = act.activation(junk_a[:, :], ring[:, q, :], ACT.Sign, bias=nbig[:, :],
                                         accum_out=sg[:, bass.ds(col, 1)])
                    if q in ACT_ZERO_SLOTS:
                        ins = act.activation(junk_b[:, :], ring[:, q, :], ACT.Exp, scale=-2.0 ** 100,
                                             accum_out=nz[:, bass.ds(col, 1)])
                    ins.then_inc(S.slot_act, 1)
                else:
                    act.sem_inc(S.slot_act, 1)

            def panel(p, par):
                post = not (isinstance(p, int) and p == 0)
                for q in range(SLOTS):
                    count_slot(p, q)
                    if not post and detect and q == 3:
                        act_setup(act)
                    if post and q == 2:
                        copies(p - 1, 1 - par)
                    if post and q == 5:
                        normalise(p - 1)
                    if post and q == 6:
                        relus(p - 1)
            panel_loop(act, None, 0, panel)

        def layer_norm_factors(pool, steps, out_sem):
            v, t, y, nm = ln[:, 0, :], ln[:, 2, :], ln[:, 3, :], ln[:, 1, :]
            steps.did(pool.tensor_tensor(v, mv[:, :, 1], lnc[:, 0, :], ALU.add))
            steps.did(pool.tensor_tensor(nm, mv[:, :, 0], lnc[:, 3, :], ALU.mult))
            steps.settle()
            steps.did(pool.tensor_tensor(y, v, lnc[:, 1, :], ALU.pow))
            steps.settle()
            steps.did(pool.tensor_tensor(t, y, y, ALU.mult))
            steps.settle()
            steps.did(pool.tensor_tensor(t, t, v, ALU.mult))
            steps.settle()
            steps.did(pool.tensor_tensor(t, t, lnc[:, 1, :], ALU.mult))
            steps.settle()
            steps.did(pool.tensor_tensor(t, t, lnc[:, 2, :], ALU.add))
            steps.settle()
            steps.did(pool.tensor_tensor(y, y, t, ALU.mult))
            steps.settle()
            pool.tensor_tensor(ln[:, 4, :], nm, y, ALU.mult).then_inc(out_sem, 1)

        def pool_post1(pool, S, steps, r, rp):
            pool.wait_ge(S.edge_ready, r + 1)
            steps.did(pool.tensor_tensor(t1[:, :, :], bw1B[:, :].unsqueeze(1).to_broadcast([P, BLK, H]),
                                         st[:, rp, 2, :].unsqueeze(2).to_broadcast([P, BLK, H]), ALU.mult))
            steps.settle()
            pool.tensor_tensor(t1[:, :, :], t1[:, :, :], bs1B[:, :].unsqueeze(1).to_broadcast([P, BLK, H]),
                               ALU.add).then_inc(S.t1_ready, 1)
            pool.wait_ge(S.stats_ready, r + 1)
            layer_norm_factors(pool, steps, S.factors)

        def pool_pass1(pool, S):
            steps = Steps(pool, S.pool_step)

            def panel(p, par):
                if not (isinstance(p, int) and p == 0):
                    pool_post1(pool, S, steps, p - 1, 1 - par)
            panel_loop(pool, steps, PER_POOL1, panel)
            return steps

        def ln_stats(steps, dve, rows, ready):
            for b in range(BLK):
                steps.did(dve.bn_stats(bnst[:, b, :], rows(b)))
            steps.settle()
            ln_aggregate(steps, dve, ready)

        def ln_aggregate(steps, dve, ready):
            dve.memset(spare[:, :], 0.0)
            for b in range(BLK):
                last = dve.bn_aggr(mv[:, b, :], bnst[:, b, :])
            last.then_inc(ready, 1)

        def dve_save_sums(dve, steps, r):
            steps.did(dve.tensor_copy(blocks(cs_all, r), ps[:, SMALL, 0:BLK]))
            steps.settle()

        def dve_stages1(dve, S, steps, own_sums):

            def edge(r, rp):
                cs, e, w = ps[:, SMALL, 0:BLK], ed, st[:, rp]
                dve.wait_ge(S.sums_out, r + 1)
                if own_sums and not (isinstance(r, int) and r == PANELS - 1):
                    dve_save_sums(dve, steps, r)
                steps.did(dve.tensor_scalar(e[:, 0, :], blocks(cs_all, r), EPS, None, ALU.add))
                steps.did(dve.tensor_scalar(e[:, 2, :], cs, 0.0, None, ALU.not_equal))
                steps.settle()
                steps.did(dve.reciprocal(e[:, 1, :], e[:, 0, :]))
                steps.did(dve.tensor_scalar(w[:, 1, :], e[:, 2, :], -1.0, 1.0, ALU.mult, ALU.add))
                steps.settle()
                steps.did(dve.tensor_tensor(e[:, 3, :], cs, e[:, 1, :], ALU.mult))
                for b in range(BLK):
                    steps.did(dve.tensor_scalar(diag[:, b, :], ident[:, :], w[:, 1, b:b + 1], None, ALU.mult))
                steps.settle()
                steps.did(dve.tensor_scalar(e[:, 0, :], e[:, 3, :], EPS, None, ALU.add))
                steps.settle()
                steps.did(dve.reciprocal(e[:, 4, :], e[:, 0, :]))
                steps.settle()
                steps.did(dve.tensor_tensor(e[:, 5, :], e[:, 4, :], e[:, 2, :], ALU.mult))
                steps.settle()
                steps.did(dve.tensor_tensor(e[:, 1, :], e[:, 1, :], e[:, 5, :], ALU.mult))
                steps.did(dve.tensor_tensor(e[:, 3, :], e[:, 3, :], e[:, 5, :], ALU.mult))
                steps.settle()
                steps.did(dve.tensor_tensor(w[:, 0, :], e[:, 1, :], w[:, 1, :], ALU.add))
                steps.did(dve.tensor_tensor(w[:, 2, :], e[:, 3, :], w[:, 1, :], ALU.add))
                steps.settle()
                dve.tensor_copy(blocks(s_all, r), w[:, 0, :]).then_inc(S.edge_ready, 1)

            def layer1(r, rp):
                dve.wait_ge(S.t1_ready, r + 1)
                for b in range(BLK):
                    dve.wait_ge(S.p12_done, r * BLK + (b + 1))
                    steps.did(dve.scalar_tensor_tensor(z[:, b, :], ps[:, T[b], 0:H], st[:, rp, 0, b:b + 1],
                                                       t1[:, b, :], ALU.mult, ALU.add))
                steps.settle()
                for b in range(BLK):
                    ins = dve.tensor_tensor(z[:, b, :], z[:, b, :], ps[:, T[b], H:2 * H], ALU.add)
                    steps.did(ins)
                steps.settle()
                dve.sem_inc(S.z_ready, 1)
                ln_stats(steps, dve, lambda b: z[:, b, :], S.stats_ready)

            def layer2(r, rp):
                dve.wait_ge(S.w2_done, r + 1)
                v, t = z[:, :, 0:D], z[:, :, D:2 * D]
                for g in range(2):
                    res = T2(2 + g).rearrange("p (b n) -> p b n", b=2)
                    steps.did(dve.tensor_tensor(v[:, 2 * g:2 * g + 2, :], res[:, :, 0:D],
                                                bb2B[:, :].unsqueeze(1).to_broadcast([P, 2, D]), ALU.add))
                steps.settle()
                steps.did(dve.tensor_copy(blocks3(vh, r), v))
                for b in range(BLK):
                    steps.did(dve.scalar_tensor_tensor(t[:, b, :], v[:, b, :], st[:, rp, 1, b:b + 1], bo2B[:, :],
                                                       ALU.mult, ALU.add))
                steps.settle()
                steps.did(dve.tensor_tensor(blocks3(vl, r), v, blocks3(vh, r).bitcast(FP32), ALU.subtract))
                for g in range(2):
                    res = T2(2 + g).rearrange("p (b n) -> p b n", b=2)
                    steps.did(dve.tensor_tensor(self2[:, bass.ds(r * BLK + 2 * g, 2), :], t[:, 2 * g:2 * g + 2, :],
                                                res[:, :, D:2 * D], ALU.add))
                steps.settle()
                dve.sem_inc(S.v_done, 1)

            return edge, layer1, layer2

        def dve_pass1(dve, S, detect, per_panel):
            steps = Steps(dve, S.dve_step)
            edge, layer1, layer2 = dve_stages1(dve, S, steps, detect)

            def slot(p, q):
                dve.wait_ge(S.loaded[q], (p + 1) * 16)
                if detect and q in DVE_ZERO_SLOTS:
                    if not (isinstance(p, int) and p == 0 and q <= 1):
                        dve.wait_ge(S.slot_dve, p * SLOTS + (q if q > 1 else 0))
                    dve.tensor_scalar(junk_d[:, :], ring[:, q, :], 0.0, None, ALU.is_equal, ALU.add,
                                      accum_out=nz[:, bass.ds(p * SLOTS + q, 1)])
                if q == 1:
                    if not (isinstance(p, int) and p == 0):
                        dve.wait_ge(S.folded, p)
                    dve.tensor_tensor(acc[:, :], ring[:, 0, :], ring[:, 1, :], ALU.add).then_inc(S.slot_dve, 2)
                elif q > 1:
                    dve.wait_ge(S.slot_dve, p * SLOTS + q)
                    dve.tensor_tensor(acc[:, :], acc[:, :], ring[:, q, :], ALU.add).then_inc(S.slot_dve, 1)

            def fold(p):
                dve.wait_ge(S.slot_dve, p * SLOTS + SLOTS)
                steps.did(dve.tensor_tensor(acc[:, 0:2 * PANEL], acc[:, 0:2 * PANEL], acc[:, 2 * PANEL:], ALU.add))
                steps.settle()
                dve.tensor_tensor(accf[:, :], acc[:, 0:PANEL], acc[:, PANEL:2 * PANEL], ALU.add).then_inc(S.folded, 1)

            def panel(p, par):
                post = not (isinstance(p, int) and p == 0)
                for q in range(SLOTS):
                    slot(p, q)
                    if not post and detect and q == 3:
                        dve_setup(dve)
                    if not post and detect and q == 5:
                        dve_setup_products(dve)
                    if post and q == 1:
                        edge(p - 1, 1 - par)
                    if post and q == 4:
                        layer1(p - 1, 1 - par)
                if post:
                    dve.wait_ge(S.sums_out, p)
                fold(p)
                if post and not (isinstance(p, int) and p == PANELS - 1):
                    layer2(p - 1, 1 - par)
            panel_loop(dve, steps, per_panel, panel)
            return steps, layer2

        def general_gate(eng, gate):
            eng.drain().then_inc(gate, 1)
            eng.wait_ge(gate, 5)

        def sp_general(sp):
            for q in range(SLOTS):
                sp.wait_ge(loaded[q], 16 * (PANELS + 1))
            general_gate(sp, gen_enter)
            sp.wait_ge(gen_cs_row, 1)
            sp.dma_start(cs_dram.rearrange("(k p) -> k p", p=P), crow[:, :]).then_inc(gen_stored, 16)
            sp.wait_ge(gen_stored, 16)
            with sp.Fori(0, PANELS) as p:
                sp.dma_start(t1[:, 0:2, :].rearrange("p b n -> p (b n)"),
                             cs_dram[bass.ds(p * PANEL, PANEL)].partition_broadcast(P)).then_inc(gen_cs_in, 16)
                for q in range(SLOTS):
                    sp.wait_ge(gen_stored, p * (16 * SLOTS) + (16 * q + 16))
                    sp.dma_start(slot_view(0), column_panel(adj, p, q)).then_inc(gen_in, 16)
                    sp.wait_ge(gen_masked, p * SLOTS + (q + 1))
                    sp.dma_start(column_panel(masked_dram, p, q), slot_view(0)).then_inc(gen_stored, 16)
            sp.wait_ge(gen_stored, 16 * PANELS * SLOTS + 16)
            sp_pass1(sp, SG, masked_dram, False)
            sp_pass2_first(sp, SG, masked_dram, [gen_again] * SLOTS)
            sp.wait_ge(gen_again, 16 * SLOTS)
            general_gate(sp, gen_leave)

        def dve_general(dve):
            general_gate(dve, gen_enter)
            steps = Steps(dve, gen_step)
            per = 2 + SLOTS * BLK * 2
            rB, tmp = z[:, 0:2, :].rearrange("p b n -> p (b n)"), z[:, 2:4, :].rearrange("p b n -> p (b n)")
            with dve.Fori(0, PANELS) as p:
                steps.enter(p * per)
                dve.wait_ge(gen_cs_in, p * 16 + 16)
                steps.did(dve.tensor_scalar(rB, t1[:, 0:2, :].rearrange("p b n -> p (b n)"), EPS, None, ALU.add))
                steps.settle()
                steps.did(dve.reciprocal(rB, rB))
                steps.settle()
                for q in range(SLOTS):
                    dve.wait_ge(gen_in, p * (16 * SLOTS) + 16 * (q + 1))
                    for b in range(BLK):
                        m = ring[:, 0, b * PANEL:(b + 1) * PANEL]
                        steps.did(dve.tensor_tensor(tmp, m, rB, ALU.mult))
                        steps.settle()
                        steps.did(dve.scalar_tensor_tensor(m, tmp, THRESH, m, ALU.is_gt, ALU.mult))
                        steps.settle()
                    dve.sem_inc(gen_masked, 1)
                assert steps.n == per
            _, layer2 = dve_pass1(dve, SG, False, PER_DVE1G)
            layer2(PANELS - 2, 0)
            general_gate(dve, gen_leave)

        def pe_general(pe):
            general_gate(pe, gen_enter)
            pe.transpose(ps[0:CHUNKS, T[0], 0:P], cs_all[:, :], ident[:, :]).then_inc(gen_cs_t, 1)
            pe_pass1(pe, SG, False)
            general_gate(pe, gen_leave)

        def act_general(act):
            general_gate(act, gen_enter)
            act.wait_ge(gen_cs_t, 1)
            act.activation(crow[:, :], ps[0:CHUNKS, T[0], 0:P], ACT.Copy).then_inc(gen_cs_row, 1)
            act_pass1(act, SG, False)
            general_gate(act, gen_leave)

        def pool_general(pool):
            general_gate(pool, gen_enter)
            pool_pass1(pool, SG)
            general_gate(pool, gen_leave)

        def general(eng, path):
            eng.wait_ge(flag_ready, 1)
            flag = eng.value_load(flag_i[0:1, 0:1], min_val=0, max_val=1)
            with eng.If(flag > 0):
                path(eng)

        PER_DVE1, PER_DVE1G, PER_DVE2, PER_DVE3 = 40, 39, 14, 5
        PER_POOL1, PER_POOL2, PER_POOL3 = 9, 17, 8

        HALF = SLOTW // 2

        def half_of(t, h):
            k = h % 4
            return t[:, 2 * k:2 * k + 2, :].rearrange("p a n -> p (a n)")

        def split_waits(eng, p, h):
            if isinstance(p, int) and p == 0:
                if h >= 4:
                    eng.wait_ge(used2, h - 3)
            else:
                eng.wait_ge(used2, p * (2 * SLOTS) + (h - 3))

        def act_post2(act):
            def copy_y(r, rp):
                act.wait_ge(used2, r * (2 * SLOTS) + 2 * SLOTS)
                act.activation(uts[:, :], ps[:, rp, :], ACT.Copy).then_inc(y_copied, 1)

            def norm(r, which):
                act.wait_ge(factors2, r * 2 + (which + 1))
                if which == 0:
                    act.wait_ge(x1_stored, r * 16 + 16)
                for b in range(BLK):
                    last = act.activation(z[:, b, D:2 * D], z[:, b, 0:D], ACT.Identity, scale=ln[:, 3, b:b + 1],
                                          bias=ln[:, 4, b:b + 1])
                last.then_inc(normed2, 1)
                if which == 1:
                    act.wait_ge(normed2, r * 2 + 2)
                    act.dma_start(blocks3(x1_rows, r), z[:, :, D:2 * D]).then_inc(x1_stored, 16)
            return copy_y, norm

        def act_pass2(act):
            copies1, normalise1, relus1 = act_stages1(act, S1)
            copy_y, norm = act_post2(act)
            act.sem_inc(x1_stored, 16)
            act.wait_ge(S1.slot_pe, PANELS * SLOTS)
            act.wait_ge(S1.sums_out, PANELS)

            def half(p, h):
                if h % 2 == 0:
                    act.wait_ge(loaded[h // 2], (p + (PANELS + 1)) * 16)
                split_waits(act, p, h)
                act.activation(half_of(mh, h), ring[:, h // 2, (h % 2) * HALF:(h % 2 + 1) * HALF],
                               ACT.Copy).then_inc(hi2, 1)

            def panel(p, par):
                post = not (isinstance(p, int) and p == 0)
                for h in range(2 * SLOTS):
                    half(p, h)
                    if not post and h == 2:
                        copies1(PANELS - 1, 1)
                    if not post and h == 9:
                        normalise1(PANELS - 1)
                    if not post and h == 11:
                        relus1(PANELS - 1)
                    if post and h == 3:
                        copy_y(p - 1, 1 - par)
                    if post and h == 8:
                        norm(p - 1, 0)
                    if post and h == 15:
                        norm(p - 1, 1)
            panel_loop(act, None, 0, panel)

        def pool_post2(pool, steps, r):
            pool.wait_ge(stats2, r * 2 + 1)
            layer_norm_factors(pool, steps, factors2)
            pool.wait_ge(normed2, r * 2 + 1)
            steps.did(pool.tensor_tensor(z[:, :, D:2 * D], z[:, :, D:2 * D],
                                         g2B[:, :].unsqueeze(1).to_broadcast([P, BLK, D]), ALU.mult))
            steps.settle()
            pool.tensor_tensor(z[:, :, D:2 * D], z[:, :, D:2 * D],
                               be2B[:, :].unsqueeze(1).to_broadcast([P, BLK, D]), ALU.add).then_inc(affine2, 1)
            pool.wait_ge(stats2, r * 2 + 2)
            layer_norm_factors(pool, steps, factors2)

        def pool_pass2(pool):
            steps = Steps(pool, pool_step2)

            def panel(p, par):
                if not (isinstance(p, int) and p == 0):
                    pool_post2(pool, steps, p - 1)
            panel_loop(pool, steps, PER_POOL2, panel)
            pool_x2(pool, 0)
            pool_x2(pool, 1)
            pool_post2(pool, steps, PANELS - 1)
            pool_x2(pool, 2)
            pool_x2(pool, 3)

        def pool_x2(pool, k):
            part = slice(QC * k, QC * k + QC)
            pool.wait_ge(x2_hi, k + 1)
            pool.tensor_tensor(vl[:, part, :], self2[:, part, :], vh[:, part, :].bitcast(FP32), ALU.subtract) \
                .then_inc(x2_lo, 1)

        def pool_pass3(pool):
            steps = Steps(pool, pool_step3)
            pool.sem_inc(base3, 1)

            def post(r, rp):
                pool.wait_ge(xp_in[rp], xp_count3(r, rp))
                pool.wait_ge(relu_done, r * 6 + 2)
                pool.tensor_tensor(z[:, :, 0:D], xp[:, rp], bmB[:, :].unsqueeze(1).to_broadcast([P, BLK, D]),
                                   ALU.add).then_inc(base3, 1)
                pool.wait_ge(stats3, r + 1)
                layer_norm_factors(pool, steps, factors3)

            def panel(p, par):
                if not (isinstance(p, int) and p == 0):
                    post(p - 1, 1 - par)
            panel_loop(pool, steps, PER_POOL3, panel)
            post(PANELS - 1, 1)

        def xp_count3(r, par):
            if isinstance(r, int):
                return 16 * (PANELS + r // 2 + 1)
            return (r - par) * 8 + (16 + 16 * PANELS)

        def dve_post2(dve, steps):
            def layer(r):
                steps.did(dve.tensor_copy(s4[:, :], blocks(s_all, r)))
                steps.settle()
                dve.wait_ge(yt_done, r + 1)
                for b in range(BLK):
                    steps.did(dve.scalar_tensor_tensor(z[:, b, 0:D], ps[:, YT, b * P:(b + 1) * P], s4[:, b:b + 1],
                                                       one_block(self2, r, b), ALU.mult, ALU.add))
                steps.settle()
                dve.sem_inc(self_used, 1)
                dve.sem_inc(z2_ready, 1)
                ln_stats(steps, dve, lambda b: z[:, b, 0:D], stats2)

            def residual(r, rp):
                dve.wait_ge(affine2, r + 1)
                dve.wait_ge(xp_in[rp], xp2_count(r, rp))
                steps.did(dve.scalar_tensor_tensor(z[:, :, 0:D], z[:, :, D:2 * D], 0.0, xp[:, rp], ALU.max, ALU.add))
                steps.settle()
                ln_stats(steps, dve, lambda b: z[:, b, 0:D], stats2)

            return layer, residual

        def dve_pass2(dve, steps1):
            steps = Steps(dve, dve_step2)
            edge1, layer1, layer2 = dve_stages1(dve, S1, steps1, True)
            layer, residual = dve_post2(dve, steps)

            def half(p, h):
                if h % 2 == 0:
                    dve.wait_ge(loaded[h // 2], (p + (PANELS + 1)) * 16)
                split_waits(dve, p, h)
                dve.wait_ge(hi2, p * (2 * SLOTS) + (h + 1))
                dve.tensor_tensor(half_of(ml, h), ring[:, h // 2, (h % 2) * HALF:(h % 2 + 1) * HALF],
                                  half_of(mh, h).bitcast(FP32), ALU.subtract).then_inc(lo2, 1)

            def panel(p, par):
                post = not (isinstance(p, int) and p == 0)
                if not post:
                    edge1(PANELS - 1, 1)
                for h in range(2 * SLOTS):
                    half(p, h)
                    if not post and h == 7:
                        layer1(PANELS - 1, 1)
                    if not post and h == 13:
                        layer2(PANELS - 1, 1)
                    if post and h == 4:
                        layer(p - 1)
                    if post and h == 11:
                        residual(p - 1, 1 - par)
            panel_loop(dve, steps, PER_DVE2, panel)
            return steps

        def xp2_count(r, par):
            if isinstance(r, int):
                return 16 * (PANELS // 2 + r // 2 + 1)
            return (r - par) * 8 + (16 + 8 * PANELS)

        def pe_turn_y(pe, r):
            pe.wait_ge(y_copied, r + 1)
            for b in range(BLK):
                last = pe.transpose(ps[:, YT, b * P:(b + 1) * P], uts[:, b * P:(b + 1) * P], ident[:, :])
            last.then_inc(yt_done, 1)

        def pe_pass2(pe):
            _, stage_own, stage_layer1, stage_hT, stage_layer2 = pe_stages1(pe, S1)

            def panel(p, par):
                post = not (isinstance(p, int) and p == 0)
                for h in range(2 * SLOTS):
                    pe.wait_ge(hi2, p * (2 * SLOTS) + (h + 1))
                    if not post and h == 0:
                        pe.wait_ge(S1.v_done, PANELS - 2)
                    if not post and h >= 2 * SLOTS - 4 and h % 2 == 0:
                        pe.wait_ge(S1.v_done, PANELS - 1 + (h - (2 * SLOTS - 4)) // 2)
                    for a in range(2):
                        k = 2 * h + a
                        m = mh[:, 2 * (h % 4) + a, :]
                        pe.matmul(ps[:, par, :], vh[:, k, :], m, start=(k == 0), stop=False)
                        pe.matmul(ps[:, par, :], vl[:, k, :], m, start=False, stop=False)
                    pe.wait_ge(lo2, p * (2 * SLOTS) + (h + 1))
                    for a in range(2):
                        k = 2 * h + a
                        last = pe.matmul(ps[:, par, :], vh[:, k, :], ml[:, 2 * (h % 4) + a, :], start=False,
                                         stop=(k == CHUNKS - 1))
                    last.then_inc(used2, 1)
                    if not post and h == 0:
                        stage_own(PANELS - 1, 1)
                    if not post and h == 3:
                        stage_layer1(PANELS - 1)
                    if not post and h == 9:
                        stage_hT(PANELS - 1)
                    if not post and h == 11:
                        stage_layer2(PANELS - 1)
                    if post and h == 1:
                        pe_turn_y(pe, p - 1)
            panel_loop(pe, None, 0, panel)

        M3 = (5, 6)
        A3 = ((0, 2), (1, 3))

        def pieces(t, q):
            return t[:, BLK * (q % 2):BLK * (q % 2) + BLK, :].rearrange("p a n -> p (a n)")

        def turned_slot(q):
            return ring[:, SLOTS - 2 + q % 2, :]

        def pe_pass3(pe):
            def products(p, par, q):
                a1, a2 = A3[par]
                pe.wait_ge(hi3, p * SLOTS + (q + 1))
                if isinstance(p, int) and p == 0 and q % 2 == 0:
                    pe.wait_ge(x2_lo, q // 2 + 1)
                    pe.wait_ge(x1_lo, q // 2 + 1)
                for t in range(BLK):
                    k, h = BLK * q + t, mh[:, BLK * (q % 2) + t, :]
                    for bank, sh, sl in ((a1, x1h, x1l), (a2, vh, vl)):
                        pe.matmul(ps[:, bank, :], sh[:, k, :], h, start=(k == 0), stop=False)
                        pe.matmul(ps[:, bank, :], sl[:, k, :], h, start=False, stop=False)
                pe.wait_ge(lo3, p * SLOTS + (q + 1))
                for t in range(BLK):
                    k, l = BLK * q + t, ml[:, BLK * (q % 2) + t, :]
                    for bank, sh in ((a1, x1h), (a2, vh)):
                        last = pe.matmul(ps[:, bank, :], sh[:, k, :], l, start=False, stop=(k == CHUNKS - 1))
                last.then_inc(used3, 1)

            def mlp(r, layer):
                if layer == 0:
                    pe.wait_ge(a_copied, r * 2 + 2)
                else:
                    pe.wait_ge(relu_done, r * 6 + 2 * layer)
                for g, (w, src) in enumerate(((w1t, uts), (w2t, xts))):
                    last = pe.matmul(ps[:, M3[g], :], w[:, layer, :], src[:, :], start=True, stop=True)
                    last.then_inc(mlp_done, 1)

            def merge(r):
                pe.wait_ge(relu_done, r * 6 + 6)
                for b in range(BLK):
                    pe.matmul(ps[:, M3[0], b * P:(b + 1) * P], uts[:, b * P:(b + 1) * P], wmt[:, 0, :],
                              start=True, stop=False, skip_group_check=True)
                    last = pe.matmul(ps[:, M3[0], b * P:(b + 1) * P], xts[:, b * P:(b + 1) * P], wmt[:, 1, :],
                                     start=False, stop=True, skip_group_check=True)
                last.then_inc(merged, 1)

            def panel(p, par):
                post = not (isinstance(p, int) and p == 0)
                if not post:
                    pe_turn_y(pe, PANELS - 1)
                for q in range(SLOTS):
                    products(p, par, q)
                    if post and q < 3:
                        mlp(p - 1, q)
                    if post and q == 3:
                        merge(p - 1)
            panel_loop(pe, None, 0, panel)
            r = PANELS - 1
            for layer in range(3):
                mlp(r, layer)
            merge(r)

        def act_x2(act, k):
            part = slice(QC * k, QC * k + QC)
            act.wait_ge(used2, (PANELS - 1) * 2 * SLOTS + (QC // 2) * (k + 1))
            act.wait_ge(x2_in[k], 16 * QUADS)
            act.activation(vh[:, part, :], self2[:, part, :], ACT.Copy).then_inc(x2_hi, 1)

        def x1_piece(k):
            return ring[:, ROW_SLOTS + k // 2, (k % 2) * QC * D:(k % 2 + 1) * QC * D].rearrange("p (t d) -> p t d", d=D)

        def act_x1(act, k):
            act.wait_ge(x1_in[k // 2], 16 * QUADS)
            act.activation(x1h[:, QC * k:QC * k + QC, :], x1_piece(k), ACT.Copy).then_inc(x1_hi, 1)

        def dve_x1(dve, k):
            part = slice(QC * k, QC * k + QC)
            dve.wait_ge(x1_hi, k + 1)
            dve.tensor_tensor(x1l[:, part, :], x1_piece(k), x1h[:, part, :].bitcast(FP32), ALU.subtract) \
                .then_inc(x1_lo, 1)

        def buffer_free(eng, p, q):
            if isinstance(p, int) and p == 0 and q < 2:
                eng.wait_ge(used2, PANELS * 2 * SLOTS)
            else:
                eng.wait_ge(used3, p * SLOTS + (q - 1))

        def act_pass3(act):
            act.sem_inc(stored, 16)
            copy_y, norm2 = act_post2(act)

            def high_parts(p, q):
                act.wait_ge(turned, p * SLOTS + (q + 1))
                buffer_free(act, p, q)
                act.activation(pieces(mh, q), turned_slot(q), ACT.Copy).then_inc(hi3, 1)

            def copies(r, rp):
                act.wait_ge(used3, r * SLOTS + SLOTS)
                for g, dst in enumerate((uts, xts)):
                    act.activation(dst[:, :], ps[:, A3[rp][g], :], ACT.Copy, scale=scl[:, g:g + 1]) \
                        .then_inc(a_copied, 1)

            def relus(r, layer):
                for g, dst in enumerate((uts, xts)):
                    act.wait_ge(mlp_done, r * 6 + (2 * layer + 2))
                    act.activation(dst[:, :], ps[:, M3[g], :], ACT.Relu, bias=bcol[:, g, layer:layer + 1]) \
                        .then_inc(relu_done, 1)

            def norm(r, rp):
                act.wait_ge(factors3, r + 1)
                act.wait_ge(stored, r * 16 + 16)
                for b in range(BLK):
                    last = act.activation(z[:, b, D:2 * D], z[:, b, 0:D], ACT.Identity, scale=ln[:, 3, b:b + 1],
                                          bias=ln[:, 4, b:b + 1])
                last.then_inc(normed3, 1)
                act.wait_ge(normed3, r + 1)
                act.dma_start(blocks3(out_rows, r), z[:, :, D:2 * D]).then_inc(stored, 16)

            def panel(p, par):
                post = not (isinstance(p, int) and p == 0)
                if not post:
                    act_x2(act, 0)
                    act_x2(act, 1)
                    copy_y(PANELS - 1, 1)
                for q in range(SLOTS):
                    high_parts(p, q)
                    if not post and q == 0:
                        act_x1(act, 0)
                    if not post and q == 1:
                        act_x2(act, 2)
                        norm2(PANELS - 1, 0)
                        act_x1(act, 1)
                    if not post and q == 3:
                        norm2(PANELS - 1, 1)
                        act.wait_ge(x1_stored, 16 * PANELS + 16)
                        act_x2(act, 3)
                    if not post and q in (4, 5):
                        act_x1(act, q - 2)
                    if post and q == 0:
                        copies(p - 1, 1 - par)
                    if post and q in (2, 3, 4):
                        relus(p - 1, q - 2)
                    if post and q == 7:
                        norm(p - 1, 1 - par)
            panel_loop(act, None, 0, panel)
            r = PANELS - 1
            copies(r, 1)
            for layer in range(3):
                relus(r, layer)
            norm(r, 1)
            act.wait_ge(stored, 16 * PANELS + 16)

        def dve_pass3(dve, steps2):
            steps = Steps(dve, dve_step3)
            layer, residual2 = dve_post2(dve, steps2)

            def turn(p, q):
                if isinstance(p, int):
                    dve.wait_ge(rows_in[q % ROW_SLOTS], 16 * QUADS * (2 * p + q // ROW_SLOTS + 1))
                else:
                    dve.wait_ge(rows_in[q % ROW_SLOTS], p * (32 * QUADS) + 16 * QUADS * (q // ROW_SLOTS + 1))
                if isinstance(p, int) and p == 0 and q < 2:
                    dve.wait_ge(hi2, (PANELS - 1) * 2 * SLOTS + 2 * (SLOTS - 2 + q) + 2)
                    dve.wait_ge(lo2, (PANELS - 1) * 2 * SLOTS + 2 * (SLOTS - 2 + q) + 2)
                else:
                    dve.wait_ge(hi3, p * SLOTS + (q - 1))
                    dve.wait_ge(lo3, p * SLOTS + (q - 1))
                dve.transpose(turned_slot(q).rearrange("p (t g c) -> p g t c", t=BLK, c=SQ),
                              ring[:, q % ROW_SLOTS, :].rearrange("p (g t c) -> p g t c", t=BLK, c=SQ)) \
                    .then_inc(turned, 1)

            def low_parts(p, q):
                buffer_free(dve, p, q)
                dve.wait_ge(hi3, p * SLOTS + (q + 1))
                dve.tensor_tensor(pieces(ml, q), turned_slot(q), pieces(mh, q).bitcast(FP32),
                                  ALU.subtract).then_inc(lo3, 1)

            def add(r):
                zz = z[:, :, 0:D]
                dve.wait_ge(base3, r + 2)
                dve.wait_ge(merged, r + 1)
                steps.did(dve.tensor_tensor(zz, zz, ps[:, M3[0], :].rearrange("p (b d) -> p b d", b=BLK), ALU.add))
                steps.settle()
                ln_stats(steps, dve, lambda b: z[:, b, 0:D], stats3)

            def panel(p, par):
                post = not (isinstance(p, int) and p == 0)
                if not post:
                    turn(0, 0)
                for q in range(SLOTS):
                    if q + 1 < SLOTS:
                        turn(p, q + 1)
                    elif not (isinstance(p, int) and p == PANELS - 1):
                        turn(p + 1, 0)
                    if not post and q == 0:
                        layer(PANELS - 1)
                    low_parts(p, q)
                    if not post and q in (0, 1, 4, 5):
                        dve_x1(dve, (0, 1, None, None, 2, 3)[q])
                    if not post and q == 2:
                        residual2(PANELS - 1, 1)
                    if post and q == 5:
                        add(p - 1)
            panel_loop(dve, steps, PER_DVE3, panel)
            add(PANELS - 1)

        block = ctx.enter_context(nc.Block())

        @block.sync
        def _(sp):
            sp_pass1(sp, S1, adj, True)
            sp_pass2_first(sp, S1, adj, loaded)
            sp.wait_ge(flag_ready, 1)
            flag = sp.value_load(flag_i[0:1, 0:1], min_val=0, max_val=1)
            with sp.If(flag > 0):
                sp_general(sp)
                sp_pass2(sp, masked_dram)
            with sp.Else():
                sp_pass2(sp, adj)
            sp_pass3(sp)

        @block.gpsimd
        def _(pool):
            pool.memset(ident[:, :], 0.0).then_inc(const_ready, 1)
            pool.memset(ones[:, :], 1.0).then_inc(const_ready, 1)
            pool.memset(nbig[:, :], -BIG).then_inc(const_ready, 1)
            pool.wait_ge(const_ready, 3)
            pool.affine_select(out=ident[:, :], in_=ident[:, :], compare_op=ALU.not_equal, fill=1.0, base=0,
                               pattern=[[-1, P]], channel_multiplier=1).then_inc(const_ready, 1)
            for n, c in enumerate((LN_EPS, -0.5, 1.5, -1.0)):
                pool.memset(lnc[:, n, :], c).then_inc(const_ready, 1)
            steps1 = pool_pass1(pool, S1)
            general(pool, pool_general)
            pool_post1(pool, S1, steps1, PANELS - 1, 1)
            pool_pass2(pool)
            pool_pass3(pool)

        @block.scalar
        def _(act):
            act.dma_start(st_in1, W_in1).then_inc(weights_in, 16)
            act.dma_start(st_out1, W_out1.rearrange("(c k) n -> k c n", c=2)).then_inc(weights_in, 16)
            act.dma_start(st_in2, W_in2.rearrange("(c k) n -> k c n", c=2)).then_inc(weights_in, 16)
            act.dma_start(st_out2, W_out2).then_inc(weights_in, 16)
            act.dma_start(st_w1, W1.rearrange("l o i -> o l i")).then_inc(weights_in, 16)
            act.dma_start(st_w2, W2.rearrange("l o i -> o l i")).then_inc(weights_in, 16)
            act.dma_start(st_wm, Wm).then_inc(weights_in, 16)
            for dst, src in ((wA[:, 1, :], W_self1), (wB[:, :, D:2 * D], W_self2.rearrange("(c k) n -> k c n", c=2)),
                             (bs1B[:, :], b_out1.partition_broadcast(P)), (st_bs, b_self1.partition_broadcast(P)),
                             (bo2B[:, :], b_out2.partition_broadcast(P)), (st_bo, b_self2.partition_broadcast(P)),
                             (g2B[:, :], g2.partition_broadcast(P)), (be2B[:, :], be2.partition_broadcast(P)),
                             (bmB[:, :], bm.partition_broadcast(P)),
                             (scl[:, 0:1], eps1.partition_broadcast(P)), (scl[:, 1:2], eps2.partition_broadcast(P))):
                act.dma_start(dst, src).then_inc(consts_in, 16)
            with nc.allow_non_contiguous_dma("columns of the small bias vectors"):
                for dst, src in ((bincol[:, 0:2], b_in1.rearrange("(c k) -> k c", c=2)),
                                 (bincol[:, 2:3], b_in2.rearrange("(c k) -> k c", c=1)),
                                 (g1col[:, :], g1.rearrange("(c k) -> k c", c=2)),
                                 (be1col[:, :], be1.rearrange("(c k) -> k c", c=2)),
                                 (bcol[:, 0, :], b1.rearrange("l d -> d l")),
                                 (bcol[:, 1, :], b2.rearrange("l d -> d l"))):
                    act.dma_start(dst, src).then_inc(consts_in, 16)
            act.wait_ge(const_ready, 3)
            act_pass1(act, S1, True)
            general(act, act_general)
            act_pass2(act)
            act_pass3(act)

        @block.tensor
        def _(pe):
            pe_pass1(pe, S1, True)
            pe.wait_ge(bad_ready, 1)
            pe.matmul(ps[:, SMALL, 8:9], ones[:, :], fl[:, 3:4], start=True, stop=True).then_inc(bad_summed, 1)
            general(pe, pe_general)
            pe_pass2(pe)
            pe_pass3(pe)

        @block.vector
        def _(dve):
            dve.wait_ge(const_ready, 8)
            steps1, layer2 = dve_pass1(dve, S1, True, PER_DVE1)
            dve.wait_ge(S1.sums_out, PANELS)
            dve_save_sums(dve, steps1, PANELS - 1)
            dve.wait_ge(S1.slot_act, PANELS * SLOTS)
            dve.scalar_tensor_tensor(sg[:, :], nz[:, :], 2.0, sg[:, :], ALU.mult, ALU.add, accum_out=fl[:, 0:1])
            dve.reduce_max(fl[:, 1:2], cs_all[:, :], AX.X)
            dve.drain()
            dve.tensor_scalar(fl[:, 0:1], fl[:, 0:1], float(PANELS * SLOTS * SLOTW), None, ALU.not_equal)
            dve.tensor_scalar(fl[:, 1:2], fl[:, 1:2], CS_LIMIT, None, ALU.is_gt)
            dve.drain()
            dve.tensor_tensor(fl[:, 3:4], fl[:, 0:1], fl[:, 1:2], ALU.max).then_inc(bad_ready, 1)
            dve.wait_ge(bad_summed, 1)
            dve.tensor_scalar(flag_i[:, :], ps[:, SMALL, 8:9], 1.0, None, ALU.min).then_inc(flag_ready, 1)
            layer2(PANELS - 2, 0)
            general(dve, dve_general)
            steps2 = dve_pass2(dve, steps1)
            dve_pass3(dve, steps2)


_INS = ['x', 'adj'] + ['L0_gnn_' + n for n in ('W_in1', 'b_in1', 'W_out1', 'b_out1', 'W_self1', 'b_self1', 'g1', 'be1',
                                               'W_in2', 'b_in2', 'W_out2', 'b_out2', 'W_self2', 'b_self2', 'g2', 'be2')] \
    + ['L1_gnn_' + n for n in ('x2', 'eps1', 'eps2', 'W1', 'b1', 'W2', 'b2', 'Wm', 'bm')]
_OUTS = [((N, D), 'float32')]


def kernel(**inputs):
    import numpy as _np
    import concourse.bacc as _bacc
    from concourse import mybir as _mybir
    from concourse.bass_utils import run_bass_kernel_spmd as _run

    nc = _bacc.Bacc("TRN2", target_bir_lowering=False, num_devices=1)
    arrays, args = {}, []
    for name in _INS:
        a = _np.ascontiguousarray(inputs[name])
        arrays[f"in_{name}_dram"] = a
        args.append(nc.dram_tensor(f"in_{name}_dram", a.shape, _mybir.dt.from_np(a.dtype), kind="ExternalInput").ap())
    for i, (shape, dtype) in enumerate(_OUTS):
        dt = _mybir.dt.from_np(_np.dtype(dtype))
        args.append(nc.dram_tensor(f"out_{i}_dram", shape, dt, kind="ExternalOutput").ap())
    gnn_program(nc, *args)
    r = _run(nc, [arrays], core_ids=[0])
    got = tuple(r.results[0][f"out_{i}_dram"] for i in range(len(_OUTS)))
    return got[0]
```

```python
from contextlib import ExitStack

import concourse.bass as bass
from concourse import mybir

FP32 = mybir.dt.float32
F32R = mybir.dt.float32r
I32 = mybir.dt.int32
I8 = mybir.dt.int8
U8 = mybir.dt.uint8
ALU = mybir.AluOpType
ACT = mybir.ActivationFunctionType
AX = mybir.AxisListType

N = 4096
D = 128
H = 256
P = 128
PANEL = 512
PANELS = N // PANEL
SLOTS = 8
BLK = PANEL // P
CHUNKS = N // P
SLOTW = BLK * PANEL
SQ = 32
QUADS = P // SQ
POOL_HALVES = (1, 7)
DVE_HALVES = tuple(h for h in range(2 * SLOTS) if h not in POOL_HALVES)
ROW_SLOTS = 4
QUARTERS = 4
QC = CHUNKS // QUARTERS
X_ORDER = (2, 3, 1, 0)
PIECES = (4, 5, 6, 7, 2, 3, 0, 1)
THRESH = 1e-06
EPS = 1e-08
LN_EPS = 1e-05
BIG = 2.0 ** -7
CS_LIMIT = 0.99 * BIG / THRESH
RSQRT_SEED = float(0x5F3759DF)
ACT_ZERO_SLOTS = (0, 1, 2, 4, 5, 7)
DVE_ZERO_SLOTS = tuple(q for q in range(SLOTS) if q not in ACT_ZERO_SLOTS)


class Steps:

    def __init__(self, eng, sem):
        self.eng, self.sem, self.base, self.n = eng, sem, 0, 0

    def did(self, ins):
        ins.then_inc(self.sem, 1)
        self.n += 1

    def settle(self):
        self.eng.wait_ge(self.sem, self.base + self.n)

    def enter(self, base):
        self.base, self.n = base, 0


class Pass1Signals:

    def __init__(self, sem, tag, loaded, xp_in):
        self.loaded, self.xp_in = loaded, xp_in
        self.slot_pe = sem("slot_pe_" + tag)
        self.slot_act = sem("slot_act_" + tag)
        self.slot_dve = sem("slot_dve_" + tag)
        self.folded = sem("folded_" + tag)
        self.sums_out = sem("sums_out_" + tag)
        self.edge_ready = sem("edge_ready_" + tag)
        self.u_done = sem("u_done_" + tag)
        self.xp_used = sem("xp_used_" + tag)
        self.u_copied = sem("u_copied_" + tag)
        self.xt_copied = sem("xt_copied_" + tag)
        self.p12_done = sem("p12_done_" + tag)
        self.t1_ready = sem("t1_ready_" + tag)
        self.factors = sem("factors_" + tag)
        self.stats_ready = sem("stats_ready_" + tag)
        self.normed = sem("normed_" + tag)
        self.ht_done = sem("ht_done_" + tag)
        self.ht_copied = sem("ht_copied_" + tag)
        self.w2_done = sem("w2_done_" + tag)
        self.v_done = sem("v_done_" + tag)
        self.dve_step = sem("dve_step_" + tag)
        self.pool_step = sem("pool_step_" + tag)


def panel_loop(eng, steps, per_panel, body):
    body(0, 0)
    before = steps.n if steps else 0
    assert not steps or steps.base == 0
    with eng.Fori(0, (PANELS - 2) // 2) as pair:
        for k in range(2):
            p = pair * 2 + (1 + k)
            if steps:
                steps.enter(pair * (2 * per_panel) + (before + k * per_panel))
            body(p, (1 + k) % 2)
            assert not steps or steps.n == per_panel, (steps.n, per_panel)
    if steps:
        steps.enter(before + (PANELS - 2) * per_panel)
    body(PANELS - 1, (PANELS - 1) % 2)


def panel_loop2(eng, steps, per_panel, body):
    body(0, 0)
    body(1, 1)
    before = steps.n if steps else 0
    assert not steps or steps.base == 0
    with eng.Fori(0, (PANELS - 2) // 2) as pair:
        for k in range(2):
            if steps:
                steps.enter(pair * (2 * per_panel) + (before + k * per_panel))
            body(pair * 2 + (2 + k), k)
            assert not steps or steps.n == per_panel, (steps.n, per_panel)
    if steps:
        steps.enter(before + (PANELS - 2) * per_panel)


def gnn_program(nc, x, adj, W_in1, b_in1, W_out1, b_out1, W_self1, b_self1, g1, be1,
                W_in2, b_in2, W_out2, b_out2, W_self2, b_self2, g2, be2,
                x2, eps1, eps2, W1, b1, W2, b2, Wm, bm, out):
    ctx = ExitStack()
    with ctx:
        def sb(name, shape, dt=FP32, where=ctx):
            return where.enter_context(nc.sbuf_tensor(name, shape, dt))

        def sem(name):
            return ctx.enter_context(nc.semaphore(name))

        masked_dram = nc.dram_tensor("masked_adj", [N, N], FP32, kind="Internal").ap()
        cs_dram = nc.dram_tensor("column_sums", [N], FP32, kind="Internal").ap()
        x1_dram = nc.dram_tensor("x1_rows", [N, D], FP32, kind="Internal").ap()

        ring = sb("ring", [P, SLOTS, SLOTW])
        vh = sb("vh", [P, CHUNKS, D], F32R)
        vl = sb("vl", [P, CHUNKS, D], F32R)
        self2 = sb("self2", [P, CHUNKS, D])
        z = sb("z", [P, BLK, H])
        uts = sb("uts", [P, PANEL])
        xts = sb("xts", [P, PANEL])
        xp = sb("xp", [P, 2, BLK, D])
        ident = sb("ident", [P, P])
        ones = sb("ones", [P, P])
        w1t = sb("w1t", [P, 3, D])
        w2t = sb("w2t", [P, 3, D])
        wmt = sb("wmt", [P, 2, D])
        g2B = sb("g2B", [P, D])
        be2B = sb("be2B", [P, D])
        bmB = sb("bmB", [P, D])
        bcol = sb("bcol", [P, 2, 3])
        scl = sb("scl", [P, 2])
        s_all = sb("s_all", [P, CHUNKS])
        cs_all = sb("cs_all", [P, CHUNKS])
        s4 = sb("s4", [P, BLK])
        bnst = sb("bnst", [P, BLK, 6])
        mv = sb("mv", [P, BLK, 2])
        ln = sb("ln", [P, 5, BLK])
        spare = sb("spare", [P, 1])
        flag_i = sb("flag_i", [P, 1], I32)

        lnc = sb("lnc", [P, 4, BLK])

        first = ExitStack()
        xs = sb("xs", [P, CHUNKS, D], where=first)
        acc = sb("acc", [P, SLOTW], where=first)
        accf = sb("accf", [P, PANEL], where=first)
        junk_a = sb("junk_a", [P, SLOTW], I8, where=first)
        junk_b = sb("junk_b", [P, SLOTW], I8, where=first)
        junk_d = sb("junk_d", [P, SLOTW], U8, where=first)
        first.close()
        mh = sb("mh", [P, 8, PANEL], F32R)
        ml = sb("ml", [P, 8, PANEL], F32R)

        second = ExitStack()
        t1 = sb("t1", [P, BLK, H], where=second)
        hT = sb("hT", [P, 2, PANEL], where=second)
        diag = sb("diag", [P, BLK, P], where=second)
        wA = sb("wA", [P, 2, H], where=second)
        wB = sb("wB", [P, 2, H], where=second)
        bw1B = sb("bw1B", [P, H], where=second)
        bs1B = sb("bs1B", [P, H], where=second)
        bb2B = sb("bb2B", [P, D], where=second)
        bo2B = sb("bo2B", [P, D], where=second)
        g1col = sb("g1col", [P, 2], where=second)
        be1col = sb("be1col", [P, 2], where=second)
        st = sb("st", [P, 2, 3, BLK], where=second)
        ed = sb("ed", [P, 6, BLK], where=second)
        nz = sb("nz", [P, PANELS * SLOTS], where=second)
        sg = sb("sg", [P, PANELS * SLOTS], where=second)
        fl = sb("fl", [P, 4], where=second)
        nbig = sb("nbig", [P, 1], where=second)
        crow = sb("crow", [CHUNKS, P], where=second)
        bincol = sb("bincol", [P, 3], where=second)
        second.close()
        x1h = sb("x1h", [P, CHUNKS, D], F32R)
        x1l = sb("x1l", [P, CHUNKS, D], F32R)

        ps = ctx.enter_context(nc.psum_tensor("ps", [P, 8, PANEL], FP32))

        stage = self2[:, :, :].rearrange("p k n -> p (k n)")
        st_in1 = stage[:, 0:256]
        st_out1 = stage[:, 256:768].rearrange("p (c n) -> p c n", c=2)
        st_in2 = stage[:, 768:1024].rearrange("p (c n) -> p c n", c=2)
        st_out2 = stage[:, 1024:1152]
        st_w1 = stage[:, 1152:1536].rearrange("p (l n) -> p l n", l=3)
        st_w2 = stage[:, 1536:1920].rearrange("p (l n) -> p l n", l=3)
        st_wm = stage[:, 1920:2176]
        st_b = stage[:, 2176:2560].rearrange("p (k n) -> p k n", k=3)
        st_in1T = stage[:, 2560:2816].rearrange("p (c n) -> p c n", c=2)
        st_in2T = stage[:, 2816:3072].rearrange("p (c n) -> p c n", c=2)
        st_bs = stage[:, 3072:3328]
        st_bo = stage[:, 3328:3456]

        SMALL, T, YT = 2, (3, 4, 5, 6), 7

        def T2(i):
            return ps[:, T[i], :]

        weights_in = sem("weights_in")
        consts_in = sem("consts_in")
        bias_in = sem("bias_in")
        x_in = [sem(f"x_in{q}") for q in range(SLOTS)]
        const_ready = sem("const_ready")
        setup_t = sem("setup_t")
        setup_c = sem("setup_c")
        setup_m = sem("setup_m")
        setup_done = sem("setup_done")
        bad_ready = sem("bad_ready")
        bad_summed = sem("bad_summed")
        flag_ready = sem("flag_ready")
        loaded = [sem(f"loaded{q}") for q in range(SLOTS)]
        xp_in = [sem(f"xp_in{k}") for k in range(2)]
        rows_in = [sem(f"rows_in{k}") for k in range(ROW_SLOTS)]
        x2_in = [sem(f"x2_in{k}") for k in range(QUARTERS)]
        x1_in = [sem(f"x1_in{k}") for k in range(2)]

        S1 = Pass1Signals(sem, "a", loaded, xp_in)
        SG = Pass1Signals(sem, "g", [sem(f"loaded_g{q}") for q in range(SLOTS)], [sem(f"xp_in_g{k}") for k in range(2)])
        gen_enter = sem("gen_enter")
        gen_leave = sem("gen_leave")
        gen_cs_t = sem("gen_cs_t")
        gen_cs_row = sem("gen_cs_row")
        gen_cs_in = sem("gen_cs_in")
        gen_in = sem("gen_in")
        gen_masked = sem("gen_masked")
        gen_stored = sem("gen_stored")
        gen_step = sem("gen_step")

        hi2 = sem("hi2")
        lo2 = sem("lo2")
        lo2_pool = sem("lo2_pool")
        used2 = sem("used2")
        y_copied = sem("y_copied")
        yt_done = sem("yt_done")
        stats2 = sem("stats2")
        factors2 = sem("factors2")
        normed2 = sem("normed2")
        affine2 = sem("affine2")
        x1_stored = sem("x1_stored")
        self_used = sem("self_used")
        dve_step2 = sem("dve_step2")
        pool_step2 = sem("pool_step2")
        x2_hi = sem("x2_hi")
        x2_lo = sem("x2_lo")
        x1_hi = sem("x1_hi")
        x1_lo = sem("x1_lo")
        turned = sem("turned")
        hi3 = sem("hi3")
        lo3 = sem("lo3")
        used3 = sem("used3")
        a_copied = sem("a_copied")
        mlp_done = sem("mlp_done")
        relu_done = sem("relu_done")
        merged = sem("merged")
        z3_ready = sem("z3_ready")
        stats3 = sem("stats3")
        factors3 = sem("factors3")
        base3 = sem("base3")
        pool_step3 = sem("pool_step3")
        normed3 = sem("normed3")
        stored = sem("stored")
        dve_step3 = sem("dve_step3")

        rows_of = x.rearrange("(k p) d -> p k d", p=P)
        x1_rows = x1_dram.rearrange("(k p) d -> p k d", p=P)
        out_rows = out.rearrange("(k p) d -> p k d", p=P)

        def column_panel(src, p, q):
            return src.rearrange("(q b r) c -> r q b c", b=BLK, r=P)[:, q, :, bass.ds(p * PANEL, PANEL)]

        by_squares = adj.rearrange("(g i) (a c) -> a i g c", i=SQ, a=QUADS)
        x1_squares = x1_dram.rearrange("(a t j) d -> a j t d", a=QUADS, j=SQ)
        x2_squares = x2.rearrange("(a t j) d -> a j t d", a=QUADS, j=SQ)

        def quadrant(t, a):
            return t[a * SQ:(a + 1) * SQ]

        def blocks(t, p):
            return t[:, bass.ds(p * BLK, BLK)]

        def blocks3(t, p):
            return t[:, bass.ds(p * BLK, BLK), :]

        def node_start(p, unit, extra=0):
            if isinstance(p, int):
                return ((p - 1) % PANELS) * unit + extra
            return p * unit + (extra - unit)

        def node_blocks3(t, p):
            return t[:, bass.ds(node_start(p, BLK), BLK), :]

        def node_block(t, p, b):
            return t[:, bass.ds(node_start(p, BLK, b), 1), :].rearrange("p o d -> p (o d)")

        def slot_view(q):
            return ring[:, q, :].rearrange("p (b c) -> p b c", b=BLK)

        def sp_pass1(sp, S, src, load_x):
            def panel(p, par):
                for q in range(SLOTS):
                    if isinstance(p, int) and p == 0:
                        if load_x:
                            sp.dma_start(xs[:, BLK * q:BLK * q + BLK, :], rows_of[:, BLK * q:BLK * q + BLK, :]) \
                                .then_inc(x_in[q], 16)
                    else:
                        sp.wait_ge(S.slot_pe, p * SLOTS + (q + 1 - SLOTS))
                        sp.wait_ge(S.slot_act, p * SLOTS + (q + 1 - SLOTS))
                        sp.wait_ge(S.slot_dve, p * SLOTS + (q + 1 - SLOTS))
                    sp.dma_start(slot_view(q), column_panel(src, p, q)).then_inc(S.loaded[q], 16)
                    if q == 3:
                        sp.dma_start(xp[:, par], blocks3(rows_of, p)).then_inc(S.xp_in[par], 16)
            panel_loop(sp, None, 0, panel)

        def sp_pass2(sp, src):
            columns = src.rearrange("(q b r) c -> r q b c", b=BLK, r=P)

            def panel(p, par):
                if not (isinstance(p, int) and p == 0):
                    for q in range(SLOTS):
                        wait_slot_split(sp, p, q, back=1)
                        sp.dma_start(slot_view(q), columns[:, q, :, bass.ds(node_start(p, PANEL), PANEL)]) \
                            .then_inc(loaded[q], 16)
                if isinstance(p, int) and p < 2:
                    sp.wait_ge(S1.xp_used, PANELS - 1 + p)
                else:
                    sp.wait_ge(S1.xp_used, PANELS)
                sp.dma_start(xp[:, par], node_blocks3(rows_of, p)).then_inc(xp_in[par], 16)
            panel_loop2(sp, None, 0, panel)

        def quarter(n):
            return slice(QC * n, QC * n + QC)

        def sp_x2(sp, n):
            sp.wait_ge(self_used, min(2 * n + 3, PANELS))
            for a in range(QUADS):
                sp.dma_start(quadrant(self2[:, quarter(n), :], a), x2_squares[a, :, quarter(X_ORDER[n]), :]) \
                    .then_inc(x2_in[n], 16)

        def sp_x1(sp, k):
            if k == 1:
                wait_slot_split(sp, PANELS - 1, ROW_SLOTS)
                wait_slot_split(sp, PANELS - 1, ROW_SLOTS + 1)
            sp.wait_ge(x1_stored, 16 * (PANELS + 1 - k))
            for a in range(QUADS):
                dst = quadrant(ring[:, ROW_SLOTS + k, :], a).rearrange("p (t d) -> p t d", d=D)
                sp.dma_start(dst, x1_squares[a, :, 2 * QC * k:2 * QC * (k + 1), :]).then_inc(x1_in[k], 16)

        def sp_pass3(sp):
            def panel(p, par):
                first_panel = isinstance(p, int) and p == 0
                if first_panel:
                    for n in range(QUARTERS - 1):
                        sp_x2(sp, n)
                for q in range(SLOTS):
                    if first_panel and q < ROW_SLOTS:
                        wait_slot_split(sp, PANELS - 1, q)
                    else:
                        sp.wait_ge(turned, p * SLOTS + (q + 1 - ROW_SLOTS))
                    for a in reversed(range(QUADS)):
                        sp.dma_start(quadrant(ring[:, q % ROW_SLOTS, :], a).rearrange("p (g c) -> p g c", c=P),
                                     by_squares[a, :, bass.ds(p * (PANEL // SQ), PANEL // SQ),
                                                PIECES[q] * P:(PIECES[q] + 1) * P]) \
                            .then_inc(rows_in[q % ROW_SLOTS], 16)
                    if first_panel and q == 1:
                        sp_x1(sp, 1)
                    if first_panel and q == 4:
                        sp_x2(sp, QUARTERS - 1)
                    if first_panel and q == 6:
                        sp_x1(sp, 0)
                    if q == 6:
                        if not first_panel:
                            sp.wait_ge(base3, p)
                        sp.wait_ge(x1_stored, 16 * PANELS + 16)
                        sp.dma_start(xp[:, par], blocks3(x1_rows, p)).then_inc(xp_in[par], 16)
            panel_loop(sp, None, 0, panel)

        def pe_setup(pe):
            pe.wait_ge(const_ready, 8)
            pe.wait_ge(weights_in, 16 * 7)
            for c in range(2):
                pe.transpose(ps[:, T[0], c * P:(c + 1) * P], st_in1[:, c * P:(c + 1) * P], ident[:, :])
                pe.transpose(ps[:, T[0], (2 + c) * P:(3 + c) * P], st_in2[:, c, :], ident[:, :])
                last = pe.transpose(ps[:, T[3], c * P:(c + 1) * P], st_wm[:, c * P:(c + 1) * P], ident[:, :])
            for l in range(3):
                pe.transpose(ps[:, T[1], l * P:(l + 1) * P], st_w1[:, l, :], ident[:, :])
                last = pe.transpose(ps[:, T[2], l * P:(l + 1) * P], st_w2[:, l, :], ident[:, :])
            last.then_inc(setup_t, 1)

        def pe_setup_products(pe):
            pe.wait_ge(setup_c, 7)
            for c in range(2):
                pe.matmul(ps[:, T[0], 0:H], st_in1T[:, c, :], st_out1[:, c, :], start=(c == 0), stop=(c == 1))
            for c in range(2):
                pe.matmul(ps[:, T[0], H:2 * H], st_b[:, c, :], st_out1[:, c, :], start=(c == 0), stop=(c == 1))
            for c in range(2):
                pe.matmul(ps[:, T[1], c * D:(c + 1) * D], st_in2T[:, c, :], st_out2, start=True, stop=True)
            pe.matmul(ps[:, T[1], 2 * D:3 * D], st_b[:, 2, :], st_out2, start=True, stop=True).then_inc(setup_m, 1)

        def act_setup(act):
            act.wait_ge(setup_t, 1)
            act.activation(st_in1T, ps[:, T[0], 0:2 * P].rearrange("p (c n) -> p c n", c=2), ACT.Copy) \
                .then_inc(setup_c, 1)
            act.activation(st_in2T, ps[:, T[0], 2 * P:4 * P].rearrange("p (c n) -> p c n", c=2), ACT.Copy) \
                .then_inc(setup_c, 1)
            act.activation(w1t[:, :, :], ps[:, T[1], 0:3 * P].rearrange("p (c n) -> p c n", c=3), ACT.Copy) \
                .then_inc(setup_c, 1)
            act.activation(w2t[:, :, :], ps[:, T[2], 0:3 * P].rearrange("p (c n) -> p c n", c=3), ACT.Copy) \
                .then_inc(setup_c, 1)
            act.activation(wmt[:, :, :], ps[:, T[3], 0:2 * P].rearrange("p (c n) -> p c n", c=2), ACT.Copy) \
                .then_inc(setup_c, 1)

        def dve_setup(dve):
            dve.wait_ge(const_ready, 8)
            dve.wait_ge(bias_in, 16 * 2)
            for k in range(3):
                last = dve.tensor_scalar(st_b[:, k, :], ones[:, :], bincol[:, k:k + 1], None, ALU.mult)
            dve.drain()
            dve.sem_inc(setup_c, 2)

        def dve_setup_products(dve):
            dve.wait_ge(consts_in, 16 * 15)
            dve.tensor_tensor(bs1B[:, :], bs1B[:, :], st_bs, ALU.add)
            dve.tensor_tensor(bo2B[:, :], bo2B[:, :], st_bo, ALU.add)
            dve.tensor_scalar(scl[:, :], scl[:, :], 2.0, None, ALU.add)
            dve.wait_ge(setup_m, 1)
            dve.tensor_copy(wA[:, 0, :], ps[:, T[0], 0:H])
            dve.tensor_copy(bw1B[:, :], ps[:, T[0], H:2 * H])
            dve.tensor_copy(wB[:, :, 0:D], ps[:, T[1], 0:2 * D].rearrange("p (c n) -> p c n", c=2))
            dve.tensor_copy(bb2B[:, :], ps[:, T[1], 2 * D:3 * D])
            dve.drain().then_inc(setup_done, 1)

        def pe_stages1(pe, S):
            def stage_sums(r):
                pe.wait_ge(S.folded, r + 1)
                for b in range(BLK):
                    last = pe.matmul(ps[:, SMALL, b:b + 1], accf[:, b * P:(b + 1) * P], ones[:, 0:1],
                                     start=True, stop=True)
                last.then_inc(S.sums_out, 1)

            def stage_own(r, par):
                pe.wait_ge(S.edge_ready, r + 1)
                pe.wait_ge(S.xp_in[par], xp_count(r, par))
                for b in range(BLK):
                    last = pe.matmul(ps[:, par, b * P:(b + 1) * P], xp[:, par, b, :], diag[:, b, :],
                                     start=False, stop=True, skip_group_check=True)
                last.then_inc(S.u_done, 1)
                for b in range(BLK):
                    last = pe.transpose(ps[:, T[0], b * P:(b + 1) * P], xp[:, par, b, :], ident[:, :])
                last.then_inc(S.xp_used, 1)

            def stage_layer1(r):
                pe.wait_ge(S.u_copied, r + 1)
                pe.wait_ge(S.xt_copied, r + 1)
                if isinstance(r, int) and r == PANELS - 1:
                    pe.wait_ge(S.v_done, r)
                else:
                    pe.wait_ge(S.slot_dve, r * SLOTS + (SLOTS + 2))
                for b in range(BLK):
                    pe.matmul(ps[:, T[b], 0:H], uts[:, b * P:(b + 1) * P], wA[:, 0, :], start=True, stop=True)
                    pe.matmul(ps[:, T[b], H:2 * H], xts[:, b * P:(b + 1) * P], wA[:, 1, :],
                              start=True, stop=True).then_inc(S.p12_done, 1)

            def stage_hT(r):
                pe.wait_ge(S.normed, r + 1)
                for c in range(2):
                    for b in range(BLK):
                        last = pe.transpose(ps[:, T[c], b * P:(b + 1) * P], z[:, b, c * P:(c + 1) * P], ident[:, :])
                    last.then_inc(S.ht_done, 1)

            def stage_layer2(r):
                pe.wait_ge(S.ht_copied, r * 2 + 2)
                for b in range(BLK):
                    for c in range(2):
                        last = pe.matmul(ps[:, T[2 + b // 2], (b % 2) * H:(b % 2) * H + H],
                                         hT[:, c, b * P:(b + 1) * P], wB[:, c, :], start=(c == 0), stop=(c == 1))
                last.then_inc(S.w2_done, 1)

            return stage_sums, stage_own, stage_layer1, stage_hT, stage_layer2

        def pe_pass1(pe, S, wait_x):
            stage_sums, stage_own, stage_layer1, stage_hT, stage_layer2 = pe_stages1(pe, S)

            def panel(p, par):
                post = not (isinstance(p, int) and p == 0)
                for q in range(SLOTS):
                    pe.wait_ge(S.loaded[q], (p + 1) * 16)
                    if wait_x and not post:
                        pe.wait_ge(x_in[q], 16)
                    for b in range(BLK):
                        k = BLK * q + b
                        last = pe.matmul(ps[:, par, :], xs[:, k, :], ring[:, q, b * PANEL:(b + 1) * PANEL],
                                         start=(k == 0), stop=False, skip_group_check=True)
                    last.then_inc(S.slot_pe, 1)
                    if wait_x and not post and q == 3:
                        pe_setup(pe)
                    if wait_x and not post and q == 5:
                        pe_setup_products(pe)
                    if post and q == 0:
                        stage_sums(p - 1)
                    if post and q == 2:
                        stage_own(p - 1, 1 - par)
                    if post and q == 3:
                        stage_layer1(p - 1)
                    if post and q == 6:
                        stage_hT(p - 1)
                    if q == 7 and isinstance(p, int) and p == PANELS - 1:
                        stage_sums(p)
                    if post and q == 7:
                        stage_layer2(p - 1)
            panel_loop(pe, None, 0, panel)

        def xp_count(r, par):
            if isinstance(r, int):
                return 16 * (r // 2 + 1)
            return (r - par) * 8 + 16

        def act_stages1(act, S):
            def copies(r, rp):
                act.wait_ge(S.u_done, r + 1)
                act.activation(uts[:, :], ps[:, rp, :], ACT.Copy).then_inc(S.u_copied, 1)
                act.wait_ge(S.xp_used, r + 1)
                act.activation(xts[:, :], T2(0), ACT.Copy).then_inc(S.xt_copied, 1)

            def normalise(r):
                act.wait_ge(S.factors, r + 1)
                for b in range(BLK):
                    last = act.activation(z[:, b, :], z[:, b, :], ACT.Identity, scale=ln[:, 3, b:b + 1],
                                          bias=ln[:, 4, b:b + 1])
                last.then_inc(S.normed, 1)

            def relus(r):
                for c in range(2):
                    act.wait_ge(S.ht_done, r * 2 + (c + 1))
                    act.activation(hT[:, c, :], T2(c), ACT.Relu, scale=g1col[:, c:c + 1],
                                   bias=be1col[:, c:c + 1]).then_inc(S.ht_copied, 1)
            return copies, normalise, relus

        def act_pass1(act, S, detect):
            copies, normalise, relus = act_stages1(act, S)

            def count_slot(p, q):
                act.wait_ge(S.loaded[q], (p + 1) * 16)
                col = p * SLOTS + q
                if detect:
                    if not (isinstance(p, int) and p == 0 and q == 0):
                        act.wait_ge(S.slot_act, p * SLOTS + q)
                    ins = act.activation(junk_a[:, :], ring[:, q, :], ACT.Sign, bias=nbig[:, :],
                                         accum_out=sg[:, bass.ds(col, 1)])
                    if q in ACT_ZERO_SLOTS:
                        ins = act.activation(junk_b[:, :], ring[:, q, :], ACT.Exp, scale=-2.0 ** 100,
                                             accum_out=nz[:, bass.ds(col, 1)])
                    ins.then_inc(S.slot_act, 1)
                else:
                    act.sem_inc(S.slot_act, 1)

            def panel(p, par):
                post = not (isinstance(p, int) and p == 0)
                for q in range(SLOTS):
                    count_slot(p, q)
                    if not post and detect and q == 3:
                        act_setup(act)
                    if post and q == 2:
                        copies(p - 1, 1 - par)
                    if post and q == 5:
                        normalise(p - 1)
                    if post and q == 6:
                        relus(p - 1)
            panel_loop(act, None, 0, panel)

        def layer_norm_factors(pool, steps, out_sem):
            v, t, y, nm = ln[:, 0, :], ln[:, 2, :], ln[:, 3, :], ln[:, 1, :]
            steps.did(pool.tensor_tensor(v, mv[:, :, 1], lnc[:, 0, :], ALU.add))
            steps.did(pool.tensor_tensor(nm, mv[:, :, 0], lnc[:, 3, :], ALU.mult))
            steps.settle()
            steps.did(pool.tensor_tensor(y, v, lnc[:, 1, :], ALU.pow))
            steps.settle()
            steps.did(pool.tensor_tensor(t, y, y, ALU.mult))
            steps.settle()
            steps.did(pool.tensor_tensor(t, t, v, ALU.mult))
            steps.settle()
            steps.did(pool.tensor_tensor(t, t, lnc[:, 1, :], ALU.mult))
            steps.settle()
            steps.did(pool.tensor_tensor(t, t, lnc[:, 2, :], ALU.add))
            steps.settle()
            steps.did(pool.tensor_tensor(y, y, t, ALU.mult))
            steps.settle()
            pool.tensor_tensor(ln[:, 4, :], nm, y, ALU.mult).then_inc(out_sem, 1)

        def pool_t1(pool, S, steps, r, rp):
            pool.wait_ge(S.edge_ready, r + 1)
            steps.did(pool.tensor_tensor(t1[:, :, :], bw1B[:, :].unsqueeze(1).to_broadcast([P, BLK, H]),
                                         st[:, rp, 2, :].unsqueeze(2).to_broadcast([P, BLK, H]), ALU.mult))
            steps.settle()
            pool.tensor_tensor(t1[:, :, :], t1[:, :, :], bs1B[:, :].unsqueeze(1).to_broadcast([P, BLK, H]),
                               ALU.add).then_inc(S.t1_ready, 1)

        def pool_factors1(pool, S, steps, r):
            pool.wait_ge(S.stats_ready, r + 1)
            layer_norm_factors(pool, steps, S.factors)

        def pool_pass1(pool, S):
            steps = Steps(pool, S.pool_step)

            def panel(p, par):
                if not (isinstance(p, int) and p == 0):
                    pool_t1(pool, S, steps, p - 1, 1 - par)
                    pool_factors1(pool, S, steps, p - 1)
            panel_loop(pool, steps, PER_POOL1, panel)
            return steps

        def ln_stats(steps, dve, rows, ready):
            for b in range(BLK):
                steps.did(dve.bn_stats(bnst[:, b, :], rows(b)))
            steps.settle()
            ln_aggregate(steps, dve, ready)

        def ln_aggregate(steps, dve, ready):
            dve.memset(spare[:, :], 0.0)
            for b in range(BLK):
                last = dve.bn_aggr(mv[:, b, :], bnst[:, b, :])
            last.then_inc(ready, 1)

        def dve_save_sums(dve, steps, r):
            steps.did(dve.tensor_copy(blocks(cs_all, r), ps[:, SMALL, 0:BLK]))
            steps.settle()

        def dve_stages1(dve, S, steps, own_sums):

            def edge(r, rp):
                cs, e, w = ps[:, SMALL, 0:BLK], ed, st[:, rp]
                dve.wait_ge(S.sums_out, r + 1)
                if own_sums and not (isinstance(r, int) and r == PANELS - 1):
                    dve_save_sums(dve, steps, r)
                steps.did(dve.tensor_scalar(e[:, 0, :], blocks(cs_all, r), EPS, None, ALU.add))
                steps.did(dve.tensor_scalar(e[:, 2, :], cs, 0.0, None, ALU.not_equal))
                steps.settle()
                steps.did(dve.reciprocal(e[:, 1, :], e[:, 0, :]))
                steps.did(dve.tensor_scalar(w[:, 1, :], e[:, 2, :], -1.0, 1.0, ALU.mult, ALU.add))
                steps.settle()
                steps.did(dve.tensor_tensor(e[:, 3, :], cs, e[:, 1, :], ALU.mult))
                for b in range(BLK):
                    steps.did(dve.tensor_scalar(diag[:, b, :], ident[:, :], w[:, 1, b:b + 1], None, ALU.mult))
                steps.settle()
                steps.did(dve.tensor_scalar(e[:, 0, :], e[:, 3, :], EPS, None, ALU.add))
                steps.settle()
                steps.did(dve.reciprocal(e[:, 4, :], e[:, 0, :]))
                steps.settle()
                steps.did(dve.tensor_tensor(e[:, 5, :], e[:, 4, :], e[:, 2, :], ALU.mult))
                steps.settle()
                steps.did(dve.tensor_tensor(e[:, 1, :], e[:, 1, :], e[:, 5, :], ALU.mult))
                steps.did(dve.tensor_tensor(e[:, 3, :], e[:, 3, :], e[:, 5, :], ALU.mult))
                steps.settle()
                steps.did(dve.tensor_tensor(w[:, 0, :], e[:, 1, :], w[:, 1, :], ALU.add))
                steps.did(dve.tensor_tensor(w[:, 2, :], e[:, 3, :], w[:, 1, :], ALU.add))
                steps.settle()
                dve.tensor_copy(blocks(s_all, r), w[:, 0, :]).then_inc(S.edge_ready, 1)

            def layer1(r, rp):
                dve.wait_ge(S.t1_ready, r + 1)
                for b in range(BLK):
                    dve.wait_ge(S.p12_done, r * BLK + (b + 1))
                    steps.did(dve.scalar_tensor_tensor(z[:, b, :], ps[:, T[b], 0:H], st[:, rp, 0, b:b + 1],
                                                       t1[:, b, :], ALU.mult, ALU.add))
                steps.settle()
                for b in range(BLK):
                    steps.did(dve.tensor_tensor(z[:, b, :], z[:, b, :], ps[:, T[b], H:2 * H], ALU.add))
                steps.settle()
                ln_stats(steps, dve, lambda b: z[:, b, :], S.stats_ready)

            def layer2(r, rp):
                dve.wait_ge(S.w2_done, r + 1)
                v, t = z[:, :, 0:D], z[:, :, D:2 * D]
                for g in range(2):
                    res = T2(2 + g).rearrange("p (b n) -> p b n", b=2)
                    steps.did(dve.tensor_tensor(v[:, 2 * g:2 * g + 2, :], res[:, :, 0:D],
                                                bb2B[:, :].unsqueeze(1).to_broadcast([P, 2, D]), ALU.add))
                steps.settle()
                steps.did(dve.tensor_copy(blocks3(vh, r), v))
                for b in range(BLK):
                    steps.did(dve.scalar_tensor_tensor(t[:, b, :], v[:, b, :], st[:, rp, 1, b:b + 1], bo2B[:, :],
                                                       ALU.mult, ALU.add))
                steps.settle()
                steps.did(dve.tensor_tensor(blocks3(vl, r), v, blocks3(vh, r).bitcast(FP32), ALU.subtract))
                for g in range(2):
                    res = T2(2 + g).rearrange("p (b n) -> p b n", b=2)
                    steps.did(dve.tensor_tensor(self2[:, bass.ds(r * BLK + 2 * g, 2), :], t[:, 2 * g:2 * g + 2, :],
                                                res[:, :, D:2 * D], ALU.add))
                steps.settle()
                dve.sem_inc(S.v_done, 1)

            return edge, layer1, layer2

        def dve_pass1(dve, S, detect, per_panel):
            steps = Steps(dve, S.dve_step)
            edge, layer1, layer2 = dve_stages1(dve, S, steps, detect)

            def slot(p, q):
                dve.wait_ge(S.loaded[q], (p + 1) * 16)
                if detect and q in DVE_ZERO_SLOTS:
                    if not (isinstance(p, int) and p == 0 and q <= 1):
                        dve.wait_ge(S.slot_dve, p * SLOTS + (q if q > 1 else 0))
                    dve.tensor_scalar(junk_d[:, :], ring[:, q, :], 0.0, None, ALU.is_equal, ALU.add,
                                      accum_out=nz[:, bass.ds(p * SLOTS + q, 1)])
                if q == 1:
                    if not (isinstance(p, int) and p == 0):
                        dve.wait_ge(S.folded, p)
                    dve.tensor_tensor(acc[:, :], ring[:, 0, :], ring[:, 1, :], ALU.add).then_inc(S.slot_dve, 2)
                elif q > 1:
                    dve.wait_ge(S.slot_dve, p * SLOTS + q)
                    dve.tensor_tensor(acc[:, :], acc[:, :], ring[:, q, :], ALU.add).then_inc(S.slot_dve, 1)

            def fold(p):
                dve.wait_ge(S.slot_dve, p * SLOTS + SLOTS)
                steps.did(dve.tensor_tensor(acc[:, 0:2 * PANEL], acc[:, 0:2 * PANEL], acc[:, 2 * PANEL:], ALU.add))
                steps.settle()
                dve.tensor_tensor(accf[:, :], acc[:, 0:PANEL], acc[:, PANEL:2 * PANEL], ALU.add).then_inc(S.folded, 1)

            def panel(p, par):
                post = not (isinstance(p, int) and p == 0)
                for q in range(SLOTS):
                    slot(p, q)
                    if not post and detect and q == 2:
                        dve_setup(dve)
                    if not post and detect and q == 7:
                        dve_setup_products(dve)
                    if post and q == 1:
                        edge(p - 1, 1 - par)
                    if post and q == 4:
                        layer1(p - 1, 1 - par)
                if post:
                    dve.wait_ge(S.sums_out, p)
                fold(p)
                if post and not (isinstance(p, int) and p == PANELS - 1):
                    layer2(p - 1, 1 - par)
            panel_loop(dve, steps, per_panel, panel)
            return steps, layer2

        def general_gate(eng, gate):
            eng.drain().then_inc(gate, 1)
            eng.wait_ge(gate, 5)

        def sp_general(sp):
            general_gate(sp, gen_enter)
            sp.wait_ge(gen_cs_row, 1)
            sp.dma_start(cs_dram.rearrange("(k p) -> k p", p=P), crow[:, :]).then_inc(gen_stored, 16)
            sp.wait_ge(gen_stored, 16)
            with sp.Fori(0, PANELS) as p:
                sp.dma_start(t1[:, 0:2, :].rearrange("p b n -> p (b n)"),
                             cs_dram[bass.ds(p * PANEL, PANEL)].partition_broadcast(P)).then_inc(gen_cs_in, 16)
                for q in range(SLOTS):
                    sp.wait_ge(gen_stored, p * (16 * SLOTS) + (16 * q + 16))
                    sp.dma_start(slot_view(0), column_panel(adj, p, q)).then_inc(gen_in, 16)
                    sp.wait_ge(gen_masked, p * SLOTS + (q + 1))
                    sp.dma_start(column_panel(masked_dram, p, q), slot_view(0)).then_inc(gen_stored, 16)
            sp.wait_ge(gen_stored, 16 * PANELS * SLOTS + 16)
            sp_pass1(sp, SG, masked_dram, False)
            general_gate(sp, gen_leave)

        def dve_general(dve):
            general_gate(dve, gen_enter)
            steps = Steps(dve, gen_step)
            per = 2 + SLOTS * BLK * 2
            rB, tmp = z[:, 0:2, :].rearrange("p b n -> p (b n)"), z[:, 2:4, :].rearrange("p b n -> p (b n)")
            with dve.Fori(0, PANELS) as p:
                steps.enter(p * per)
                dve.wait_ge(gen_cs_in, p * 16 + 16)
                steps.did(dve.tensor_scalar(rB, t1[:, 0:2, :].rearrange("p b n -> p (b n)"), EPS, None, ALU.add))
                steps.settle()
                steps.did(dve.reciprocal(rB, rB))
                steps.settle()
                for q in range(SLOTS):
                    dve.wait_ge(gen_in, p * (16 * SLOTS) + 16 * (q + 1))
                    for b in range(BLK):
                        m = ring[:, 0, b * PANEL:(b + 1) * PANEL]
                        steps.did(dve.tensor_tensor(tmp, m, rB, ALU.mult))
                        steps.settle()
                        steps.did(dve.scalar_tensor_tensor(m, tmp, THRESH, m, ALU.is_gt, ALU.mult))
                        steps.settle()
                    dve.sem_inc(gen_masked, 1)
                assert steps.n == per
            _, layer2 = dve_pass1(dve, SG, False, PER_DVE1G)
            layer2(PANELS - 2, 0)
            general_gate(dve, gen_leave)

        def pe_general(pe):
            general_gate(pe, gen_enter)
            pe.transpose(ps[0:CHUNKS, T[0], 0:P], cs_all[:, :], ident[:, :]).then_inc(gen_cs_t, 1)
            pe_pass1(pe, SG, False)
            general_gate(pe, gen_leave)

        def act_general(act):
            general_gate(act, gen_enter)
            act.wait_ge(gen_cs_t, 1)
            act.activation(crow[:, :], ps[0:CHUNKS, T[0], 0:P], ACT.Copy).then_inc(gen_cs_row, 1)
            act_pass1(act, SG, False)
            general_gate(act, gen_leave)

        def pool_general(pool):
            general_gate(pool, gen_enter)
            pool_pass1(pool, SG)
            general_gate(pool, gen_leave)

        def general(eng, path):
            eng.wait_ge(flag_ready, 1)
            flag = eng.value_load(flag_i[0:1, 0:1], min_val=0, max_val=1)
            with eng.If(flag > 0):
                path(eng)

        PER_DVE1, PER_DVE1G, PER_DVE2, PER_DVE3 = 40, 39, 14, 5
        PER_POOL1, PER_POOL2, PER_POOL3 = 9, 17, 8

        HALF = SLOTW // 2

        def half_of(t, h):
            k = h % 4
            return t[:, 2 * k:2 * k + 2, :].rearrange("p a n -> p (a n)")

        def low_counts(h, halves):
            behind = [k for k in halves if k > h]
            return (behind[0] if behind else 2 * SLOTS) - (h if h != halves[0] else 0)

        def wait_low(eng, p, h):
            eng.wait_ge(lo2_pool if h in POOL_HALVES else lo2, p * (2 * SLOTS) + (h + 1))

        def wait_slot_split(eng, p, q, back=0):
            for done in (hi2, lo2, lo2_pool):
                eng.wait_ge(done, p * (2 * SLOTS) + (2 * q + 2 - back * 2 * SLOTS))

        def split_waits(eng, p, h):
            if isinstance(p, int) and p == 0:
                if h >= 4:
                    eng.wait_ge(used2, h - 3)
            else:
                eng.wait_ge(used2, p * (2 * SLOTS) + (h - 3))

        def low_half(eng, p, h, done, halves):
            eng.wait_ge(loaded[h // 2], (p + PANELS) * 16)
            split_waits(eng, p, h)
            eng.wait_ge(hi2, p * (2 * SLOTS) + (h + 1))
            eng.tensor_tensor(half_of(ml, h), ring[:, h // 2, (h % 2) * HALF:(h % 2 + 1) * HALF],
                              half_of(mh, h).bitcast(FP32), ALU.subtract).then_inc(done, low_counts(h, halves))

        def act_post2(act):
            def copy_y(r, rp):
                act.wait_ge(used2, r * (2 * SLOTS) + 2 * SLOTS)
                act.activation(uts[:, :], ps[:, rp, :], ACT.Copy).then_inc(y_copied, 1)

            def norm(r, which):
                act.wait_ge(factors2, r * 2 + (which + 1))
                if which == 0:
                    act.wait_ge(x1_stored, r * 16 + 16)
                for b in range(BLK):
                    last = act.activation(z[:, b, D:2 * D], z[:, b, 0:D], ACT.Identity, scale=ln[:, 3, b:b + 1],
                                          bias=ln[:, 4, b:b + 1])
                last.then_inc(normed2, 1)
                if which == 1:
                    act.wait_ge(normed2, r * 2 + 2)
                    act.dma_start(node_blocks3(x1_rows, r), z[:, :, D:2 * D]).then_inc(x1_stored, 16)
            return copy_y, norm

        def act_pass2(act):
            copies1, normalise1, relus1 = act_stages1(act, S1)
            copy_y, norm = act_post2(act)
            act.sem_inc(x1_stored, 16)
            act.wait_ge(S1.slot_pe, PANELS * SLOTS)
            act.wait_ge(S1.sums_out, PANELS)

            def half(p, h):
                if h % 2 == 0:
                    act.wait_ge(loaded[h // 2], (p + PANELS) * 16)
                split_waits(act, p, h)
                act.activation(half_of(mh, h), ring[:, h // 2, (h % 2) * HALF:(h % 2 + 1) * HALF],
                               ACT.Copy).then_inc(hi2, 1)

            def panel(p, par):
                post = not (isinstance(p, int) and p == 0)
                for h in range(2 * SLOTS):
                    half(p, h)
                    if not post and h == 4:
                        copies1(PANELS - 1, 1)
                    if not post and h == 11:
                        normalise1(PANELS - 1)
                    if not post and h == 12:
                        relus1(PANELS - 1)
                    if post and h == 3:
                        copy_y(p - 1, 1 - par)
                    if post and h == 8:
                        norm(p - 1, 0)
                    if post and h == 15:
                        norm(p - 1, 1)
            panel_loop2(act, None, 0, panel)

        def pool_factors2(pool, steps, r, which):
            pool.wait_ge(stats2, r * 2 + (1 + which))
            layer_norm_factors(pool, steps, factors2)

        def pool_affine2(pool, steps, r):
            pool.wait_ge(normed2, r * 2 + 1)
            steps.did(pool.tensor_tensor(z[:, :, D:2 * D], z[:, :, D:2 * D],
                                         g2B[:, :].unsqueeze(1).to_broadcast([P, BLK, D]), ALU.mult))
            steps.settle()
            pool.tensor_tensor(z[:, :, D:2 * D], z[:, :, D:2 * D],
                               be2B[:, :].unsqueeze(1).to_broadcast([P, BLK, D]), ALU.add).then_inc(affine2, 1)

        def pool_pass2(pool, steps1):
            steps = Steps(pool, pool_step2)

            def panel(p, par):
                post = not (isinstance(p, int) and p == 0)
                low_half(pool, p, POOL_HALVES[0], lo2_pool, POOL_HALVES)
                if not post:
                    pool_t1(pool, S1, steps1, PANELS - 1, 1)
                else:
                    pool_factors2(pool, steps, p - 1, 0)
                low_half(pool, p, POOL_HALVES[1], lo2_pool, POOL_HALVES)
                if not post:
                    pool_factors1(pool, S1, steps1, PANELS - 1)
                else:
                    pool_affine2(pool, steps, p - 1)
                    pool_factors2(pool, steps, p - 1, 1)
            panel_loop2(pool, steps, PER_POOL2, panel)
            pool_x2(pool, 0)
            pool_x2(pool, 1)
            pool_factors2(pool, steps, PANELS - 1, 0)
            pool_affine2(pool, steps, PANELS - 1)
            pool_factors2(pool, steps, PANELS - 1, 1)
            pool_x2(pool, 2)
            pool_x2(pool, 3)

        def pool_x2(pool, n):
            part = quarter(X_ORDER[n])
            pool.wait_ge(x2_hi, n + 1)
            pool.tensor_tensor(vl[:, part, :], self2[:, quarter(n), :], vh[:, part, :].bitcast(FP32), ALU.subtract) \
                .then_inc(x2_lo, 1)

        def pool_pass3(pool):
            steps = Steps(pool, pool_step3)
            pool.sem_inc(base3, 1)

            def post(r, rp):
                pool.wait_ge(xp_in[rp], xp_count3(r, rp))
                pool.wait_ge(relu_done, r * 6 + 2)
                pool.tensor_tensor(z[:, :, 0:D], xp[:, rp], bmB[:, :].unsqueeze(1).to_broadcast([P, BLK, D]),
                                   ALU.add).then_inc(base3, 1)
                pool.wait_ge(stats3, r + 1)
                layer_norm_factors(pool, steps, factors3)

            def panel(p, par):
                if not (isinstance(p, int) and p == 0):
                    post(p - 1, 1 - par)
            panel_loop(pool, steps, PER_POOL3, panel)
            post(PANELS - 1, 1)

        def xp_count3(r, par):
            if isinstance(r, int):
                return 16 * (PANELS + r // 2 + 1)
            return (r - par) * 8 + (16 + 16 * PANELS)

        def dve_post2(dve, steps):
            def layer(r):
                steps.did(dve.tensor_copy(s4[:, :], s_all[:, bass.ds(node_start(r, BLK), BLK)]))
                steps.settle()
                dve.wait_ge(yt_done, r + 1)
                for b in range(BLK):
                    steps.did(dve.scalar_tensor_tensor(z[:, b, 0:D], ps[:, YT, b * P:(b + 1) * P], s4[:, b:b + 1],
                                                       node_block(self2, r, b), ALU.mult, ALU.add))
                steps.settle()
                dve.sem_inc(self_used, 1)
                ln_stats(steps, dve, lambda b: z[:, b, 0:D], stats2)

            def residual(r, rp):
                dve.wait_ge(affine2, r + 1)
                dve.wait_ge(xp_in[rp], xp2_count(r, rp))
                steps.did(dve.scalar_tensor_tensor(z[:, :, 0:D], z[:, :, D:2 * D], 0.0, xp[:, rp], ALU.max, ALU.add))
                steps.settle()
                ln_stats(steps, dve, lambda b: z[:, b, 0:D], stats2)

            return layer, residual

        def dve_pass2(dve, steps1):
            steps = Steps(dve, dve_step2)
            edge1, layer1, layer2 = dve_stages1(dve, S1, steps1, True)
            layer, residual = dve_post2(dve, steps)

            def panel(p, par):
                post = not (isinstance(p, int) and p == 0)
                for h in range(2 * SLOTS):
                    if h not in POOL_HALVES:
                        low_half(dve, p, h, lo2, DVE_HALVES)
                    if not post and h == 0:
                        edge1(PANELS - 1, 1)
                    if not post and h == 7:
                        layer1(PANELS - 1, 1)
                    if not post and h == 13:
                        layer2(PANELS - 1, 1)
                    if post and h == 4:
                        layer(p - 1)
                    if post and h == 10:
                        residual(p - 1, 1 - par)
            panel_loop2(dve, steps, PER_DVE2, panel)
            return steps

        def xp2_count(r, par):
            if isinstance(r, int):
                return 16 * (PANELS // 2 + r // 2 + 1)
            return (r - par) * 8 + (16 + 8 * PANELS)

        def pe_turn_y(pe, r):
            pe.wait_ge(y_copied, r + 1)
            for b in range(BLK):
                last = pe.transpose(ps[:, YT, b * P:(b + 1) * P], uts[:, b * P:(b + 1) * P], ident[:, :])
            last.then_inc(yt_done, 1)

        def pe_pass2(pe):
            _, stage_own, stage_layer1, stage_hT, stage_layer2 = pe_stages1(pe, S1)

            def panel(p, par):
                post = not (isinstance(p, int) and p == 0)
                for h in range(2 * SLOTS):
                    pe.wait_ge(hi2, p * (2 * SLOTS) + (h + 1))
                    if not post and h == 0:
                        pe.wait_ge(S1.v_done, PANELS - 2)
                    if not post and h >= 2 * SLOTS - 4 and h % 2 == 0:
                        pe.wait_ge(S1.v_done, PANELS - 1 + (h - (2 * SLOTS - 4)) // 2)
                    for a in range(2):
                        k = 2 * h + a
                        m = mh[:, 2 * (h % 4) + a, :]
                        pe.matmul(ps[:, par, :], vh[:, k, :], m, start=(k == 0), stop=False)
                        pe.matmul(ps[:, par, :], vl[:, k, :], m, start=False, stop=False)
                    wait_low(pe, p, h)
                    for a in range(2):
                        k = 2 * h + a
                        last = pe.matmul(ps[:, par, :], vh[:, k, :], ml[:, 2 * (h % 4) + a, :], start=False,
                                         stop=(k == CHUNKS - 1))
                    last.then_inc(used2, 1)
                    if not post and h == 1:
                        stage_own(PANELS - 1, 1)
                    if not post and h == 4:
                        stage_layer1(PANELS - 1)
                    if not post and h == 9:
                        stage_hT(PANELS - 1)
                    if not post and h == 10:
                        stage_layer2(PANELS - 1)
                    if post and h == 1:
                        pe_turn_y(pe, p - 1)
            panel_loop2(pe, None, 0, panel)

        M3, MERGE = (5, 6), 4
        A3 = ((0, 2), (1, 3))

        def pieces(t, q):
            return t[:, BLK * (q % 2):BLK * (q % 2) + BLK, :].rearrange("p a n -> p (a n)")

        def turned_slot(q):
            return ring[:, SLOTS - 2 + q % 2, :]

        def pe_pass3(pe):
            def products(p, par, q, sides=(0, 1)):
                pe.wait_ge(hi3, p * SLOTS + (q + 1))
                operands = [(A3[par][g], ((x1h, x1l), (vh, vl))[g]) for g in sides]
                for t in range(BLK):
                    k, h = BLK * PIECES[q] + t, mh[:, BLK * (q % 2) + t, :]
                    for bank, (sh, sl) in operands:
                        pe.matmul(ps[:, bank, :], sh[:, k, :], h, start=(q == 0 and t == 0), stop=False)
                        pe.matmul(ps[:, bank, :], sl[:, k, :], h, start=False, stop=False)
                pe.wait_ge(lo3, p * SLOTS + (q + 1))
                for t in range(BLK):
                    k, l = BLK * PIECES[q] + t, ml[:, BLK * (q % 2) + t, :]
                    for bank, (sh, sl) in operands:
                        last = pe.matmul(ps[:, bank, :], sh[:, k, :], l, start=False,
                                         stop=(q == SLOTS - 1 and t == BLK - 1))
                if 0 in sides:
                    last.then_inc(used3, 1)

            def first_products(par):
                for q in range(SLOTS):
                    if q != 5:
                        if q % 2 == 0:
                            pe.wait_ge(x2_lo, q // 2 + 1)
                        products(0, par, q, (1,))
                    if q == 4:
                        products(0, par, 5, (1,))
                    if q % 2 == 0:
                        pe.wait_ge(x1_lo, q // 2 + 1)
                    products(0, par, q, (0,))

            def mlp(r, layer):
                for g, (w, src) in enumerate(((w1t, uts), (w2t, xts))):
                    if layer == 0:
                        pe.wait_ge(a_copied, r * 2 + (1 + g))
                    else:
                        pe.wait_ge(relu_done, r * 6 + (2 * layer - 1 + g))
                    last = pe.matmul(ps[:, M3[g], :], w[:, layer, :], src[:, :], start=True, stop=True)
                    last.then_inc(mlp_done, 1)

            def merge(r):
                for g, src in enumerate((uts, xts)):
                    pe.wait_ge(relu_done, r * 6 + (5 + g))
                    for b in range(BLK):
                        last = pe.matmul(ps[:, MERGE, b * P:(b + 1) * P], src[:, b * P:(b + 1) * P], wmt[:, g, :],
                                         start=(g == 0 and b == 0), stop=(g == 1), skip_group_check=True)
                last.then_inc(merged, 1)

            def panel(p, par):
                post = not (isinstance(p, int) and p == 0)
                if not post:
                    pe_turn_y(pe, PANELS - 1)
                    first_products(par)
                else:
                    for q in range(SLOTS):
                        products(p, par, q)
                        if q < 3:
                            mlp(p - 1, q)
                        if q == 3:
                            merge(p - 1)
            panel_loop(pe, None, 0, panel)
            r = PANELS - 1
            for layer in range(3):
                mlp(r, layer)
            merge(r)

        def act_x2(act, n):
            act.wait_ge(used2, (PANELS - 1) * 2 * SLOTS + (QC // 2) * (X_ORDER[n] + 1))
            act.wait_ge(x2_in[n], 16 * QUADS)
            act.activation(vh[:, quarter(X_ORDER[n]), :], self2[:, quarter(n), :], ACT.Copy).then_inc(x2_hi, 1)

        def x1_piece(k):
            return ring[:, ROW_SLOTS + k // 2, (k % 2) * QC * D:(k % 2 + 1) * QC * D].rearrange("p (t d) -> p t d", d=D)

        def act_x1(act, n):
            k = X_ORDER[n]
            act.wait_ge(x1_in[k // 2], 16 * QUADS)
            act.activation(x1h[:, QC * k:QC * k + QC, :], x1_piece(k), ACT.Copy).then_inc(x1_hi, 1)

        def dve_x1(dve, n):
            k = X_ORDER[n]
            part = slice(QC * k, QC * k + QC)
            dve.wait_ge(x1_hi, n + 1)
            dve.tensor_tensor(x1l[:, part, :], x1_piece(k), x1h[:, part, :].bitcast(FP32), ALU.subtract) \
                .then_inc(x1_lo, 1)

        def buffer_free(eng, p, q):
            if isinstance(p, int) and p == 0 and q < 2:
                eng.wait_ge(used2, PANELS * 2 * SLOTS)
            else:
                eng.wait_ge(used3, p * SLOTS + (q - 1))

        def act_pass3(act):
            act.sem_inc(stored, 16)
            copy_y, norm2 = act_post2(act)

            def high_parts(p, q):
                act.wait_ge(turned, p * SLOTS + (q + 1))
                buffer_free(act, p, q)
                act.activation(pieces(mh, q), turned_slot(q), ACT.Copy).then_inc(hi3, 1)

            def copies(r, rp):
                act.wait_ge(used3, r * SLOTS + SLOTS)
                for g, dst in enumerate((uts, xts)):
                    act.activation(dst[:, :], ps[:, A3[rp][g], :], ACT.Copy, scale=scl[:, g:g + 1]) \
                        .then_inc(a_copied, 1)

            def relus(r, layer):
                for g, dst in enumerate((uts, xts)):
                    act.wait_ge(mlp_done, r * 6 + (2 * layer + 1 + g))
                    act.activation(dst[:, :], ps[:, M3[g], :], ACT.Relu, bias=bcol[:, g, layer:layer + 1]) \
                        .then_inc(relu_done, 1)

            def norm(r, rp):
                act.wait_ge(factors3, r + 1)
                act.wait_ge(stored, r * 16 + 16)
                for b in range(BLK):
                    last = act.activation(z[:, b, D:2 * D], z[:, b, 0:D], ACT.Identity, scale=ln[:, 3, b:b + 1],
                                          bias=ln[:, 4, b:b + 1])
                last.then_inc(normed3, 1)
                act.wait_ge(normed3, r + 1)
                act.dma_start(blocks3(out_rows, r), z[:, :, D:2 * D]).then_inc(stored, 16)

            def panel(p, par):
                post = not (isinstance(p, int) and p == 0)
                if not post:
                    act_x2(act, 0)
                    copy_y(PANELS - 1, 1)
                for q in range(SLOTS):
                    high_parts(p, q)
                    if not post and q == 0:
                        act_x2(act, 1)
                        act_x1(act, 0)
                        act_x2(act, 2)
                    if not post and q == 1:
                        norm2(PANELS - 1, 0)
                        act_x1(act, 1)
                        act_x2(act, 3)
                    if not post and q == 2:
                        norm2(PANELS - 1, 1)
                    if not post and q == 5:
                        act_x1(act, 2)
                        act_x1(act, 3)
                    if not post and q == 7:
                        act.wait_ge(x1_stored, 16 * PANELS + 16)
                    if post and q == 0:
                        copies(p - 1, 1 - par)
                    if post and q in (2, 3, 4):
                        relus(p - 1, q - 2)
                    if post and q == 7:
                        norm(p - 1, 1 - par)
            panel_loop(act, None, 0, panel)
            r = PANELS - 1
            copies(r, 1)
            for layer in range(3):
                relus(r, layer)
            norm(r, 1)
            act.wait_ge(stored, 16 * PANELS + 16)

        def dve_pass3(dve, steps2):
            steps = Steps(dve, dve_step3)
            layer, residual2 = dve_post2(dve, steps2)

            def turn(p, q):
                if isinstance(p, int):
                    dve.wait_ge(rows_in[q % ROW_SLOTS], 16 * QUADS * (2 * p + q // ROW_SLOTS + 1))
                else:
                    dve.wait_ge(rows_in[q % ROW_SLOTS], p * (32 * QUADS) + 16 * QUADS * (q // ROW_SLOTS + 1))
                if isinstance(p, int) and p == 0 and q < 2:
                    wait_slot_split(dve, PANELS - 1, SLOTS - 2 + q)
                else:
                    dve.wait_ge(hi3, p * SLOTS + (q - 1))
                    dve.wait_ge(lo3, p * SLOTS + (q - 1))
                dve.transpose(turned_slot(q).rearrange("p (t g c) -> p g t c", t=BLK, c=SQ),
                              ring[:, q % ROW_SLOTS, :].rearrange("p (g t c) -> p g t c", t=BLK, c=SQ)) \
                    .then_inc(turned, 1)

            def low_parts(p, q):
                buffer_free(dve, p, q)
                dve.wait_ge(hi3, p * SLOTS + (q + 1))
                dve.tensor_tensor(pieces(ml, q), turned_slot(q), pieces(mh, q).bitcast(FP32),
                                  ALU.subtract).then_inc(lo3, 1)

            def add(r):
                zz = z[:, :, 0:D]
                dve.wait_ge(base3, r + 2)
                dve.wait_ge(merged, r + 1)
                steps.did(dve.tensor_tensor(zz, zz, ps[:, MERGE, :].rearrange("p (b d) -> p b d", b=BLK), ALU.add))
                steps.settle()
                ln_stats(steps, dve, lambda b: z[:, b, 0:D], stats3)

            def panel(p, par):
                post = not (isinstance(p, int) and p == 0)
                if not post:
                    turn(0, 0)
                    layer(PANELS - 1)
                for q in range(SLOTS):
                    if not post and q == 2:
                        residual2(PANELS - 1, 1)
                    if not post and q == 0:
                        low_parts(0, 0)
                    if q + 1 < SLOTS:
                        turn(p, q + 1)
                    elif not (isinstance(p, int) and p == PANELS - 1):
                        turn(p + 1, 0)
                    if post or q != 0:
                        low_parts(p, q)
                    if not post and q < 2:
                        dve_x1(dve, q)
                    if not post and q == 5:
                        dve_x1(dve, 2)
                        dve_x1(dve, 3)
                    if post and q == 5:
                        add(p - 1)
            panel_loop(dve, steps, PER_DVE3, panel)
            add(PANELS - 1)

        block = ctx.enter_context(nc.Block())

        @block.sync
        def _(sp):
            sp_pass1(sp, S1, adj, True)
            sp.wait_ge(flag_ready, 1)
            flag = sp.value_load(flag_i[0:1, 0:1], min_val=0, max_val=1)
            with sp.If(flag > 0):
                sp_general(sp)
                sp_pass2(sp, masked_dram)
            with sp.Else():
                sp_pass2(sp, adj)
            sp_pass3(sp)

        @block.gpsimd
        def _(pool):
            pool.memset(ident[:, :], 0.0).then_inc(const_ready, 1)
            pool.memset(ones[:, :], 1.0).then_inc(const_ready, 1)
            pool.memset(nbig[:, :], -BIG).then_inc(const_ready, 1)
            pool.wait_ge(const_ready, 3)
            pool.affine_select(out=ident[:, :], in_=ident[:, :], compare_op=ALU.not_equal, fill=1.0, base=0,
                               pattern=[[-1, P]], channel_multiplier=1).then_inc(const_ready, 1)
            for n, c in enumerate((LN_EPS, -0.5, 1.5, -1.0)):
                pool.memset(lnc[:, n, :], c).then_inc(const_ready, 1)
            for dst, src in ((wA[:, 1, :], W_self1), (wB[:, :, D:2 * D], W_self2.rearrange("(c k) n -> k c n", c=2)),
                             (bs1B[:, :], b_out1.partition_broadcast(P)), (st_bs, b_self1.partition_broadcast(P)),
                             (bo2B[:, :], b_out2.partition_broadcast(P)), (st_bo, b_self2.partition_broadcast(P)),
                             (g2B[:, :], g2.partition_broadcast(P)), (be2B[:, :], be2.partition_broadcast(P)),
                             (bmB[:, :], bm.partition_broadcast(P)),
                             (scl[:, 0:1], eps1.partition_broadcast(P)), (scl[:, 1:2], eps2.partition_broadcast(P))):
                pool.dma_start(dst, src).then_inc(consts_in, 16)
            with nc.allow_non_contiguous_dma("columns of the small bias vectors"):
                for dst, src in ((g1col[:, :], g1.rearrange("(c k) -> k c", c=2)),
                                 (be1col[:, :], be1.rearrange("(c k) -> k c", c=2)),
                                 (bcol[:, 0, :], b1.rearrange("l d -> d l")),
                                 (bcol[:, 1, :], b2.rearrange("l d -> d l"))):
                    pool.dma_start(dst, src).then_inc(consts_in, 16)
            steps1 = pool_pass1(pool, S1)
            general(pool, pool_general)
            pool_pass2(pool, steps1)
            pool_pass3(pool)

        @block.scalar
        def _(act):
            with nc.allow_non_contiguous_dma("columns of the small bias vectors"):
                act.dma_start(bincol[:, 0:2], b_in1.rearrange("(c k) -> k c", c=2)).then_inc(bias_in, 16)
                act.dma_start(bincol[:, 2:3], b_in2.rearrange("(c k) -> k c", c=1)).then_inc(bias_in, 16)
            act.dma_start(st_in1, W_in1).then_inc(weights_in, 16)
            act.dma_start(st_out1, W_out1.rearrange("(c k) n -> k c n", c=2)).then_inc(weights_in, 16)
            act.dma_start(st_in2, W_in2.rearrange("(c k) n -> k c n", c=2)).then_inc(weights_in, 16)
            act.dma_start(st_out2, W_out2).then_inc(weights_in, 16)
            act.dma_start(st_w1, W1.rearrange("l o i -> o l i")).then_inc(weights_in, 16)
            act.dma_start(st_w2, W2.rearrange("l o i -> o l i")).then_inc(weights_in, 16)
            act.dma_start(st_wm, Wm).then_inc(weights_in, 16)
            act.wait_ge(const_ready, 3)
            act_pass1(act, S1, True)
            general(act, act_general)
            act_pass2(act)
            act_pass3(act)

        @block.tensor
        def _(pe):
            pe_pass1(pe, S1, True)
            pe.wait_ge(bad_ready, 1)
            pe.matmul(ps[:, SMALL, 8:9], ones[:, :], fl[:, 3:4], start=True, stop=True).then_inc(bad_summed, 1)
            general(pe, pe_general)
            pe_pass2(pe)
            pe_pass3(pe)

        @block.vector
        def _(dve):
            dve.wait_ge(const_ready, 8)
            steps1, layer2 = dve_pass1(dve, S1, True, PER_DVE1)
            dve.wait_ge(S1.sums_out, PANELS)
            dve_save_sums(dve, steps1, PANELS - 1)
            dve.wait_ge(S1.slot_act, PANELS * SLOTS)
            dve.scalar_tensor_tensor(sg[:, :], nz[:, :], 2.0, sg[:, :], ALU.mult, ALU.add, accum_out=fl[:, 0:1])
            dve.reduce_max(fl[:, 1:2], cs_all[:, :], AX.X)
            dve.drain()
            dve.tensor_scalar(fl[:, 0:1], fl[:, 0:1], float(PANELS * SLOTS * SLOTW), None, ALU.not_equal)
            dve.tensor_scalar(fl[:, 1:2], fl[:, 1:2], CS_LIMIT, None, ALU.is_gt)
            dve.drain()
            dve.tensor_tensor(fl[:, 3:4], fl[:, 0:1], fl[:, 1:2], ALU.max).then_inc(bad_ready, 1)
            dve.wait_ge(bad_summed, 1)
            dve.tensor_scalar(flag_i[:, :], ps[:, SMALL, 8:9], 1.0, None, ALU.min).then_inc(flag_ready, 1)
            layer2(PANELS - 2, 0)
            general(dve, dve_general)
            steps2 = dve_pass2(dve, steps1)
            dve_pass3(dve, steps2)


_INS = ['x', 'adj'] + ['L0_gnn_' + n for n in ('W_in1', 'b_in1', 'W_out1', 'b_out1', 'W_self1', 'b_self1', 'g1', 'be1',
                                               'W_in2', 'b_in2', 'W_out2', 'b_out2', 'W_self2', 'b_self2', 'g2', 'be2')] \
    + ['L1_gnn_' + n for n in ('x2', 'eps1', 'eps2', 'W1', 'b1', 'W2', 'b2', 'Wm', 'bm')]
_OUTS = [((N, D), 'float32')]


def kernel(**inputs):
    import numpy as _np
    import concourse.bacc as _bacc
    from concourse import mybir as _mybir
    from concourse.bass_utils import run_bass_kernel_spmd as _run

    nc = _bacc.Bacc("TRN2", target_bir_lowering=False, num_devices=1)
    arrays, args = {}, []
    for name in _INS:
        a = _np.ascontiguousarray(inputs[name])
        arrays[f"in_{name}_dram"] = a
        args.append(nc.dram_tensor(f"in_{name}_dram", a.shape, _mybir.dt.from_np(a.dtype), kind="ExternalInput").ap())
    for i, (shape, dtype) in enumerate(_OUTS):
        dt = _mybir.dt.from_np(_np.dtype(dtype))
        args.append(nc.dram_tensor(f"out_{i}_dram", shape, dt, kind="ExternalOutput").ap())
    gnn_program(nc, *args)
    r = _run(nc, [arrays], core_ids=[0])
    got = tuple(r.results[0][f"out_{i}_dram"] for i in range(len(_OUTS)))
    return got[0]
```
